# Optimizing a Trainium2 kernel written in Bass

```python
import numpy as np
import jax
import jax.numpy as jnp

def _softmax(x, axis=-1):
    return jax.nn.softmax(x, axis=axis)

def _gelu(x):
    return jax.nn.gelu(x, approximate=True)

def _silu(x):
    return jax.nn.silu(x)

def _sigmoid(x):
    return jax.nn.sigmoid(x)

def _layernorm(x, axis=-1, eps=1e-05):
    m = jnp.mean(x, axis=axis, keepdims=True)
    v = jnp.var(x, axis=axis, keepdims=True)
    return (x - m) / jnp.sqrt(v + eps)

def _scatter_add(tgt, idx, src, axis=0):
    return tgt.at[idx].add(src)

def _segment_sum(src, seg, n):
    return jax.ops.segment_sum(src, seg, n)
kernel_name = 'mk_flamingo_gated_d2_seqx_r8_bbdc80'

def setup_inputs(seed: int=0):
    np.random.seed(seed)
    _w = jnp.asarray

    def _rec_inputs():
        import jax
        import jax.numpy as jnp
        _rk = jax.random.key(seed)
        x = 7.22e-05 + 1 * jax.random.normal(jax.random.fold_in(_rk, 1), (32, 128, 128), jnp.float32)
        _lenS = 128 - jax.random.randint(jax.random.fold_in(_rk, 7), (32,), 0, max(1, 128 // 4) + 1, jnp.int32)
        _lenS2 = 120 - jax.random.randint(jax.random.fold_in(_rk, 8), (32,), 0, max(1, 120 // 4) + 1, jnp.int32)
        _ctx_768P = jax.random.normal(jax.random.fold_in(_rk, 11), (32, 16, 96), jnp.float32)
        _ctx_768c = jax.random.dirichlet(jax.random.fold_in(_rk, 511), 0.3 * jnp.ones((16,), jnp.float32), (32, 120))
        _ctx_768t = jnp.einsum('bsk,bkd->bsd', _ctx_768c, _ctx_768P)
        _ctx_768t = _ctx_768t * jax.lax.rsqrt(jnp.mean(jnp.square(_ctx_768t)) + 1e-12) * 0.953939
        ctx_768 = -0.000191848 + 0.999787 * (_ctx_768t + 0.3 * jax.random.normal(jax.random.fold_in(_rk, 611), (32, 120, 96), jnp.float32))
        _g = jax.random.normal(jax.random.fold_in(_rk, 9001), (2, 2), jnp.float32)
        _g = jnp.sign(_g) * jnp.maximum(jnp.abs(_g), 1.0) + (_g == 0) * 1.0
        g_xattn = _g[0]
        g_ffn = _g[1]
        return (x, ctx_768, g_xattn, g_ffn)
    x, ctx_768, g_xattn, g_ffn = _rec_inputs()

    def _L0_xattn_setup():
        import jax, jax.numpy as jnp
        import numpy as np
        NUM_HEADS = 16
        CLAMP = 10000.0
        key = jax.random.key(seed)
        ks = jax.random.split(key, 8)
        B, Nq, Nkv, Cq, Ckv = (4, 256, 256, 128, 96)
        s_q = 1.0 / np.sqrt(Cq)
        s_kv = 1.0 / np.sqrt(Ckv)
        return {'query': jax.random.normal(ks[0], (B, Nq, Cq), jnp.float32), 'key_value': jax.random.normal(ks[1], (B, Nkv, Ckv), jnp.float32), 'Wq': jax.random.normal(ks[2], (Cq, Cq), jnp.float32) * s_q, 'bq': jnp.zeros((Cq,), jnp.float32), 'Wk': jax.random.normal(ks[3], (Ckv, Cq), jnp.float32) * s_kv, 'bk': jnp.zeros((Cq,), jnp.float32), 'Wv': jax.random.normal(ks[4], (Ckv, Cq), jnp.float32) * s_kv, 'bv': jnp.zeros((Cq,), jnp.float32), 'Wo': jax.random.normal(ks[5], (Cq, Cq), jnp.float32) * s_q, 'bo': jnp.zeros((Cq,), jnp.float32)}
    _L0_xattn_all = _L0_xattn_setup()
    _L0_xattn_in = {k: v for k, v in _L0_xattn_all.items() if k in ('Wq', 'bq', 'Wk', 'bk', 'Wv', 'bv', 'Wo', 'bo')}
    del _L0_xattn_all

    def _L0_ffn_setup():
        import jax, jax.numpy as jnp
        import numpy as np
        from jax import lax
        HIDDEN = 128
        INTER = 64
        E = 64
        K = 6
        G = 8
        TG = 4
        NSH = 2
        ISH = INTER * NSH

        def _moe_forward(hidden_states, gate_w, gate_bias, eg_w, eu_w, ed_w, sg_w, su_w, sd_w):
            B, S, H = hidden_states.shape
            x = hidden_states.reshape(-1, H)
            T = x.shape[0]
            shared = jax.nn.silu(x @ sg_w.T) * (x @ su_w.T) @ sd_w.T
            logits = x @ gate_w.T
            scores = jax.nn.sigmoid(logits) + gate_bias
            group_scores = scores.reshape(T, G, E // G).max(axis=-1)
            _, sel_groups = lax.top_k(group_scores, TG)
            group_mask = jnp.zeros((T, G), scores.dtype).at[jnp.arange(T)[:, None], sel_groups].set(1.0)
            mask = jnp.repeat(group_mask, E // G, axis=1)
            masked_scores = scores * mask
            topk_w, topk_i = lax.top_k(masked_scores, K)
            topk_w = topk_w / (topk_w.sum(axis=-1, keepdims=True) + 1e-08)
            comb = jnp.zeros((T, E), x.dtype).at[jnp.arange(T)[:, None], topk_i].add(topk_w)
            h = jax.nn.silu(jnp.einsum('th,eih->eti', x, eg_w)) * jnp.einsum('th,eih->eti', x, eu_w)
            routed = jnp.einsum('eti,ehi,te->th', h, ed_w, comb)
            return (shared + routed).reshape(B, S, H)
        key = jax.random.key(seed)
        ks = jax.random.split(key, 9)
        s = 0.02
        return {'hidden_states': jax.random.normal(ks[0], (1, 128, HIDDEN), jnp.float32), 'gate_w': jax.random.normal(ks[1], (E, HIDDEN), jnp.float32) * s, 'gate_bias': jnp.zeros((E,), jnp.float32), 'eg_w': jax.random.normal(ks[2], (E, INTER, HIDDEN), jnp.float32) * s, 'eu_w': jax.random.normal(ks[3], (E, INTER, HIDDEN), jnp.float32) * s, 'ed_w': jax.random.normal(ks[4], (E, HIDDEN, INTER), jnp.float32) * s, 'sg_w': jax.random.normal(ks[5], (ISH, HIDDEN), jnp.float32) * s, 'su_w': jax.random.normal(ks[6], (ISH, HIDDEN), jnp.float32) * s, 'sd_w': jax.random.normal(ks[7], (HIDDEN, ISH), jnp.float32) * s}
    _L0_ffn_all = _L0_ffn_setup()
    _L0_ffn_in = {k: v for k, v in _L0_ffn_all.items() if k in ('gate_w', 'gate_bias', 'eg_w', 'eu_w', 'ed_w', 'sg_w', 'su_w', 'sd_w')}
    del _L0_ffn_all

    def _L1_xattn_setup():
        import jax, jax.numpy as jnp
        import numpy as np
        HEADS = 16
        DIM_HEAD = 64
        key = jax.random.key(seed)
        ks = jax.random.split(key, 8)
        B, S, D = (16, 512, 128)
        K, DE = (77, 96)
        inner = HEADS * DIM_HEAD
        hidden_states = jax.random.normal(ks[0], (B, S, D), dtype=jnp.float32)
        encoder_hidden_states = jax.random.normal(ks[1], (B, K, DE), dtype=jnp.float32)
        sc_q = 1.0 / np.sqrt(D)
        sc_kv = 1.0 / np.sqrt(DE)
        sc_o = 1.0 / np.sqrt(inner)
        Wq = jax.random.normal(ks[2], (D, inner), dtype=jnp.float32) * sc_q
        Wk = jax.random.normal(ks[3], (DE, inner), dtype=jnp.float32) * sc_kv
        Wv = jax.random.normal(ks[4], (DE, inner), dtype=jnp.float32) * sc_kv
        Wo = jax.random.normal(ks[5], (inner, D), dtype=jnp.float32) * sc_o
        bo = jax.random.normal(ks[6], (D,), dtype=jnp.float32) * 0.01
        return {'hidden_states': hidden_states, 'encoder_hidden_states': encoder_hidden_states, 'Wq': Wq, 'Wk': Wk, 'Wv': Wv, 'Wo': Wo, 'bo': bo}
    _L1_xattn_all = _L1_xattn_setup()
    _L1_xattn_in = {k: v for k, v in _L1_xattn_all.items() if k in ('Wq', 'Wk', 'Wv', 'Wo', 'bo')}
    del _L1_xattn_all

    def _L1_ffn_setup():
        import jax, jax.numpy as jnp
        import numpy as np
        B, S, D = (2, 128, 128)
        L, H = (64, 16)
        HD = L // H
        F, E, K = (256, 8, 2)
        THETA = 10000.0
        EPS = 1e-05

        def _rmsnorm(x, g):
            return x * g * jax.lax.rsqrt(jnp.mean(x * x, axis=-1, keepdims=True) + EPS)

        def _rope(t, pos):
            inv_freq = 1.0 / THETA ** (jnp.arange(0, HD, 2, dtype=jnp.float32) / HD)
            ang = pos[:, None].astype(jnp.float32) * inv_freq[None, :]
            cos, sin = (jnp.cos(ang), jnp.sin(ang))
            t1, t2 = (t[..., 0::2], t[..., 1::2])
            r1 = t1 * cos - t2 * sin
            r2 = t1 * sin + t2 * cos
            return jnp.stack([r1, r2], axis=-1).reshape(t.shape)

        def _forward(x, g1, g2, w_down, wq, wk, wv, w_up, router_w, w1, w2, w3):
            b, s, _ = x.shape
            pos = jnp.arange(s)
            h = _rmsnorm(x, g1)
            c = h @ w_down
            split = lambda t: t.reshape(b, s, H, HD).transpose(0, 2, 1, 3)
            q = _rope(split(c @ wq), pos)
            k = _rope(split(c @ wk), pos)
            v = split(c @ wv)
            scores = jnp.einsum('bhqd,bhkd->bhqk', q, k) / jnp.sqrt(jnp.float32(HD))
            causal = jnp.tril(jnp.ones((s, s), bool))
            scores = jnp.where(causal, scores, -jnp.inf)
            attn = jax.nn.softmax(scores, axis=-1)
            o = jnp.einsum('bhqk,bhkd->bhqd', attn, v).transpose(0, 2, 1, 3).reshape(b, s, L)
            x = x + o @ w_up
            res = x
            t = _rmsnorm(x, g2).reshape(-1, D)
            probs = jax.nn.softmax(t @ router_w, axis=-1)
            vals, idx = jax.lax.top_k(probs, K)
            w = vals / jnp.sum(vals, axis=-1, keepdims=True)
            gate = jnp.sum(jax.nn.one_hot(idx, E, dtype=t.dtype) * w[..., None], axis=1)
            hid = jax.nn.silu(jnp.einsum('td,edf->tef', t, w1)) * jnp.einsum('td,edf->tef', t, w3)
            y_e = jnp.einsum('tef,efd->ted', hid, w2)
            y = jnp.einsum('ted,te->td', y_e, gate)
            return res + y.reshape(b, s, D)
        key = jax.random.key(seed)
        ks = jax.random.split(key, 12)
        g = lambda k, shape, scale: jax.random.normal(k, shape, dtype=jnp.float32) * scale
        return {'x': g(ks[0], (B, S, D), 1.0), 'g1': jnp.ones((D,), jnp.float32), 'g2': jnp.ones((D,), jnp.float32), 'w_down': g(ks[1], (D, L), 0.02), 'wq': g(ks[2], (L, L), 0.02), 'wk': g(ks[3], (L, L), 0.02), 'wv': g(ks[4], (L, L), 0.02), 'w_up': g(ks[5], (L, D), 0.02), 'router_w': g(ks[6], (D, E), 0.02), 'w1': g(ks[7], (E, D, F), 0.02), 'w3': g(ks[8], (E, D, F), 0.02), 'w2': g(ks[9], (E, F, D), 0.02)}
    _L1_ffn_all = _L1_ffn_setup()
    _L1_ffn_in = {k: v for k, v in _L1_ffn_all.items() if k in ('g1', 'g2', 'w_down', 'wq', 'wk', 'wv', 'w_up', 'router_w', 'w1', 'w2', 'w3')}
    del _L1_ffn_all
    return {'x': x, 'ctx_768': ctx_768, 'g_xattn': g_xattn, 'g_ffn': g_ffn, 'L0_xattn_Wq': _L0_xattn_in['Wq'], 'L0_xattn_bq': _L0_xattn_in['bq'], 'L0_xattn_Wk': _L0_xattn_in['Wk'], 'L0_xattn_bk': _L0_xattn_in['bk'], 'L0_xattn_Wv': _L0_xattn_in['Wv'], 'L0_xattn_bv': _L0_xattn_in['bv'], 'L0_xattn_Wo': _L0_xattn_in['Wo'], 'L0_xattn_bo': _L0_xattn_in['bo'], 'L0_ffn_gate_w': _L0_ffn_in['gate_w'], 'L0_ffn_gate_bias': _L0_ffn_in['gate_bias'], 'L0_ffn_eg_w': _L0_ffn_in['eg_w'], 'L0_ffn_eu_w': _L0_ffn_in['eu_w'], 'L0_ffn_ed_w': _L0_ffn_in['ed_w'], 'L0_ffn_sg_w': _L0_ffn_in['sg_w'], 'L0_ffn_su_w': _L0_ffn_in['su_w'], 'L0_ffn_sd_w': _L0_ffn_in['sd_w'], 'L1_xattn_Wq': _L1_xattn_in['Wq'], 'L1_xattn_Wk': _L1_xattn_in['Wk'], 'L1_xattn_Wv': _L1_xattn_in['Wv'], 'L1_xattn_Wo': _L1_xattn_in['Wo'], 'L1_xattn_bo': _L1_xattn_in['bo'], 'L1_ffn_g1': _L1_ffn_in['g1'], 'L1_ffn_g2': _L1_ffn_in['g2'], 'L1_ffn_w_down': _L1_ffn_in['w_down'], 'L1_ffn_wq': _L1_ffn_in['wq'], 'L1_ffn_wk': _L1_ffn_in['wk'], 'L1_ffn_wv': _L1_ffn_in['wv'], 'L1_ffn_w_up': _L1_ffn_in['w_up'], 'L1_ffn_router_w': _L1_ffn_in['router_w'], 'L1_ffn_w1': _L1_ffn_in['w1'], 'L1_ffn_w2': _L1_ffn_in['w2'], 'L1_ffn_w3': _L1_ffn_in['w3']}

def reference(x, ctx_768, g_xattn, g_ffn, L0_xattn_Wq, L0_xattn_bq, L0_xattn_Wk, L0_xattn_bk, L0_xattn_Wv, L0_xattn_bv, L0_xattn_Wo, L0_xattn_bo, L0_ffn_gate_w, L0_ffn_gate_bias, L0_ffn_eg_w, L0_ffn_eu_w, L0_ffn_ed_w, L0_ffn_sg_w, L0_ffn_su_w, L0_ffn_sd_w, L1_xattn_Wq, L1_xattn_Wk, L1_xattn_Wv, L1_xattn_Wo, L1_xattn_bo, L1_ffn_g1, L1_ffn_g2, L1_ffn_w_down, L1_ffn_wq, L1_ffn_wk, L1_ffn_wv, L1_ffn_w_up, L1_ffn_router_w, L1_ffn_w1, L1_ffn_w2, L1_ffn_w3):
    import jax
    import jax.numpy as jnp

    def _L0_xattn_ref(query, key_value, Wq, bq, Wk, bk, Wv, bv, Wo, bo):
        import jax, jax.numpy as jnp
        import numpy as np
        NUM_HEADS = 16
        CLAMP = 10000.0
        B, Nq, Cq = query.shape
        Nkv = key_value.shape[1]
        H = NUM_HEADS
        D = Cq // H
        scale = D ** (-0.5)
        q = (query @ Wq + bq).reshape(B, Nq, H, D).transpose(0, 2, 1, 3)
        k = (key_value @ Wk + bk).reshape(B, Nkv, H, D).transpose(0, 2, 1, 3)
        v = (key_value @ Wv + bv).reshape(B, Nkv, H, D).transpose(0, 2, 1, 3)
        attn = jnp.einsum('bhqd,bhkd->bhqk', q, k) * scale
        attn = jnp.clip(attn, -CLAMP, CLAMP)
        attn = jax.nn.softmax(attn, axis=-1)
        attn = jnp.where(jnp.any(jnp.isnan(attn)), jnp.asarray(1.0 / Nkv, attn.dtype), attn)
        x = jnp.einsum('bhqk,bhkd->bqhd', attn, v).reshape(B, Nq, Cq)
        return x @ Wo + bo

    def _L0_ffn_ref(hidden_states, gate_w, gate_bias, eg_w, eu_w, ed_w, sg_w, su_w, sd_w):
        import jax, jax.numpy as jnp
        import numpy as np
        from jax import lax
        HIDDEN = 128
        INTER = 64
        E = 64
        K = 6
        G = 8
        TG = 4
        NSH = 2
        ISH = INTER * NSH

        def _moe_forward(hidden_states, gate_w, gate_bias, eg_w, eu_w, ed_w, sg_w, su_w, sd_w):
            B, S, H = hidden_states.shape
            x = hidden_states.reshape(-1, H)
            T = x.shape[0]
            shared = jax.nn.silu(x @ sg_w.T) * (x @ su_w.T) @ sd_w.T
            logits = x @ gate_w.T
            scores = jax.nn.sigmoid(logits) + gate_bias
            group_scores = scores.reshape(T, G, E // G).max(axis=-1)
            _, sel_groups = lax.top_k(group_scores, TG)
            group_mask = jnp.zeros((T, G), scores.dtype).at[jnp.arange(T)[:, None], sel_groups].set(1.0)
            mask = jnp.repeat(group_mask, E // G, axis=1)
            masked_scores = scores * mask
            topk_w, topk_i = lax.top_k(masked_scores, K)
            topk_w = topk_w / (topk_w.sum(axis=-1, keepdims=True) + 1e-08)
            comb = jnp.zeros((T, E), x.dtype).at[jnp.arange(T)[:, None], topk_i].add(topk_w)
            h = jax.nn.silu(jnp.einsum('th,eih->eti', x, eg_w)) * jnp.einsum('th,eih->eti', x, eu_w)
            routed = jnp.einsum('eti,ehi,te->th', h, ed_w, comb)
            return (shared + routed).reshape(B, S, H)
        return _moe_forward(hidden_states, gate_w, gate_bias, eg_w, eu_w, ed_w, sg_w, su_w, sd_w)

    def _L1_xattn_ref(hidden_states, encoder_hidden_states, Wq, Wk, Wv, Wo, bo):
        import jax, jax.numpy as jnp
        import numpy as np
        HEADS = 16
        DIM_HEAD = 64
        B, S, D = hidden_states.shape
        K = encoder_hidden_states.shape[1]
        H, Dh = (HEADS, DIM_HEAD)
        scale = 1.0 / np.sqrt(Dh)
        q = hidden_states @ Wq
        k = encoder_hidden_states @ Wk
        v = encoder_hidden_states @ Wv
        q = q.reshape(B, S, H, Dh).transpose(0, 2, 1, 3)
        k = k.reshape(B, K, H, Dh).transpose(0, 2, 1, 3)
        v = v.reshape(B, K, H, Dh).transpose(0, 2, 1, 3)
        scores = jnp.einsum('bhsd,bhkd->bhsk', q, k) * scale
        probs = jax.nn.softmax(scores, axis=-1)
        out = jnp.einsum('bhsk,bhkd->bhsd', probs, v)
        out = out.transpose(0, 2, 1, 3).reshape(B, S, H * Dh)
        out = out @ Wo + bo
        return out

    def _L1_ffn_ref(x, g1, g2, w_down, wq, wk, wv, w_up, router_w, w1, w2, w3):
        import jax, jax.numpy as jnp
        import numpy as np
        B, S, D = (2, 128, 128)
        L, H = (64, 16)
        HD = L // H
        F, E, K = (256, 8, 2)
        THETA = 10000.0
        EPS = 1e-05

        def _rmsnorm(x, g):
            return x * g * jax.lax.rsqrt(jnp.mean(x * x, axis=-1, keepdims=True) + EPS)

        def _rope(t, pos):
            inv_freq = 1.0 / THETA ** (jnp.arange(0, HD, 2, dtype=jnp.float32) / HD)
            ang = pos[:, None].astype(jnp.float32) * inv_freq[None, :]
            cos, sin = (jnp.cos(ang), jnp.sin(ang))
            t1, t2 = (t[..., 0::2], t[..., 1::2])
            r1 = t1 * cos - t2 * sin
            r2 = t1 * sin + t2 * cos
            return jnp.stack([r1, r2], axis=-1).reshape(t.shape)

        def _forward(x, g1, g2, w_down, wq, wk, wv, w_up, router_w, w1, w2, w3):
            b, s, _ = x.shape
            pos = jnp.arange(s)
            h = _rmsnorm(x, g1)
            c = h @ w_down
            split = lambda t: t.reshape(b, s, H, HD).transpose(0, 2, 1, 3)
            q = _rope(split(c @ wq), pos)
            k = _rope(split(c @ wk), pos)
            v = split(c @ wv)
            scores = jnp.einsum('bhqd,bhkd->bhqk', q, k) / jnp.sqrt(jnp.float32(HD))
            causal = jnp.tril(jnp.ones((s, s), bool))
            scores = jnp.where(causal, scores, -jnp.inf)
            attn = jax.nn.softmax(scores, axis=-1)
            o = jnp.einsum('bhqk,bhkd->bhqd', attn, v).transpose(0, 2, 1, 3).reshape(b, s, L)
            x = x + o @ w_up
            res = x
            t = _rmsnorm(x, g2).reshape(-1, D)
            probs = jax.nn.softmax(t @ router_w, axis=-1)
            vals, idx = jax.lax.top_k(probs, K)
            w = vals / jnp.sum(vals, axis=-1, keepdims=True)
            gate = jnp.sum(jax.nn.one_hot(idx, E, dtype=t.dtype) * w[..., None], axis=1)
            hid = jax.nn.silu(jnp.einsum('td,edf->tef', t, w1)) * jnp.einsum('td,edf->tef', t, w3)
            y_e = jnp.einsum('tef,efd->ted', hid, w2)
            y = jnp.einsum('ted,te->td', y_e, gate)
            return res + y.reshape(b, s, D)
        return _forward(x, g1, g2, w_down, wq, wk, wv, w_up, router_w, w1, w2, w3)
    x = x + jnp.tanh(g_xattn[0]) * _L0_xattn_ref(_layernorm(x, axis=-1), ctx_768, L0_xattn_Wq, L0_xattn_bq, L0_xattn_Wk, L0_xattn_bk, L0_xattn_Wv, L0_xattn_bv, L0_xattn_Wo, L0_xattn_bo)
    x = x + jnp.tanh(g_ffn[0]) * _L0_ffn_ref(_layernorm(x, axis=-1), L0_ffn_gate_w, L0_ffn_gate_bias, L0_ffn_eg_w, L0_ffn_eu_w, L0_ffn_ed_w, L0_ffn_sg_w, L0_ffn_su_w, L0_ffn_sd_w)
    x = x + jnp.tanh(g_xattn[1]) * _L1_xattn_ref(_layernorm(x, axis=-1), ctx_768, L1_xattn_Wq, L1_xattn_Wk, L1_xattn_Wv, L1_xattn_Wo, L1_xattn_bo)
    x = x + jnp.tanh(g_ffn[1]) * _L1_ffn_ref(_layernorm(x, axis=-1), L1_ffn_g1, L1_ffn_g2, L1_ffn_w_down, L1_ffn_wq, L1_ffn_wk, L1_ffn_wv, L1_ffn_w_up, L1_ffn_router_w, L1_ffn_w1, L1_ffn_w2, L1_ffn_w3)
    return x

_drawn_inputs = setup_inputs


def setup_inputs(seed=0):
    import zlib

    import numpy as np

    out = dict(_drawn_inputs(seed))
    spreads = {'g_ffn': (-1.0, 0.2),
     'L0_xattn_bq': (0.0, 0.447),
     'L0_xattn_bk': (0.0, 0.8),
     'L0_xattn_bv': (0.0, 0.1),
     'L0_xattn_bo': (0.0, 0.1),
     'L0_ffn_gate_bias': (0.0, 0.8),
     'L1_ffn_g1': (1.0, 0.6),
     'L1_ffn_g2': (1.0, 0.6)}
    factors = {'L0_ffn_gate_w': 8.0,
     'L0_ffn_eg_w': 8.0,
     'L0_ffn_eu_w': 8.0,
     'L0_ffn_ed_w': 8.0,
     'L0_ffn_sg_w': 8.0,
     'L0_ffn_su_w': 8.0,
     'L0_ffn_sd_w': 8.0,
     'L1_xattn_bo': 6.931,
     'L1_ffn_w_down': 8.0,
     'L1_ffn_wq': 8.0,
     'L1_ffn_wk': 8.0,
     'L1_ffn_wv': 8.0,
     'L1_ffn_w_up': 8.0,
     'L1_ffn_router_w': 5.179,
     'L1_ffn_w1': 4.575,
     'L1_ffn_w2': 4.545,
     'L1_ffn_w3': 4.557}
    for name, (base, spread) in spreads.items():
        noise = np.random.default_rng([zlib.crc32(name.encode()), seed]).standard_normal(out[name].shape)
        drawn = base * np.exp(spread * noise) if base else spread * noise
        out[name] = jnp.asarray(drawn.astype(out[name].dtype))
    for name, factor in factors.items():
        out[name] = (out[name] * factor).astype(out[name].dtype)
    return out
```

```python
from contextlib import ExitStack, contextmanager

import numpy as np
import concourse.bass as bass
from concourse import mybir

F32 = mybir.dt.float32
F16 = mybir.dt.float16
BF16 = mybir.dt.bfloat16
I32 = mybir.dt.int32
ALU = mybir.AluOpType
ACT = mybir.ActivationFunctionType
AX = mybir.AxisListType

P = 128
NB = 32
NQ = NB // 4
D = 128
DC = 96
NKV = 120
H = 16
HG = 4
NG = H // HG
EPS = 1e-5
CLAMP = 1e4
A_SCALE = 8 ** -0.5
C_DH = 64
E0, I0, TG0, K0 = 64, 64, 4, 6
E1, I1, K1 = 8, 256, 2
COMB_UP = 4096.0
LAT = 64


def wait(eng, sem, count):
    if isinstance(count, int) and count <= 0:
        return
    eng.wait_ge(sem, count)


@contextmanager
def stepped(eng, start, end, step):
    with eng.Fori(start // step, end // step) as k:
        yield k * step


def absent(base, k, items):
    return isinstance(base, int) and not 0 <= base + k < items


def build(nc, x, ctxT, gx, gf, w, consts, out, stop_after=99):
    top = ExitStack()
    with top:
        def sb(name, shape, dt=F32, ctx=top):
            return ctx.enter_context(nc.sbuf_tensor(name, shape, dt))

        in_use = []

        def sem(name):
            in_use.append(nc.alloc_semaphore(name))
            return in_use[-1]

        def renew_semaphores():
            nc.clear_and_free_semaphores(list(in_use))
            in_use.clear()
            nc.all_engine_barrier()

        bank = [top.enter_context(nc.psum_tensor(f"bank{i}", [P, 512], F32)) for i in range(8)]

        X = sb("X", [P, NB, D])
        XC = sb("XC", [P, NB, D])
        stat = sb("stat", [P, 4, NB])
        ident = sb("ident", [P, P])
        ones = sb("ones", [P, P])
        gates = sb("gates", [P, 4])
        tg = sb("tg", [P, 4])
        headsel = sb("headsel", [P, HG])

        s_load = sem("loaded")
        s_tg = sem("gates_tanh")
        s_zrow = sem("zero_rows_set")
        small = {}

        def load_small(name, shape):
            small[name] = sb("w_" + name, shape)
            return small[name]

        for name, shape in (("a_wq", [D, D]), ("a_wk", [DC, D]), ("a_wv", [DC, D]),
                            ("a_bq", [D, 1]), ("a_bk", [D, 1]), ("a_bvc", [D, 1]), ("a_wo", [D, D]), ("a_gate", [D, E0]),
                            ("sgT", [D, D]), ("suT", [D, D]), ("sdT", [D, D]),
                            ("c_wv", [DC, H * C_DH]), ("g1", [D, 1]), ("g2", [D, 1]),
                            ("d_down", [D, LAT]), ("d_q", [LAT, LAT]), ("d_k", [LAT, LAT]),
                            ("d_v", [LAT, LAT]), ("d_router", [D, E1])):
            load_small(name, shape)
        c_wo = sb("c_wo", [P, 8, D])
        a_wo4 = sb("a_wo4", [32, NG, D])
        d_up4 = sb("d_up4", [32, NG, D])
        mT = sb("mT", [DC, H, D])
        bo0 = sb("bo0", [P, D])
        bo1 = sb("bo1", [P, D])
        bv0 = sb("bv0", [P, D])
        gb0 = sb("gb0", [P, E0])
        rope = sb("rope", [P, 4, P])
        causal = sb("causal", [P, P])
        causal16 = sb("causal16", [P, HG, P], BF16)
        ident16 = sb("ident16", [P, P], BF16)
        identh = sb("identh", [P, P], F16)

        prep = ExitStack()
        wkT = sb("wkT", [C_DH, H, DC], ctx=prep)
        wqT = sb("wqT", [C_DH, H, D], ctx=prep)
        s_mt = sem("m_ready")
        s_mtfree = sem("m_copied")
        s_const = sem("constants_ready")
        n_loads = []
        with nc.Block() as block:
            @block.sync
            def _(sp):
                def load(dst, src):
                    sp.dma_start(dst, src).then_inc(s_load, 16)
                    n_loads.append(1)
                for q in range(4):
                    load(X[:, 8 * q:8 * q + 8, :], x[8 * q:8 * q + 8].rearrange("b t d -> t b d"))
                for name, t in small.items():
                    load(t[:], w[name])
                sp.wait_ge(s_zrow, 1)
                load(a_wo4[:], w["a_wo"].rearrange("(g r) n -> r g n", g=NG))
                for j in range(HG):
                    load(d_up4[8 * j:8 * j + 4], w["d_up"].rearrange("(g j d) n -> j d g n", g=NG, j=HG)[j])
                load(c_wo[:], w["c_wo"].rearrange("(j p) d -> p j d", p=P))
                load(wkT[:], w["c_wkT"].rearrange("(h p) e -> p h e", p=C_DH))
                load(wqT[:], w["c_wqT"].rearrange("(h p) d -> p h d", p=C_DH))
                for t, name in ((bo0, "a_bo"), (bo1, "c_bo"), (bv0, "a_bv"), (gb0, "a_gbias")):
                    load(t[:], w[name].partition_broadcast(P))
                load(gates[:, 0:2], gx.partition_broadcast(P))
                load(gates[:, 2:4], gf.partition_broadcast(P))
                load(ident[:], consts["ident"])
                load(headsel[:], consts["headsel"])
                load(rope[:], consts["rope"])
                load(causal[:], consts["causal"])
                sp.wait_ge(s_load, 16 * len(n_loads))

            all_loads = 16 * len(n_loads)

            @block.gpsimd
            def _(pool):
                pool.memset(d_up4[:], 0.0).then_inc(s_zrow, 1)
                pool.memset(ones[:], 1.0)
                pool.wait_ge(s_load, all_loads)
                pool.tensor_copy(ident16[:], ident[:])
                pool.tensor_copy(identh[:], ident[:])
                pool.tensor_copy(causal16[:], causal[:].unsqueeze(1).broadcast_to([P, HG, P]))

            @block.scalar
            def _(act):
                act.wait_ge(s_load, all_loads)
                act.activation(tg[:], gates[:], ACT.Tanh).then_inc(s_tg, 1)
                for g in range(NG):
                    act.wait_ge(s_mt, g + 1)
                    act.activation(mT[:, HG * g:HG * g + HG, :], bank[g][0:DC, :].rearrange("p (h d) -> p h d", h=HG),
                                   ACT.Copy, scale=C_DH ** -0.5)

            @block.tensor
            def _(pe):
                pe.wait_ge(s_load, all_loads)
                for g in range(NG):
                    for j in range(HG):
                        h = HG * g + j
                        last = pe.matmul(bank[g][0:DC, j * D:(j + 1) * D], wkT[:, h, :], wqT[:, h, :],
                                         start=True, stop=True)
                    last.then_inc(s_mt, 1)

            @block.vector
            def _(dve):
                dve.wait_ge(s_tg, 1)
                dve.tensor_scalar(small["a_wo"][:], small["a_wo"][:], tg[:, 0:1], None, ALU.mult)
                dve.tensor_scalar(a_wo4[:], a_wo4[:], tg[0:32, 0:1], None, ALU.mult)
                dve.tensor_scalar(c_wo[:], c_wo[:], tg[:, 1:2], None, ALU.mult)
                dve.tensor_scalar(bo0[:], bo0[:], tg[:, 0:1], None, ALU.mult)
                dve.tensor_scalar(bo1[:], bo1[:], tg[:, 1:2], None, ALU.mult)
                dve.tensor_scalar(small["a_bq"][:], small["a_bq"][:], A_SCALE, None, ALU.mult)
        prep.close()

        def stats(tag, bias=None, second=False, src=X):
            s_v = sem(tag + "_dve")
            s_sq = sem(tag + "_squared")
            s_rs = sem(tag + "_rstd")
            s_exp = sem(tag + "_exponent_set")
            own = ExitStack()
            sq = sb(tag + "_sq", [P, NB, D], ctx=own)
            expo = sb(tag + "_expo", [P, NB], ctx=own)
            rms_only = src is XC
            with nc.Block() as block:
                @block.vector
                def _(dve):
                    done = 0
                    if not rms_only:
                        dve.tensor_reduce(stat[:, 0, :], X[:], AX.X, ALU.add).then_inc(s_v, 1)
                        dve.wait_ge(s_v, 1)
                        dve.tensor_scalar(stat[:, 1, :], stat[:, 0, :], 1.0 / D, None, ALU.mult).then_inc(s_v, 1)
                        dve.wait_ge(s_v, 2)
                        dve.tensor_tensor(XC[:], X[:], stat[:, 1, :].unsqueeze(2).broadcast_to([P, NB, D]),
                                          ALU.subtract).then_inc(s_v, 1)
                        done = 3
                        if bias is not None:
                            dve.tensor_tensor(X[:], X[:], bias[:].unsqueeze(1).broadcast_to([P, NB, D]), ALU.add)
                    dve.wait_ge(s_sq, 1)
                    dve.tensor_reduce(stat[:, 2, :], sq[:], AX.X, ALU.add).then_inc(s_v, 1)
                    dve.wait_ge(s_v, done + 1)
                    dve.tensor_scalar(stat[:, 2, :], stat[:, 2, :], 1.0 / D, EPS, ALU.mult, ALU.add).then_inc(s_v, 1)
                    if second:
                        dve.wait_ge(s_rs, 1)
                        dve.tensor_tensor(XC[:], XC[:], stat[:, 3, :].unsqueeze(2).broadcast_to([P, NB, D]),
                                          ALU.mult).then_inc(s_v, 1)
                        dve.wait_ge(s_sq, 2)
                        dve.tensor_reduce(stat[:, 2, :], sq[:], AX.X, ALU.add).then_inc(s_v, 1)
                        dve.wait_ge(s_v, done + 4)
                        dve.tensor_scalar(stat[:, 2, :], stat[:, 2, :], 1.0 / D, EPS, ALU.mult,
                                          ALU.add).then_inc(s_v, 1)

                @block.scalar
                def _(act):
                    if not rms_only:
                        act.wait_ge(s_v, 3)
                    act.activation(sq[:], XC[:], ACT.Square).then_inc(s_sq, 1)
                    if second:
                        act.wait_ge(s_v, 6)
                        act.activation(sq[:], XC[:], ACT.Square).then_inc(s_sq, 1)

                @block.gpsimd
                def _(pool):
                    pool.memset(expo[:], -0.5).then_inc(s_exp, 1)
                    pool.wait_ge(s_exp, 1)
                    n = 2 if rms_only else 5
                    pool.wait_ge(s_v, n)
                    pool.tensor_tensor(stat[:, 3, :], stat[:, 2, :], expo[:], ALU.pow).then_inc(s_rs, 1)
                    if second:
                        pool.wait_ge(s_v, n + 3)
                        pool.tensor_tensor(stat[:, 3, :], stat[:, 2, :], expo[:], ALU.pow).then_inc(s_rs, 1)
            own.close()

        class Norm:

            def __init__(self, tag, ctx, banks, gain=None, lookahead=1):
                self.xn = [sb(f"{tag}_xn{i}", [P, 4, D], ctx=ctx) for i in range(2)]
                self.xs = [sb(f"{tag}_xs{i}", [P, 512], ctx=ctx) for i in range(2)]
                self.banks, self.gain = banks, gain
                self.s_scaled = sem(tag + "_scaled")
                self.s_turned = sem(tag + "_turned")
                self.s_xs = sem(tag + "_xs")
                self.s_used = sem(tag + "_xs_used")

            def scale(self, dve, q, u):
                wait(dve, self.s_turned, q - 1)
                dve.tensor_tensor(self.xn[u][:], XC[:, bass.ds(q * 4, 4), :],
                                  stat[:, 3, bass.ds(q * 4, 4)].unsqueeze(2).broadcast_to([P, 4, D]),
                                  ALU.mult).then_inc(self.s_scaled, 1)

            def turn(self, pe, q, u):
                pe.wait_ge(self.s_scaled, q + 1)
                wait(pe, self.s_xs, q - 1)
                for j in range(4):
                    t = pe.transpose(self.banks[u][:, j * P:(j + 1) * P], self.xn[u][:, j, :], ident[:])
                t.then_inc(self.s_turned, 1)

            def copy(self, act, q, u):
                act.wait_ge(self.s_turned, q + 1)
                wait(act, self.s_used, q - 1)
                if self.gain is None:
                    i = act.activation(self.xs[u][:], self.banks[u][:], ACT.Copy)
                else:
                    i = act.activation(self.xs[u][:], self.banks[u][:], ACT.Copy, scale=self.gain[:, 0:1])
                i.then_inc(self.s_xs, 1)

        def over_quads(eng, body):
            body(0, 0)
            body(1, 1)
            with stepped(eng, 2, NQ, 2) as q:
                body(q, 0)
                body(q + 1, 1)

        def attend(tag, ctx, QT, KT, V, nk, wo, raw, dst):
            clamp = raw is not None
            qs = [sb(f"{tag}_qs{i}", [P, P], ctx=ctx) for i in range(2)]
            kd = [sb(f"{tag}_kd{i}", [P, HG, nk], ctx=ctx) for i in range(2)]
            vh = [sb(f"{tag}_vh{i}", [nk, H, 64], ctx=ctx) for i in range(2)]
            prob = [sb(f"{tag}_prob{i}", [P, HG, nk], ctx=ctx) for i in range(4)]
            probT = [sb(f"{tag}_probT{i}", [nk, HG * P], ctx=ctx) for i in range(2)]
            negmax = sb(tag + "_negmax", [P, 4, HG], ctx=ctx)
            shift = sb(tag + "_shift", [P, 4, HG], ctx=ctx)
            floor = sb(tag + "_floor", [P, 4, HG], ctx=ctx)
            low = sb(tag + "_low", [P, 1], ctx=ctx)
            recip = [sb(f"{tag}_recip{i}", [32, NG * P], ctx=ctx) for i in range(2)]
            headT = [sb(f"{tag}_headT{i}", [32, NG * P], ctx=ctx) for i in range(2)]
            score_b, turn_b, out_b = bank[0:4], bank[4:6], bank[6:8]
            s_prep = sem(tag + "_keys_spread")
            s_vprep = sem(tag + "_values_spread")
            s_clear = sem(tag + "_values_cleared")
            s_score = sem(tag + "_scores")
            s_max = sem(tag + "_rowmax")
            s_shift = sem(tag + "_shift_ready")
            s_exp = sem(tag + "_exp")
            s_floor = sem(tag + "_floor_done")
            s_turn = sem(tag + "_probs_turned")
            s_copied = sem(tag + "_probs_copied")
            s_pv = sem(tag + "_pv")
            s_recip = sem(tag + "_recip_ready")
            s_head = sem(tag + "_heads_ready")
            s_y = sem(tag + "_projected")
            s_out = sem(tag + "_out_done")
            s_low = sem(tag + "_low_ready")
            s_probs = s_floor if clamp else s_exp

            def at(bb, k):
                return bb + k // NG, k % NG, (k // NG) % 2

            def own_columns(t, first):
                flat = t[:].rearrange("p h c -> p (h c)")
                head0 = flat[:, first:first + 8].unsqueeze(1).unsqueeze(1)
                return bass.AP(head0.tensor, head0.offset,
                               [list(flat.ap[0]), [HG * 64, NG], [64 + 8, HG], [1, 8]])

            with nc.Block() as block:
                @block.gpsimd
                def _(pool):
                    def spread(b, u):
                        wait(pool, s_score, b * 4 - 4)
                        pool.tensor_copy(qs[u][:], QT[:, bass.ds(b * P, P)])
                        pool.tensor_tensor(kd[u][:], KT[:, bass.ds(b * nk, nk)].unsqueeze(1).broadcast_to([P, HG, nk]),
                                           headsel[:].unsqueeze(2).broadcast_to([P, HG, nk]),
                                           ALU.mult).then_inc(s_prep, 1)

                    def spread_values(b, u):
                        wait(pool, s_pv, b * 4 - 4)
                        pool.tensor_copy(own_columns(vh[u], 0),
                                         V[:, bass.ds(b * P, P)].rearrange("p (g j d) -> p g j d", g=NG, j=HG))\
                            .then_inc(s_vprep, 1)

                    pool.memset(low[:], -CLAMP).then_inc(s_low, 1)
                    for u in range(2):
                        i = pool.memset(vh[u][:], 0.0)
                    i.then_inc(s_clear, 1)
                    pool.wait_ge(s_clear, 1)
                    for u in range(2):
                        i = pool.memset(own_columns(vh[u], 32), 1.0)
                    i.then_inc(s_clear, 1)
                    spread(0, 0)

                    def slot(bb, j):
                        b, g, u = at(bb, j)
                        if g == 1 and not absent(bb, j // 4 + 1, NB):
                            spread(b + 1, 1 - u)
                        if g == 2:
                            spread_values(b, u)

                    pipeline_b(pool, slot, 0)

                @block.tensor
                def _(pe):
                    pe.wait_ge(s_clear, 2)

                    def slot(bb, j):
                        if not absent(bb, j // 4, NB):
                            b, g, u = at(bb, j)
                            n = bb * 4 + j
                            if g == 0:
                                pe.wait_ge(s_prep, b + 1)
                            wait(pe, s_exp, n - 3)
                            if not clamp:
                                pe.matmul(score_b[g][:], ident16[:], causal16[:].rearrange("p h k -> p (h k)"),
                                          start=True, stop=False)
                            pe.matmul(score_b[g][:, 0:HG * nk], qs[u][32 * g:32 * g + 32, :],
                                      kd[u][32 * g:32 * g + 32].rearrange("p h k -> p (h k)"),
                                      start=clamp, stop=True).then_inc(s_score, 1)
                        if not absent(bb, (j - 3) // 4, NB):
                            b, g, u = at(bb, j - 3)
                            n = bb * 4 + (j - 3)
                            pe.wait_ge(s_probs, n + 1)
                            wait(pe, s_copied, n - 1)
                            for h in range(HG):
                                t = pe.transpose(turn_b[g % 2][0:nk, h * P:(h + 1) * P], prob[g][:, h, :], ident[:])
                            t.then_inc(s_turn, 1)
                        if not absent(bb, (j - 4) // 4, NB):
                            b, g, u = at(bb, j - 4)
                            n = bb * 4 + (j - 4)
                            pe.wait_ge(s_copied, n + 1)
                            if g == 0:
                                pe.wait_ge(s_vprep, b + 1)
                                wait(pe, s_out, b - 1)
                            for h in range(HG):
                                t = pe.matmul(out_b[u][0:64, g * P:(g + 1) * P], vh[u][:, g * HG + h, :],
                                              probT[g % 2][:, h * P:(h + 1) * P], start=(h == 0), stop=(h == HG - 1))
                            t.then_inc(s_pv, 1)
                        if (j - 6) % 4 == 3 and not absent(bb, (j - 6) // 4, NB):
                            b, g, u = at(bb, j - 6)
                            pe.wait_ge(s_head, b + 1)
                            for g in range(NG):
                                t = pe.matmul(out_b[u][:, 0:D], headT[u][:, g * P:(g + 1) * P], wo[:, g, :],
                                              start=(g == 0), stop=(g == NG - 1))
                            t.then_inc(s_y, 1)

                    pipeline_b(pe, slot, 6)

                def copy_probs(eng, bb, k):
                    n = bb * 4 + k
                    g = k % NG
                    eng.wait_ge(s_turn, n + 1)
                    wait(eng, s_pv, n - 1)
                    if not clamp:
                        wait(eng, s_copied, n)
                    if clamp or g % 2:
                        i = nc.scalar.activation(probT[g % 2][:], turn_b[g % 2][0:nk, :], ACT.Copy)
                    else:
                        i = nc.vector.tensor_copy(probT[0][:], turn_b[0][0:nk, :])
                    i.then_inc(s_copied, 1)

                @block.scalar
                def _(act):
                    act.wait_ge(s_low, 1)

                    def slot(bb, j):
                        if not absent(bb, j // 4, NB):
                            b, g, u = at(bb, j)
                            n = bb * 4 + j
                            act.wait_ge(s_shift, n + 1)
                            wait(act, s_turn, n - 3)
                            if clamp:
                                act.activation(floor[:, g, :], shift[:, g, :], ACT.Exp, bias=low[:, 0:1])
                            for h in range(HG):
                                acc = raw[:, bass.ds(n * 4 + h, 1)] if clamp else None
                                i = act.activation(prob[g][:, h, :], score_b[g][:, h * nk:(h + 1) * nk], ACT.Exp,
                                                   bias=shift[:, g, h:h + 1], accum_out=acc)
                            i.then_inc(s_exp, 1)
                        if not absent(bb, (j - 3) // 4, NB) and (clamp or (j - 3) % 2 == 1):
                            copy_probs(act, bb, j - 3)

                    pipeline_b(act, slot, 3)

                @block.vector
                def _(dve):
                    def slot(bb, j):
                        if not absent(bb, j // 4, NB):
                            b, g, u = at(bb, j)
                            n = bb * 4 + j
                            dve.wait_ge(s_score, n + 1)
                            wait(dve, s_exp, n - 3)
                            to = negmax if clamp else shift
                            i = dve.tensor_reduce(to[:, g, :], score_b[g][:, 0:HG * nk].rearrange("p (h k) -> p h k", h=HG),
                                                  AX.X, ALU.max, negate=True)
                            i.then_inc(s_max if clamp else s_shift, 1)
                            if clamp:
                                dve.wait_ge(s_max, n + 1)
                                dve.tensor_scalar(shift[:, g, :], negmax[:, g, :], CLAMP, -CLAMP, ALU.min,
                                                  ALU.max).then_inc(s_shift, 1)
                        if clamp and not absent(bb, (j - 1) // 4, NB):
                            g = (j - 1) % NG
                            dve.wait_ge(s_exp, bb * 4 + j)
                            dve.scalar_tensor_tensor(prob[g][:], prob[g][:], 1.0,
                                                     floor[:, g, :].unsqueeze(2).broadcast_to([P, HG, nk]),
                                                     ALU.min, ALU.max).then_inc(s_floor, 1)
                        if not clamp and not absent(bb, (j - 3) // 4, NB) and (j - 3) % 2 == 0:
                            copy_probs(dve, bb, j - 3)
                        if (j - 5) % 4 == 3 and not absent(bb, (j - 5) // 4, NB):
                            b, g, u = at(bb, j - 5)
                            dve.wait_ge(s_pv, b * 4 + 4)
                            dve.reciprocal(recip[u][:], out_b[u][32:64, :]).then_inc(s_recip, 1)
                            dve.wait_ge(s_recip, b + 1)
                            wait(dve, s_y, b - 1)
                            dve.tensor_tensor(headT[u][:], out_b[u][0:32, :], recip[u][:], ALU.mult).then_inc(s_head, 1)
                        if (j - 7) % 4 == 3 and not absent(bb, (j - 7) // 4, NB):
                            b, g, u = at(bb, j - 7)
                            dve.wait_ge(s_y, b + 1)
                            d = dst[:, bass.ds(b, 1), :].rearrange("p b d -> p (b d)")
                            if clamp:
                                i = dve.tensor_copy(d, out_b[u][:, 0:D])
                            else:
                                i = dve.tensor_tensor(d, out_b[u][:, 0:D], d, ALU.add)
                            i.then_inc(s_out, 1)

                    pipeline_b(dve, slot, 7)

        def pipeline_b(eng, slot, tail):
            for bb in (0, 2):
                for j in range(8):
                    slot(bb, j)
            with stepped(eng, 4, NB - 2, 2) as bb:
                for j in range(8):
                    slot(bb, j)
            for j in range(8 + tail):
                slot(NB - 2, j)

        def dump():
            s_dump = sem("dumped")
            with nc.Block() as block:
                @block.sync
                def _(sp):
                    sp.dma_start(out.rearrange("b t d -> t b d"), X[:]).then_inc(s_dump, 16)
                    sp.wait_ge(s_dump, 16)

        stats("a_stat", bias=bo0)
        att = ExitStack()
        Y = sb("a_Y", [P, NB, D], ctx=att)
        cmean = sb("a_cmean", [DC, NB], ctx=att)
        raw = sb("a_raw", [P, NB * H], ctx=att)
        QT = sb("a_QT", [P, NB * P], ctx=att)
        KT = sb("a_KT", [P, NB * NKV], ctx=att)
        V = sb("a_V", [NKV, NB * D], ctx=att)
        own = ExitStack()
        norm = Norm("a", own, bank[0:2])
        cs = [sb(f"a_cs{i}", [DC, 4, NKV], ctx=own) for i in range(2)]
        s_cs = [sem(f"a_ctx_loaded{i}") for i in range(2)]
        s_kq = sem("a_qk_products")
        s_v = sem("a_v_product")
        s_qcopy = sem("a_q_copied")
        s_kcopy = sem("a_k_copied")
        s_vcopy = sem("a_v_copied")
        s_mean = sem("a_context_summed")
        with nc.Block() as block:
            @block.sync
            def _(sp):
                def body(q, u):
                    wait(sp, s_v, q - 1)
                    wait(sp, s_mean, q - 1)
                    sp.dma_start(cs[u][:], ctxT[bass.ds(q * 4, 4)].rearrange("b e t -> e b t")).then_inc(s_cs[u], 16)
                over_quads(sp, body)

            @block.tensor
            def _(pe):
                def body(q, u):
                    norm.turn(pe, q, u)
                    pe.wait_ge(s_cs[u], (q // 2) * 16 + 16 if isinstance(q, int) else (q - u) * 8 + 16)
                    wait(pe, s_kcopy, q)
                    pe.matmul(bank[3][:, 0:4 * NKV], small["a_wk"][:], cs[u][:].rearrange("p b t -> p (b t)"),
                              start=True, stop=True)
                    pe.wait_ge(norm.s_xs, q + 1)
                    wait(pe, s_qcopy, q)
                    pe.matmul(bank[2][:], small["a_wq"][:], norm.xs[u][:], start=True, stop=True).then_inc(norm.s_used, 1)
                    wait(pe, s_vcopy, q)
                    for j in range(4):
                        t = pe.matmul(bank[4][0:NKV, j * D:(j + 1) * D], cs[u][:, j, :], small["a_wv"][:],
                                      start=True, stop=True)
                    t.then_inc(s_v, 1)
                over_quads(pe, body)

            @block.scalar
            def _(act):
                def body(q, u):
                    norm.copy(act, q, u)
                    act.wait_ge(norm.s_used, q + 1)
                    act.activation(QT[:, bass.ds(q * 512, 512)], bank[2][:], ACT.Identity, scale=A_SCALE,
                                   bias=small["a_bq"][:, 0:1]).then_inc(s_qcopy, 1)
                over_quads(act, body)

            @block.vector
            def _(dve):
                def body(q, u):
                    norm.scale(dve, q, u)
                    dve.wait_ge(s_v, q + 1)
                    dve.tensor_scalar(KT[:, bass.ds(q * 4 * NKV, 4 * NKV)], bank[3][:, 0:4 * NKV],
                                      small["a_bk"][:, 0:1], None, ALU.add).then_inc(s_kcopy, 1)
                    dve.tensor_tensor(V[:, bass.ds(q * 512, 512)].rearrange("p (b c) -> p b c", b=4),
                                      bank[4][0:NKV, :].rearrange("p (b c) -> p b c", b=4),
                                      bv0[0:NKV, :].unsqueeze(1).broadcast_to([NKV, 4, D]), ALU.add)\
                        .then_inc(s_vcopy, 1)
                    dve.tensor_reduce(cmean[:, bass.ds(q * 4, 4)], cs[u][:], AX.X, ALU.add).then_inc(s_mean, 1)
                over_quads(dve, body)
        own.close()

        own = ExitStack()
        attend("a_att", own, QT, KT, V, NKV, a_wo4, raw, Y)
        own.close()

        own = ExitStack()
        odd = sb("odd", [P, NB * H], ctx=own)
        anyodd = sb("anyodd", [P, 1], ctx=own)
        oddmask = sb("oddmask", [P, 1], I32, ctx=own)
        vmeanT = sb("vmeanT", [D, NB], ctx=own)
        s_odd = sem("odd_found")
        s_oddsum = sem("odd_summed")
        s_vm = sem("mean_values")
        s_vmc = sem("mean_values_copied")
        s_flat = sem("uniform_projected")
        s_pick = sem("uniform_picked")
        with nc.Block() as block:
            @block.vector
            def _(dve):
                dve.tensor_tensor(odd[:], raw[:], raw[:], ALU.not_equal).then_inc(s_odd, 1)
                dve.wait_ge(s_odd, 1)
                dve.tensor_reduce(anyodd[:], odd[:], AX.X, ALU.max).then_inc(s_odd, 1)
                dve.wait_ge(s_oddsum, 1)
                dve.tensor_scalar(oddmask[:], bank[0][:, 0:1], 0.0, None, ALU.is_gt).then_inc(s_odd, 1)
                dve.wait_ge(s_odd, 3)
                for q in range(NQ):
                    dve.wait_ge(s_flat, q + 1)
                    dve.copy_predicated(Y[:, 4 * q:4 * q + 4, :].rearrange("p b d -> p (b d)"),
                                        oddmask[:].broadcast_to([P, 512]), bank[2 + q % 2][:]).then_inc(s_pick, 1)
                dve.wait_ge(s_pick, NQ)
                dve.tensor_tensor(X[:], X[:], Y[:], ALU.add)

            @block.scalar
            def _(act):
                act.wait_ge(s_vm, 1)
                act.activation(vmeanT[:], bank[1][:, 0:NB], ACT.Identity, scale=1.0 / NKV,
                               bias=small["a_bvc"][:, 0:1]).then_inc(s_vmc, 1)

            @block.tensor
            def _(pe):
                pe.matmul(bank[1][:, 0:NB], small["a_wv"][:], cmean[:], start=True, stop=True).then_inc(s_vm, 1)
                pe.wait_ge(s_odd, 2)
                pe.matmul(bank[0][:, 0:1], ones[:], anyodd[:], start=True, stop=True).then_inc(s_oddsum, 1)
                pe.wait_ge(s_vmc, 1)
                for q in range(NQ):
                    wait(pe, s_pick, q - 1)
                    for j in range(4):
                        t = pe.matmul(bank[2 + q % 2][:, j * D:(j + 1) * D],
                                      vmeanT[:, 4 * q + j:4 * q + j + 1].broadcast_to([D, P]), small["a_wo"][:],
                                      start=True, stop=True)
                    t.then_inc(s_flat, 1)
        own.close()
        att.close()
        if stop_after == 1:
            return dump()

        def experts(tag, XT, combT, nrows, wg, wu, wd, sel, units, start_from_zero, YT):
            own = ExitStack()
            groups = units // 4
            wgs = [sb(f"{tag}_wg{i}", [P, 512], ctx=own) for i in range(2)]
            wus = [sb(f"{tag}_wu{i}", [P, 512], ctx=own) for i in range(2)]
            wds = [sb(f"{tag}_wd{i}", [P, 4, D], ctx=own) for i in range(2)]
            sels = [sb(f"{tag}_sel{i}", [nrows, 512], F16, ctx=own) for i in range(2)]
            act_s = [sb(f"{tag}_silu{i}", [P, 512], ctx=own) for i in range(2)]
            gu = [sb(f"{tag}_gu{i}", [P, 512], ctx=own) for i in range(2)]
            hid = [sb(f"{tag}_hid{i}", [P, 512], ctx=own) for i in range(4)]
            gate_b, up_b, comb_b, down_b = bank[0:2], bank[2:4], bank[4:6], bank[6:8]
            s_w = [sem(f"{tag}_weights{i}") for i in range(2)]
            s_zero = sem(tag + "_sum_cleared")
            s_g = sem(tag + "_gate")
            s_u = sem(tag + "_up")
            s_c = sem(tag + "_comb")
            s_silu = sem(tag + "_silu_done")
            s_gu = sem(tag + "_gated")
            s_h = sem(tag + "_hidden")
            s_d = sem(tag + "_down")
            s_y = sem(tag + "_summed")

            def walk(eng, pair):
                def group(gr, wb, first):
                    pair(gr, 0, wb, None if first else 1 - wb)
                    with stepped(eng, 2, NQ, 2) as c:
                        pair(gr, c, wb, wb)
                group(0, 0, True)
                group(1, 1, False)
                with stepped(eng, 2, groups, 2) as gr:
                    group(gr, 0, False)
                    group(gr + 1, 1, False)

            def unit(gr, c, k):
                return gr * 32 + c * 4 + k

            with nc.Block() as block:
                @block.sync
                def _(sp):
                    def group(gr, wb):
                        wait(sp, s_d, gr * 32 - 32)
                        for dst, src in ((wgs, wg), (wus, wu)):
                            sp.dma_start(dst[wb][:], src[:, bass.ds(gr * 512, 512)]).then_inc(s_w[wb], 16)
                        sp.dma_start(wds[wb][:], wd[bass.ds(gr * 512, 512)].rearrange("(u p) d -> p u d", p=P))\
                            .then_inc(s_w[wb], 16)
                        sp.dma_start(sels[wb][:], sel[:, bass.ds(gr * 512, 512)]).then_inc(s_w[wb], 16)
                    group(0, 0)
                    group(1, 1)
                    with stepped(sp, 2, groups, 2) as gr:
                        group(gr, 0)
                        group(gr + 1, 1)

                if start_from_zero:
                    @block.gpsimd
                    def _(pool):
                        pool.memset(YT[:], 0.0).then_inc(s_zero, 1)

                @block.tensor
                def _(pe):
                    def down(gr, c, k, wb):
                        n = unit(gr, c, k)
                        u = k % 4
                        pe.wait_ge(s_h, n + 1)
                        if u == 0:
                            i = gr * 8 + c + k // 4
                            wait(pe, s_y, i - 1)
                        pe.matmul(down_b[(k // 4) % 2][:], wds[wb][:, u, :], hid[k % 4][:], start=(u == 0),
                                  stop=(u == 3)).then_inc(s_d, 1)

                    def pair(gr, c, wb, before):
                        for j in range(8):
                            n = unit(gr, c, j)
                            u = j % 4
                            chunk = bass.ds((c + j // 4) * 512, 512)
                            if j == 0 and isinstance(c, int):
                                pe.wait_ge(s_w[wb], (gr - wb) * 32 + 64)
                            wait(pe, s_silu, n - 1)
                            pe.matmul(gate_b[j % 2][:], wgs[wb][:, u * P:(u + 1) * P], XT[:, chunk],
                                      start=True, stop=True).then_inc(s_g, 1)
                            wait(pe, s_gu, n - 1)
                            pe.matmul(up_b[j % 2][:], wus[wb][:, u * P:(u + 1) * P], XT[:, chunk],
                                      start=True, stop=True).then_inc(s_u, 1)
                            wait(pe, s_h, n - 1)
                            pe.matmul(comb_b[j % 2][:], sels[wb][:, u * P:(u + 1) * P], combT[:, chunk],
                                      start=True, stop=True).then_inc(s_c, 1)
                            if j >= 2:
                                down(gr, c, j - 2, wb)
                            elif before is not None:
                                down(gr, c, j - 2, before)
                    walk(pe, pair)
                    for k in (6, 7):
                        down(groups - 1, NQ - 2, k, 1)

                @block.scalar
                def _(act):
                    def pair(gr, c, wb, before):
                        for j in range(8):
                            n = unit(gr, c, j)
                            act.wait_ge(s_g, n + 1)
                            wait(act, s_gu, n - 1)
                            act.activation(act_s[j % 2][:], gate_b[j % 2][:], ACT.Silu).then_inc(s_silu, 1)
                    walk(act, pair)

                @block.vector
                def _(dve):
                    def add(gr, c, k):
                        n = unit(gr, c, k)
                        cc = c + k // 4
                        if isinstance(cc, int) and cc < 0:
                            cc += NQ
                        dve.wait_ge(s_d, n + 1)
                        y = YT[:, bass.ds(cc * 512, 512)]
                        dve.tensor_tensor(y, down_b[(k // 4) % 2][:], y, ALU.add).then_inc(s_y, 1)

                    def pair(gr, c, wb, before):
                        for j in range(8):
                            n = unit(gr, c, j)
                            dve.wait_ge(s_u, n + 1)
                            dve.wait_ge(s_silu, n + 1)
                            wait(dve, s_h, n - 1)
                            dve.tensor_tensor(gu[j % 2][:], up_b[j % 2][:], act_s[j % 2][:], ALU.mult).then_inc(s_gu, 1)
                            dve.wait_ge(s_gu, n + 1)
                            dve.wait_ge(s_c, n + 1)
                            wait(dve, s_d, n - 3)
                            dve.tensor_tensor(hid[j % 4][:], comb_b[j % 2][:], gu[j % 2][:], ALU.mult).then_inc(s_h, 1)
                            if (j - 3) % 4 == 3 and (j >= 3 or before is not None):
                                add(gr, c, j - 3)
                    if start_from_zero:
                        dve.wait_ge(s_zero, 1)
                    walk(dve, pair)
                    add(groups - 1, NQ - 2, 7)
            own.close()

        def add_experts(tag, YT, gate, store):
            own = ExitStack()
            ys = [sb(f"{tag}_ys{i}", [P, 512], ctx=own) for i in range(2)]
            s_ys = sem(tag + "_placed")
            s_t = sem(tag + "_turned")
            s_x = sem(tag + "_added")
            s_st = sem(tag + "_stored")
            with nc.Block() as block:
                @block.scalar
                def _(act):
                    def body(q, u):
                        wait(act, s_t, q - 1)
                        act.activation(ys[u][:], YT[:, bass.ds(q * 512, 512)], ACT.Copy,
                                       scale=gate).then_inc(s_ys, 1)
                    over_quads(act, body)

                @block.tensor
                def _(pe):
                    def body(q, u):
                        pe.wait_ge(s_ys, q + 1)
                        wait(pe, s_x, q - 1)
                        for j in range(4):
                            t = pe.transpose(bank[u][:, j * P:(j + 1) * P], ys[u][:, j * P:(j + 1) * P], ident[:])
                        t.then_inc(s_t, 1)
                    over_quads(pe, body)

                @block.vector
                def _(dve):
                    def body(q, u):
                        dve.wait_ge(s_t, q + 1)
                        d = X[:, bass.ds(q * 4, 4), :].rearrange("p b d -> p (b d)")
                        dve.tensor_tensor(d, bank[u][:], d, ALU.add).then_inc(s_x, 1)
                    over_quads(dve, body)

                if store:
                    @block.sync
                    def _(sp):
                        def body(q, u):
                            sp.wait_ge(s_x, q + 1)
                            sp.dma_start(out[bass.ds(q * 4, 4)].rearrange("b t d -> t b d"),
                                         X[:, bass.ds(q * 4, 4), :]).then_inc(s_st, 16)
                        over_quads(sp, body)
                        sp.wait_ge(s_st, 16 * NQ)
            own.close()

        BIG = 1e30

        def pad_top(pool, t, first, total, last_sem):
            for k in range(first, total):
                i = pool.memset(t[:, :, k:k + 1], BIG * (k - first + 1))
            i.then_inc(last_sem, 1)

        def route(tag, ctx, XT, combT, norm, gateT, ne, logits_to_scores, keep_store):
            s_logit = sem(tag + "_logits")
            s_xt = sem(tag + "_xt_stored")
            s_cb = sem(tag + "_comb_halves")
            s_ct = sem(tag + "_comb_turned")
            s_cc = sem(tag + "_comb_copied")
            cb = [sb(f"{tag}_cb{i}", [P, 4, P], F16, ctx=ctx) for i in range(2)]
            cbank = [bank[4 + i][:].bitcast(F16)[:, 0:512] for i in range(2)]
            s_cb0 = sem(tag + "_comb_padded")
            router_b = bank[2:4]

            def finish_comb(dve, chain, comb, q, u):
                wait(dve, s_ct, q - 1)
                chain(dve.tensor_copy(cb[u][:, :, 0:ne], comb))
                dve.tensor_tensor(cb[u][:, :, ne:2 * ne], comb, cb[u][:, :, 0:ne], ALU.subtract).then_inc(s_cb, 1)

            with nc.Block() as block:
                dve_scores, act_scores, pool_setup = logits_to_scores(router_b, s_logit, finish_comb)

                @block.gpsimd
                def _(pool):
                    pool_setup(pool)
                    for u in range(2):
                        i = pool.memset(cb[u][:], 0.0)
                    i.then_inc(s_cb0, 1)

                    def body(q, u):
                        pool.wait_ge(norm.s_xs, q + 1)
                        pool.tensor_copy(XT[:, bass.ds(q * 512, 512)], norm.xs[u][:]).then_inc(s_xt, 1)
                    over_quads(pool, body)

                @block.tensor
                def _(pe):
                    def router(q, u):
                        norm.turn(pe, q, u)
                        pe.wait_ge(norm.s_xs, q + 1)
                        wait(pe, s_cb, q - 1)
                        for j in range(4):
                            t = pe.matmul(router_b[u][:, j * ne:(j + 1) * ne], norm.xs[u][:, j * P:(j + 1) * P], gateT[:],
                                          start=True, stop=True)
                        t.then_inc(s_logit, 1)

                    def turn_comb(q, u):
                        pe.wait_ge(s_cb, q + 1)
                        wait(pe, s_cc, q - 1)
                        for j in range(4):
                            t = pe.transpose(cbank[u][:, j * P:(j + 1) * P], cb[u][:, j, :], identh[:])
                        t.then_inc(s_ct, 1)

                    router(0, 0)
                    router(1, 1)
                    turn_comb(0, 0)
                    turn_comb(1, 1)
                    with stepped(pe, 2, NQ, 2) as q:
                        router(q, 0)
                        router(q + 1, 1)
                        turn_comb(q, 0)
                        turn_comb(q + 1, 1)

                @block.scalar
                def _(act):
                    def body(q, u):
                        act.wait_ge(norm.s_turned, q + 1)
                        wait(act, s_xt, q - 1)
                        wait(act, s_logit, q - 1)
                        kw = {} if norm.gain is None else {"scale": norm.gain[:, 0:1]}
                        act.activation(norm.xs[u][:], norm.banks[u][:], ACT.Copy, **kw).then_inc(norm.s_xs, 1)
                        act_scores(act, q, u)
                    over_quads(act, body)

                @block.vector
                def _(dve):
                    def early(q, u):
                        norm.scale(dve, q, u)
                        dve_scores(dve, q, u)
                    def late(q, u):
                        dve.wait_ge(s_ct, q + 1)
                        dve.tensor_copy(combT[:, bass.ds(q * 512, 512)], cbank[u]).then_inc(s_cc, 1)
                    dve.wait_ge(s_cb0, 1)
                    early(0, 0)
                    early(1, 1)
                    late(0, 0)
                    late(1, 1)
                    with stepped(dve, 2, NQ, 2) as q:
                        early(q, 0)
                        early(q + 1, 1)
                        late(q, 0)
                        late(q + 1, 1)

        token = sb("token", [P, 1])

        class Chain:

            def __init__(self, eng, s, start):
                self.eng, self.s, self.n = eng, s, start

            def carried(self, i):
                self(i)
                self.eng.memset(token[:], 0.0)

            def __call__(self, i):
                i.then_inc(self.s, 1)
                self.n = self.n + 1
                self.eng.wait_ge(self.s, self.n)

        stats("b_stat")
        moe = ExitStack()
        XT = sb("b_XT", [P, NB * P], ctx=moe)
        YT = sb("b_YT", [P, NB * P], ctx=moe)
        combT = sb("b_combT", [P, NB * P], F16, ctx=moe)
        own = ExitStack()
        norm = Norm("b", own, bank[0:2])
        G0 = 8
        sig = [sb(f"b_sig{i}", [P, 4, E0], ctx=own) for i in range(2)]
        sc = sb("b_sc", [P, 4, E0], ctx=own)
        gs = sb("b_gs", [P, 4, G0 + 4], ctx=own)
        gr_ = sb("b_gr", [P, 4, G0 + 4], ctx=own)
        g8 = sb("b_g8", [P, 4, 8], ctx=own)
        ms = sb("b_ms", [P, 4, E0 + 2], ctx=own)
        mr = sb("b_mr", [P, 4, E0 + 2], ctx=own)
        m8 = sb("b_m8", [P, 4, 8], ctx=own)
        cw = sb("b_cw", [P, 4, E0], ctx=own)
        ssum = sb("b_ssum", [P, 4], ctx=own)
        s_sig = sem("b_sigmoid")
        s_bv = sem("b_route_steps")
        s_pad = sem("b_padded")
        B_STEPS = 13

        def b_scores(router_b, s_logit, finish_comb):
            def dve_scores(dve, q, u):
                chain = Chain(dve, s_bv, q * B_STEPS)
                if isinstance(q, int) and q == 0:
                    dve.wait_ge(s_pad, 2)
                dve.wait_ge(s_sig, q + 1)
                chain(dve.tensor_tensor(sc[:], sig[u][:], gb0[:].unsqueeze(1).broadcast_to([P, 4, E0]), ALU.add))
                chain.carried(dve.tensor_reduce(gs[:, :, 0:G0], sc[:].rearrange("p j (g e) -> p j g e", g=G0), AX.X, ALU.max))
                for j in range(4):
                    i = dve.max(g8[:, j, :], gs[:, j, :])
                chain.carried(i)
                for j in range(4):
                    i = dve.match_replace(gr_[:, j, :], g8[:, j, :], gs[:, j, :], -BIG)
                chain(i)
                chain(dve.tensor_tensor(gr_[:, :, 0:G0], gr_[:, :, 0:G0], gs[:, :, 0:G0], ALU.not_equal))
                chain.carried(dve.tensor_tensor(ms[:, :, 0:E0].rearrange("p j (g e) -> p j g e", g=G0),
                                        sc[:].rearrange("p j (g e) -> p j g e", g=G0),
                                        gr_[:, :, 0:G0].unsqueeze(3).broadcast_to([P, 4, G0, E0 // G0]), ALU.mult))
                for j in range(4):
                    i = dve.max(m8[:, j, :], ms[:, j, :])
                chain.carried(i)
                for j in range(4):
                    i = dve.match_replace(mr[:, j, :], m8[:, j, :], ms[:, j, :], -BIG)
                chain(i)
                chain(dve.tensor_tensor(cw[:], mr[:, :, 0:E0], ms[:, :, 0:E0], ALU.not_equal))
                chain(dve.tensor_tensor(cw[:], cw[:], ms[:, :, 0:E0], ALU.mult))
                chain(dve.tensor_reduce(ssum[:], cw[:], AX.X, ALU.add))
                chain(dve.tensor_scalar(ssum[:], ssum[:], 1e-8, 1.0 / COMB_UP, ALU.add, ALU.mult))
                dve.reciprocal(ssum[:], ssum[:]).then_inc(s_rc, 1)
                dve.wait_ge(s_rc, q + 1)
                dve.tensor_tensor(cw[:], cw[:], ssum[:].unsqueeze(2).broadcast_to([P, 4, E0]), ALU.mult).then_inc(s_cwd, 1)
                dve.wait_ge(s_cwd, q + 1)
                finish_comb(dve, chain, cw[:], q, u)

            def act_scores(act, q, u):
                act.wait_ge(s_logit, q + 1)
                wait(act, s_bv, (q - 2) * B_STEPS + 1)
                act.activation(sig[u][:].rearrange("p j e -> p (j e)"), router_b[u][:, 0:4 * E0],
                               ACT.Sigmoid).then_inc(s_sig, 1)

            def pool_setup(pool):
                pad_top(pool, gs, G0, G0 + 4, s_pad)
                pad_top(pool, ms, E0, E0 + 2, s_pad)
            return dve_scores, act_scores, pool_setup

        s_rc = sem("b_recip")
        s_cwd = sem("b_weights_ready")
        route("b_route", own, XT, combT, norm, small["a_gate"], E0, b_scores, None)
        own.close()

        own = ExitStack()
        s_silu_t = [sb(f"sh_silu{i}", [P, 512], ctx=own) for i in range(2)]
        s_hid = [sb(f"sh_hid{i}", [P, 512], ctx=own) for i in range(2)]
        s_sg = sem("sh_gate_up")
        s_ss = sem("sh_silu_done")
        s_shh = sem("sh_hidden")
        s_sd = sem("sh_down")
        s_sy = sem("sh_copied")
        with nc.Block() as block:
            @block.tensor
            def _(pe):
                def first(q, u):
                    wait(pe, s_shh, q - 1)
                    chunk = bass.ds(q * 512, 512)
                    pe.matmul(bank[u][:], small["sgT"][:], XT[:, chunk], start=True, stop=True)
                    pe.matmul(bank[2 + u][:], small["suT"][:], XT[:, chunk], start=True, stop=True).then_inc(s_sg, 1)

                def second(q, u):
                    pe.wait_ge(s_shh, q + 1)
                    wait(pe, s_sy, q - 1)
                    pe.matmul(bank[4 + u][:], small["sdT"][:], s_hid[u][:], start=True, stop=True).then_inc(s_sd, 1)

                first(0, 0)
                first(1, 1)
                second(0, 0)
                with stepped(pe, 2, NQ, 2) as q:
                    first(q, 0)
                    second(q - 1, 1)
                    first(q + 1, 1)
                    second(q, 0)
                second(NQ - 1, 1)

            @block.scalar
            def _(act):
                def body(q, u):
                    act.wait_ge(s_sg, q + 1)
                    wait(act, s_shh, q - 1)
                    act.activation(s_silu_t[u][:], bank[u][:], ACT.Silu).then_inc(s_ss, 1)
                over_quads(act, body)

            @block.vector
            def _(dve):
                def body(q, u):
                    dve.wait_ge(s_ss, q + 1)
                    wait(dve, s_sd, q - 1)
                    dve.tensor_tensor(s_hid[u][:], bank[2 + u][:], s_silu_t[u][:], ALU.mult).then_inc(s_shh, 1)
                    dve.wait_ge(s_sd, q + 1)
                    dve.tensor_copy(YT[:, bass.ds(q * 512, 512)], bank[4 + u][:]).then_inc(s_sy, 1)
                over_quads(dve, body)
        own.close()
        experts("b_moe", XT, combT, P, w["b_wgT"], w["b_wuT"], w["b_wdT"], consts["sel0"], E0 * I0 // P, False, YT)
        add_experts("b_add", YT, tg[:, 2:3], False)
        moe.close()
        renew_semaphores()
        if stop_after == 2:
            return dump()

        stats("c_stat", bias=bo1)
        att = ExitStack()
        XT = sb("c_XT", [P, NB * P], ctx=att)
        own = ExitStack()
        norm = Norm("cn", own, bank[0:2])
        with nc.Block() as block:
            @block.tensor
            def _(pe):
                over_quads(pe, lambda q, u: norm.turn(pe, q, u))

            @block.vector
            def _(dve):
                over_quads(dve, lambda q, u: norm.scale(dve, q, u))

            @block.scalar
            def _(act):
                def body(q, u):
                    act.wait_ge(norm.s_turned, q + 1)
                    act.activation(XT[:, bass.ds(q * 512, 512)], bank[u][:], ACT.Copy).then_inc(norm.s_xs, 1)
                over_quads(act, body)
        own.close()

        own = ExitStack()
        cs = [sb(f"c_cs{i}", [DC, NKV], ctx=own) for i in range(2)]
        xs = [sb(f"c_xs{i}", [P, P], ctx=own) for i in range(2)]
        ts = [sb(f"c_ts{i}", [P, HG * NKV], ctx=own) for i in range(2)]
        vs = [sb(f"c_vs{i}", [NKV, H, C_DH + 1], ctx=own) for i in range(2)]
        prob = [sb(f"c_prob{i}", [P, HG, NKV], ctx=own) for i in range(4)]
        probT = [sb(f"c_probT{i}", [NKV, HG * P], ctx=own) for i in range(2)]
        shift = sb("c_shift", [P, 4, HG], ctx=own)
        recip = sb("c_recip", [P, 2, HG], ctx=own)
        on = [sb(f"c_on{i}", [P, H * C_DH], ctx=own) for i in range(2)]
        oT = [sb(f"c_oT{i}", [P, 8, P], ctx=own) for i in range(2)]
        key_b, side_b, score_b, turn_b, out_b = bank[0], bank[1], bank[2:4], bank[4:6], bank[6:8]
        s_cs = [sem(f"c_ctx_loaded{i}") for i in range(2)]
        s_xs = sem("c_xs_placed")
        s_key = sem("c_keys")
        s_kcopy = sem("c_keys_copied")
        s_score = sem("c_scores")
        s_shift = sem("c_shift_ready")
        s_exp = sem("c_exp")
        s_turn = sem("c_probs_turned")
        s_copied = sem("c_probs_copied")
        s_v = sem("c_values")
        s_vcopy = sem("c_values_copied")
        s_pv = sem("c_pv")
        s_recip = sem("c_recip_ready")
        s_norm = sem("c_heads_normed")
        s_ot = sem("c_heads_turned")
        s_ocopy = sem("c_heads_copied")
        s_y = sem("c_projected")
        s_add = sem("c_added")
        s_vones = sem("c_ones_set")

        def at(bb, k):
            return bb + k // NG, k % NG, (k // NG) % 2

        def here(bb, k):
            return not absent(bb, k // 4, NB)

        with nc.Block() as block:
            @block.sync
            def _(sp):
                def body(b, u):
                    wait(sp, s_key, b * 4 - 4)
                    wait(sp, s_v, b * 2 - 2)
                    sp.dma_start(cs[u][:], ctxT[b] if isinstance(b, int) else
                                 ctxT[bass.ds(b, 1)].rearrange("b e t -> e (b t)")).then_inc(s_cs[u], 16)
                body(0, 0)
                body(1, 1)
                with stepped(sp, 2, NB, 2) as b:
                    body(b, 0)
                    body(b + 1, 1)

            @block.gpsimd
            def _(pool):
                for u in range(2):
                    i = pool.memset(vs[u][:, :, C_DH:C_DH + 1], 1.0)
                i.then_inc(s_vones, 1)

                def body(b, u):
                    wait(pool, s_score, b * 4 - 4)
                    pool.tensor_copy(xs[u][:], XT[:, bass.ds(b * P, P)]).then_inc(s_xs, 1)
                body(0, 0)
                body(1, 1)
                with stepped(pool, 2, NB, 2) as b:
                    body(b, 0)
                    body(b + 1, 1)

            @block.tensor
            def _(pe):
                def values(b, u, half):
                    wait(pe, s_ocopy, b * 2 - 4 + half)
                    wait(pe, s_vcopy, b * 2 + half)
                    pe.matmul(side_b[0:NKV, :], cs[u][:], small["c_wv"][:, half * 512:(half + 1) * 512],
                              start=True, stop=True).then_inc(s_v, 1)

                def slot(bb, j):
                    if here(bb, j):
                        b, g, u = at(bb, j)
                        n = bb * 4 + j
                        if g == 0:
                            pe.wait_ge(s_cs[u], (b - u) * 8 + 16)
                        wait(pe, s_kcopy, n)
                        for h in range(HG):
                            t = pe.matmul(key_b[:, h * NKV:(h + 1) * NKV], mT[:, g * HG + h, :], cs[u][:],
                                          start=True, stop=True)
                        t.then_inc(s_key, 1)
                        if g == 0:
                            values(b, u, 0)
                        if g == 2:
                            values(b, u, 1)
                    if here(bb, j - 1):
                        b, g, u = at(bb, j - 1)
                        n = bb * 4 + (j - 1)
                        if g == 0:
                            pe.wait_ge(s_xs, b + 1)
                        pe.wait_ge(s_kcopy, n + 1)
                        wait(pe, s_exp, n - 1)
                        pe.matmul(score_b[g % 2][:, 0:HG * NKV], xs[u][:], ts[g % 2][:], start=True,
                                  stop=True).then_inc(s_score, 1)
                    if here(bb, j - 4):
                        b, g, u = at(bb, j - 4)
                        n = bb * 4 + (j - 4)
                        pe.wait_ge(s_exp, n + 1)
                        wait(pe, s_copied, n - 1)
                        for h in range(HG):
                            t = pe.transpose(turn_b[g % 2][0:NKV, h * P:(h + 1) * P], prob[g][:, h, :], ident[:])
                        t.then_inc(s_turn, 1)
                    if here(bb, j - 5):
                        b, g, u = at(bb, j - 5)
                        n = bb * 4 + (j - 5)
                        pe.wait_ge(s_copied, n + 1)
                        pe.wait_ge(s_vcopy, b * 2 + 1 + g // 2)
                        wait(pe, s_norm, n - 1)
                        for h in range(HG):
                            t = pe.matmul(out_b[g % 2][:, h * (C_DH + 1):(h + 1) * (C_DH + 1)],
                                          probT[g % 2][:, h * P:(h + 1) * P], vs[u][:, g * HG + h, :],
                                          start=True, stop=True)
                        t.then_inc(s_pv, 1)
                    if (j - 8) % 2 == 1 and here(bb, j - 8):
                        b, g, u = at(bb, j - 8)
                        half = g // 2
                        pe.wait_ge(s_norm, b * 4 + 2 + 2 * half)
                        if half == 0:
                            wait(pe, s_add, b)
                        else:
                            pe.wait_ge(s_ocopy, b * 2 + 1)
                        if not (isinstance(b, int) and b >= NB - 2):
                            pe.wait_ge(s_vcopy, b * 2 + 5 + half)
                        for k in range(4):
                            t = pe.transpose(side_b[:, k * P:(k + 1) * P],
                                             on[u][:, (half * 4 + k) * P:(half * 4 + k + 1) * P], ident[:])
                        t.then_inc(s_ot, 1)
                    if (j - 9) % 4 == 3 and here(bb, j - 9):
                        b, g, u = at(bb, j - 9)
                        pe.wait_ge(s_ocopy, b * 2 + 2)
                        if not (isinstance(b, int) and b >= NB - 3):
                            pe.wait_ge(s_vcopy, b * 2 + 7)
                        for k in range(8):
                            t = pe.matmul(side_b[:, 0:D], oT[u][:, k, :], c_wo[:, k, :], start=(k == 0), stop=(k == 7))
                        t.then_inc(s_y, 1)
                pipeline_b(pe, slot, 9)

            @block.scalar
            def _(act):
                act.wait_ge(s_vones, 1)

                def copy_values(b, u, half):
                    act.wait_ge(s_v, b * 2 + 1 + half)
                    wait(act, s_pv, b * 4 - 4)
                    act.activation(vs[u][:, half * 8:half * 8 + 8, 0:C_DH],
                                   side_b[0:NKV, :].rearrange("p (h v) -> p h v", h=8), ACT.Copy).then_inc(s_vcopy, 1)

                def slot(bb, j):
                    if here(bb, j) and j % 4 in (0, 2):
                        b, g, u = at(bb, j)
                        copy_values(b, u, g // 2)
                    if here(bb, j - 1):
                        b, g, u = at(bb, j - 1)
                        n = bb * 4 + (j - 1)
                        act.wait_ge(s_shift, n + 1)
                        wait(act, s_turn, n - 3)
                        for h in range(HG):
                            i = act.activation(prob[g][:, h, :], score_b[g % 2][:, h * NKV:(h + 1) * NKV], ACT.Exp,
                                               bias=shift[:, g, h:h + 1])
                        i.then_inc(s_exp, 1)
                    if here(bb, j - 4):
                        b, g, u = at(bb, j - 4)
                        n = bb * 4 + (j - 4)
                        act.wait_ge(s_turn, n + 1)
                        wait(act, s_pv, n - 1)
                        act.activation(probT[g % 2][:], turn_b[g % 2][0:NKV, :], ACT.Copy).then_inc(s_copied, 1)
                pipeline_b(act, slot, 4)

            @block.vector
            def _(dve):
                def slot(bb, j):
                    if here(bb, j):
                        b, g, u = at(bb, j)
                        n = bb * 4 + j
                        dve.wait_ge(s_key, n + 1)
                        wait(dve, s_score, n - 1)
                        dve.tensor_copy(ts[g % 2][:], key_b[:, 0:HG * NKV]).then_inc(s_kcopy, 1)
                    if here(bb, j - 1):
                        b, g, u = at(bb, j - 1)
                        n = bb * 4 + (j - 1)
                        dve.wait_ge(s_score, n + 1)
                        wait(dve, s_exp, n - 3)
                        dve.tensor_reduce(shift[:, g, :], score_b[g % 2][:, 0:HG * NKV].rearrange("p (h k) -> p h k", h=HG),
                                          AX.X, ALU.max, negate=True).then_inc(s_shift, 1)
                    if here(bb, j - 6):
                        b, g, u = at(bb, j - 6)
                        n = bb * 4 + (j - 6)
                        dve.wait_ge(s_pv, n + 1)
                        o = out_b[g % 2][:, 0:HG * (C_DH + 1)].rearrange("p (h v) -> p h v", h=HG)
                        dve.reciprocal(recip[:, g % 2, :], o[:, :, C_DH]).then_inc(s_recip, 1)
                        dve.wait_ge(s_recip, n + 1)
                        wait(dve, s_ot, b * 2 - 3 + g // 2)
                        dve.tensor_tensor(on[u][:, g * 256:(g + 1) * 256].rearrange("p (h v) -> p h v", h=HG),
                                          o[:, :, 0:C_DH], recip[:, g % 2, :].unsqueeze(2).broadcast_to([P, HG, C_DH]),
                                          ALU.mult).then_inc(s_norm, 1)
                    if (j - 8) % 2 == 1 and here(bb, j - 8):
                        b, g, u = at(bb, j - 8)
                        half = g // 2
                        dve.wait_ge(s_ot, b * 2 + 1 + half)
                        wait(dve, s_y, b - 1)
                        dve.tensor_copy(oT[u][:, half * 4:half * 4 + 4, :].rearrange("p k t -> p (k t)"),
                                        side_b[:]).then_inc(s_ocopy, 1)
                    if (j - 9) % 4 == 3 and here(bb, j - 9):
                        b, g, u = at(bb, j - 9)
                        dve.wait_ge(s_y, b + 1)
                        d = X[:, bass.ds(b, 1), :].rearrange("p b d -> p (b d)")
                        dve.tensor_tensor(d, side_b[:, 0:D], d, ALU.add).then_inc(s_add, 1)
                pipeline_b(dve, slot, 9)
        own.close()
        att.close()
        if stop_after == 3:
            return dump()

        stats("d_stat", second=True)
        Z = XC
        att = ExitStack()
        QT = sb("d_QT", [P, NB * P], ctx=att)
        KT = sb("d_KT", [P, NB * P], ctx=att)
        V = sb("d_V", [P, NB * P], ctx=att)
        own = ExitStack()
        norm = Norm("d", own, bank[0:2], gain=small["g1"])
        wrot = sb("d_wrot", [LAT, 4, P], ctx=own)
        lat = [sb(f"d_lat{i}", [LAT, 512], ctx=own) for i in range(2)]
        part = [sb(f"d_part{i}", [P, 4, 512], ctx=own) for i in range(2)]
        s_wrot = sem("d_wrot_ready")
        s_v0 = sem("d_values_cleared")
        s_latp = sem("d_latent")
        s_lat = sem("d_latent_copied")
        s_rot = sem("d_rope_products")
        s_part = sem("d_rope_parts")
        s_sum = sem("d_rope_summed")
        s_v = sem("d_values")
        s_vcopy = sem("d_values_copied")
        with nc.Block() as block:
            @block.gpsimd
            def _(pool):
                pool.memset(V[:], 0.0).then_inc(s_v0, 1)
                pool.memset(wrot[:], 0.0).then_inc(s_wrot, 1)
                pool.wait_ge(s_wrot, 1)
                for k, name in enumerate(("d_q", "d_k")):
                    src = small[name][:].rearrange("p (h i two) -> p h i two", h=H, two=2)
                    dst = wrot[:, 2 * k, :].rearrange("p (h i two) -> p h i two", h=H, two=2)
                    turned = wrot[:, 2 * k + 1, :].rearrange("p (h i two) -> p h i two", h=H, two=2)
                    pool.tensor_copy(dst[:, :, 0:2, :], src)
                    pool.tensor_copy(turned[:, :, 0:2, 0], src[:, :, :, 1])
                    i = pool.tensor_copy(turned[:, :, 0:2, 1], src[:, :, :, 0])
                i.then_inc(s_wrot, 1)

                def body(q, u):
                    pool.wait_ge(s_part, q + 1)
                    pool.tensor_tensor(QT[:, bass.ds(q * 512, 512)], part[u][:, 0, :], part[u][:, 1, :], ALU.add)
                    pool.tensor_tensor(KT[:, bass.ds(q * 512, 512)], part[u][:, 2, :], part[u][:, 3, :],
                                       ALU.add).then_inc(s_sum, 1)
                over_quads(pool, body)

            @block.tensor
            def _(pe):
                pe.wait_ge(s_wrot, 2)

                def body(q, u):
                    norm.turn(pe, q, u)
                    pe.wait_ge(norm.s_xs, q + 1)
                    wait(pe, s_lat, q)
                    pe.matmul(bank[2][0:LAT, :], small["d_down"][:], norm.xs[u][:], start=True,
                              stop=True).then_inc(norm.s_used, 1)
                    pe.wait_ge(s_lat, q + 1)
                    wait(pe, s_vcopy, q)
                    for j in range(4):
                        t = pe.matmul(bank[3][:, j * LAT:(j + 1) * LAT], lat[u][:, j * P:(j + 1) * P],
                                      small["d_v"][:], start=True, stop=True)
                    t.then_inc(s_v, 1)
                    wait(pe, s_part, q)
                    for k in range(4):
                        t = pe.matmul(bank[4 + k][:], wrot[:, k, :], lat[u][:], start=True, stop=True)
                    t.then_inc(s_rot, 1)
                over_quads(pe, body)

            @block.scalar
            def _(act):
                act.wait_ge(s_v0, 1)

                def body(q, u):
                    norm.copy(act, q, u)
                    act.wait_ge(norm.s_used, q + 1)
                    wait(act, s_rot, q - 1)
                    act.activation(lat[u][:], bank[2][0:LAT, :], ACT.Copy).then_inc(s_lat, 1)
                    act.wait_ge(s_v, q + 1)
                    act.activation(V[:, bass.ds(q * 512, 512)].rearrange("p (b h v) -> p b h v", b=4, h=H)[:, :, :, 0:4],
                                   bank[3][:, 0:4 * LAT].rearrange("p (b h v) -> p b h v", b=4, h=H),
                                   ACT.Copy).then_inc(s_vcopy, 1)
                over_quads(act, body)

            @block.vector
            def _(dve):
                def body(q, u):
                    norm.scale(dve, q, u)
                    dve.wait_ge(s_rot, q + 1)
                    wait(dve, s_sum, q - 1)
                    for k in range(4):
                        t = dve.tensor_tensor(part[u][:, k, :].rearrange("p (b t) -> p b t", b=4),
                                              bank[4 + k][:].rearrange("p (b t) -> p b t", b=4),
                                              rope[:, k, :].unsqueeze(1).broadcast_to([P, 4, P]), ALU.mult)
                    t.then_inc(s_part, 1)
                over_quads(dve, body)
        own.close()
        own = ExitStack()
        attend("dt", own, QT, KT, V, P, d_up4, None, Z)
        own.close()
        att.close()

        stats("e_stat", src=XC)
        moe = ExitStack()
        XT = sb("e_XT", [P, NB * P], ctx=moe)
        YT = sb("e_YT", [P, NB * P], ctx=moe)
        combT = sb("e_combT", [P, NB * P], F16, ctx=moe)
        own = ExitStack()
        norm = Norm("e", own, bank[0:2], gain=small["g2"])
        ex = [sb(f"e_exp{i}", [P, 4, E1], ctx=own) for i in range(2)]
        lg = [sb(f"e_logit{i}", [P, 4, E1], ctx=own) for i in range(2)]
        mx = sb("e_max", [P, 4], ctx=own)
        pr = sb("e_probs", [P, 4, E1 + 6], ctx=own)
        pm = sb("e_matched", [P, 4, E1 + 6], ctx=own)
        p8 = sb("e_p8", [P, 4, 8], ctx=own)
        ew = sb("e_w", [P, 4, E1], ctx=own)
        es = sb("e_sum", [P, 4], ctx=own)
        s_lg = sem("e_shifted")
        s_ex = sem("e_exp_done")
        s_mx = sem("e_max_ready")
        s_ev = sem("e_route_steps")
        s_epad = sem("e_padded")
        E_STEPS = 11

        def e_scores(router_b, s_logit, finish_comb):
            def dve_scores(dve, q, u):
                if isinstance(q, int) and q == 0:
                    dve.wait_ge(s_epad, 1)
                dve.wait_ge(s_logit, q + 1)
                logits = router_b[u][:, 0:4 * E1].rearrange("p (j e) -> p j e", j=4)
                dve.tensor_reduce(mx[:], logits, AX.X, ALU.max).then_inc(s_mx, 1)
                dve.wait_ge(s_mx, q + 1)
                dve.tensor_tensor(lg[u][:], logits, mx[:].unsqueeze(2).broadcast_to([P, 4, E1]),
                                  ALU.subtract).then_inc(s_lg, 1)
                chain = Chain(dve, s_ev, q * E_STEPS)
                dve.wait_ge(s_ex, q + 1)
                chain(dve.tensor_reduce(es[:], ex[u][:], AX.X, ALU.add))
                chain(dve.reciprocal(es[:], es[:]))
                chain.carried(dve.tensor_tensor(pr[:, :, 0:E1], ex[u][:], es[:].unsqueeze(2).broadcast_to([P, 4, E1]), ALU.mult))
                for j in range(4):
                    i = dve.max(p8[:, j, :], pr[:, j, :])
                chain.carried(i)
                for j in range(4):
                    i = dve.match_replace(pm[:, j, :], p8[:, j, :], pr[:, j, :], -BIG)
                chain(i)
                chain(dve.tensor_tensor(ew[:], pm[:, :, 0:E1], pr[:, :, 0:E1], ALU.not_equal))
                chain(dve.tensor_tensor(ew[:], ew[:], pr[:, :, 0:E1], ALU.mult))
                chain(dve.tensor_reduce(es[:], ew[:], AX.X, ALU.add))
                chain(dve.tensor_scalar(es[:], es[:], 1.0 / COMB_UP, None, ALU.mult))
                chain(dve.reciprocal(es[:], es[:]))
                dve.tensor_tensor(ew[:], ew[:], es[:].unsqueeze(2).broadcast_to([P, 4, E1]), ALU.mult).then_inc(s_ewd, 1)
                dve.wait_ge(s_ewd, q + 1)
                finish_comb(dve, chain, ew[:], q, u)

            def act_scores(act, q, u):
                act.wait_ge(s_lg, q + 1)
                wait(act, s_ev, (q - 2) * E_STEPS + 3)
                act.activation(ex[u][:], lg[u][:], ACT.Exp).then_inc(s_ex, 1)

            def pool_setup(pool):
                pad_top(pool, pr, E1, E1 + 6, s_epad)
            return dve_scores, act_scores, pool_setup

        s_ewd = sem("e_weights_ready")
        route("e_route", own, XT, combT, norm, small["d_router"], E1, e_scores, None)
        own.close()
        s_res = sem("e_residual")
        with nc.Block() as block:
            @block.vector
            def _(dve):
                dve.scalar_tensor_tensor(X[:].rearrange("p b d -> p (b d)"), Z[:].rearrange("p b d -> p (b d)"),
                                         tg[:, 3:4], X[:].rearrange("p b d -> p (b d)"), ALU.mult,
                                         ALU.add).then_inc(s_res, 1)
        experts("e_moe", XT, combT, P, w["e_wg"], w["e_wu"], w["e_wd"], consts["sel1"], E1 * I1 // P, True, YT)
        add_experts("e_add", YT, tg[:, 3:4], True)
        moe.close()


def constants():
    head = (np.arange(P) % 32) // 8
    headsel = (head[:, None] == np.arange(HG)[None, :]).astype(np.float32)
    d = np.arange(P) % 8
    inv = (np.float32(1.0) / np.float32(10000.0) ** (np.arange(0, 4, 2, dtype=np.float32) / np.float32(4))).astype(np.float32)
    ang = (np.arange(P, dtype=np.float32)[None, :] * inv[np.minimum(d // 2, 1)][:, None]).astype(np.float32)
    used = (d < 4).astype(np.float32)[:, None]
    cos = (np.cos(ang) * used).astype(np.float32)
    sin = (np.sin(ang) * used * np.where(d % 2 == 0, -1.0, 1.0)[:, None]).astype(np.float32)
    rope = np.stack([cos * 0.5, sin * 0.5, cos, sin], axis=1).astype(np.float32)
    causal = np.where(np.arange(P)[None, :] > np.arange(P)[:, None], -1e30, 0.0).astype(np.float32)

    def sel(ne, width):
        e = np.arange(ne * width) // width
        one = (np.arange(ne)[:, None] == e[None, :]).astype(np.float32) / COMB_UP
        both = np.zeros((P, ne * width), np.float16)
        both[0:ne] = one
        both[ne:2 * ne] = one
        return both
    return {"ident": np.eye(P, dtype=np.float32), "headsel": headsel, "rope": rope, "causal": causal,
            "sel0": sel(E0, I0), "sel1": sel(E1, I1)}


def layout(i):
    t = np.ascontiguousarray
    n = {k: np.asarray(v) for k, v in i.items()}
    w = {
        "a_wq": n["L0_xattn_Wq"], "a_wk": n["L0_xattn_Wk"], "a_wv": n["L0_xattn_Wv"], "a_wo": n["L0_xattn_Wo"],
        "a_bq": n["L0_xattn_bq"].reshape(D, 1), "a_bk": n["L0_xattn_bk"].reshape(D, 1),
        "a_bv": n["L0_xattn_bv"], "a_bvc": n["L0_xattn_bv"].reshape(D, 1), "a_bo": n["L0_xattn_bo"],
        "a_gate": t(n["L0_ffn_gate_w"].T), "a_gbias": n["L0_ffn_gate_bias"],
        "b_wgT": t(n["L0_ffn_eg_w"].reshape(E0 * I0, D).T), "b_wuT": t(n["L0_ffn_eu_w"].reshape(E0 * I0, D).T),
        "b_wdT": t(n["L0_ffn_ed_w"].transpose(0, 2, 1)).reshape(E0 * I0, D),
        "sgT": t(n["L0_ffn_sg_w"].T), "suT": t(n["L0_ffn_su_w"].T), "sdT": t(n["L0_ffn_sd_w"].T),
        "c_wv": n["L1_xattn_Wv"], "c_wo": n["L1_xattn_Wo"], "c_bo": n["L1_xattn_bo"],
        "c_wkT": t(n["L1_xattn_Wk"].T), "c_wqT": t(n["L1_xattn_Wq"].T),
        "g1": n["L1_ffn_g1"].reshape(D, 1), "g2": n["L1_ffn_g2"].reshape(D, 1),
        "d_down": n["L1_ffn_w_down"], "d_q": n["L1_ffn_wq"], "d_k": n["L1_ffn_wk"], "d_v": n["L1_ffn_wv"],
        "d_up": n["L1_ffn_w_up"], "d_router": n["L1_ffn_router_w"],
        "e_wg": t(n["L1_ffn_w1"].transpose(1, 0, 2)).reshape(D, E1 * I1),
        "e_wu": t(n["L1_ffn_w3"].transpose(1, 0, 2)).reshape(D, E1 * I1),
        "e_wd": n["L1_ffn_w2"].reshape(E1 * I1, D),
    }
    main = {"x": n["x"], "ctxT": t(n["ctx_768"].transpose(0, 2, 1)), "gx": n["g_xattn"], "gf": n["g_ffn"]}
    return main, w


def kernel(stop_after=99, **inputs):
    import concourse.bacc as bacc
    from concourse.bass_utils import run_bass_kernel_spmd

    nc = bacc.Bacc("TRN2", target_bir_lowering=False, num_devices=1)
    main, w = layout(inputs)
    arrays = {}

    def declare(group):
        aps = {}
        for name, a in group.items():
            arrays["in_" + name] = a
            aps[name] = nc.dram_tensor("in_" + name, a.shape, mybir.dt.from_np(a.dtype), kind="ExternalInput").ap()
        return aps

    m, weights, consts = declare(main), declare(w), declare(constants())
    out = nc.dram_tensor("out_0", (NB, P, D), F32, kind="ExternalOutput").ap()
    build(nc, m["x"], m["ctxT"], m["gx"], m["gf"], weights, consts, out, stop_after)
    r = run_bass_kernel_spmd(nc, [arrays], core_ids=[0])
    return r.results[0]["out_0"]
```

```python
from contextlib import ExitStack, contextmanager

import numpy as np
import concourse.bass as bass
from concourse import mybir

F32 = mybir.dt.float32
F32R = mybir.dt.float32r
F16 = mybir.dt.float16
BF16 = mybir.dt.bfloat16
I32 = mybir.dt.int32
ALU = mybir.AluOpType
ACT = mybir.ActivationFunctionType
AX = mybir.AxisListType

P = 128
NB = 32
NQ = NB // 4
D = 128
DC = 96
NKV = 120
H = 16
HG = 4
NG = H // HG
EPS = 1e-5
CLAMP = 1e4
A_SCALE = 8 ** -0.5
C_DH = 64
E0, I0, TG0, K0 = 64, 64, 4, 6
E1, I1, K1 = 8, 256, 2
HIGH_BITS = -4096
COMB_UP = 4096.0
LAT = 64


def wait(eng, sem, count):
    if isinstance(count, int) and count <= 0:
        return
    eng.wait_ge(sem, count)


@contextmanager
def stepped(eng, start, end, step):
    with eng.Fori(start // step, end // step) as k:
        yield k * step


def absent(base, k, items):
    return isinstance(base, int) and not 0 <= base + k < items


def keep_high(eng, high, x):
    return eng.tensor_copy(high.bitcast(F32R), x)


def keep_low(eng, low, x, high):
    return eng.tensor_tensor(low.bitcast(F32R), x, high, ALU.subtract)


def split_product(pe, out, w, x, start=True, stop=True):
    pe.matmul(out, w[0].bitcast(F32R), x[0].bitcast(F32R), start=start, stop=False)
    pe.matmul(out, w[1].bitcast(F32R), x[0].bitcast(F32R), start=False, stop=False)
    return pe.matmul(out, w[0].bitcast(F32R), x[1].bitcast(F32R), start=False, stop=stop)


def build(nc, x, ctxT, gx, gf, w, consts, out, stop_after=99):
    top = ExitStack()
    with top:
        def sb(name, shape, dt=F32, ctx=top):
            return ctx.enter_context(nc.sbuf_tensor(name, shape, dt))

        in_use = []

        def sem(name):
            in_use.append(nc.alloc_semaphore(name))
            return in_use[-1]

        def renew_semaphores():
            nc.clear_and_free_semaphores(list(in_use))
            in_use.clear()
            nc.all_engine_barrier()

        bank = [top.enter_context(nc.psum_tensor(f"bank{i}", [P, 512], F32)) for i in range(8)]

        X = sb("X", [P, NB, D])
        XC = sb("XC", [P, NB, D])
        stat = sb("stat", [P, 4, NB])
        ident = sb("ident", [P, P])
        ones = sb("ones", [P, P])
        gates = sb("gates", [P, 4])
        tg = sb("tg", [P, 4])
        headsel = sb("headsel", [P, HG])

        s_load = sem("loaded")
        s_tg = sem("gates_tanh")
        s_zrow = sem("zero_rows_set")
        small = {}

        def load_small(name, shape):
            small[name] = sb("w_" + name, shape)
            return small[name]

        for name, shape in (("a_wq", [D, D]), ("a_wk", [DC, D]), ("a_wv", [DC, D]),
                            ("a_bq", [D, 1]), ("a_bk", [D, 1]), ("a_bvc", [D, 1]), ("a_wo", [D, D]), ("a_gate", [D, E0]),
                            ("sgT", [D, D]), ("suT", [D, D]), ("sdT", [D, D]),
                            ("c_wv", [DC, H * C_DH]), ("g1", [D, 1]), ("g2", [D, 1]),
                            ("d_down", [D, LAT]), ("d_q", [LAT, LAT]), ("d_k", [LAT, LAT]),
                            ("d_v", [LAT, LAT]), ("d_router", [D, E1])):
            load_small(name, shape)
        c_wo = sb("c_wo", [P, 8, D])
        a_wo8 = sb("a_wo8", [64, 2, D])
        d_up8 = sb("d_up8", [64, 2, D])
        mT = sb("mT", [DC, H, D])
        bo0 = sb("bo0", [P, D])
        bo1 = sb("bo1", [P, D])
        bv0 = sb("bv0", [P, D])
        gb0 = sb("gb0", [P, E0])
        rope = sb("rope", [P, 4, P])
        causal = sb("causal", [P, P])
        causal16 = sb("causal16", [P, HG, P], BF16)
        ident16 = sb("ident16", [P, P], BF16)
        identh = sb("identh", [P, P], F16)

        prep = ExitStack()
        wkT = sb("wkT", [C_DH, H, DC], ctx=prep)
        wqT = sb("wqT", [C_DH, H, D], ctx=prep)
        s_mt = sem("m_ready")
        s_mtfree = sem("m_copied")
        s_const = sem("constants_ready")
        n_loads = []
        with nc.Block() as block:
            @block.sync
            def _(sp):
                def load(dst, src):
                    sp.dma_start(dst, src).then_inc(s_load, 16)
                    n_loads.append(1)
                for q in range(4):
                    load(X[:, 8 * q:8 * q + 8, :], x[8 * q:8 * q + 8].rearrange("b t d -> t b d"))
                for name, t in small.items():
                    load(t[:], w[name])
                sp.wait_ge(s_zrow, 1)
                load(a_wo8[:], w["a_wo"].rearrange("(p r) n -> r p n", p=2))
                for i in range(8):
                    load(d_up8[8 * i:8 * i + 4], w["d_up"].rearrange("(p i d) n -> i d p n", p=2, i=8)[i])
                load(c_wo[:], w["c_wo"].rearrange("(j p) d -> p j d", p=P))
                load(wkT[:], w["c_wkT"].rearrange("(h p) e -> p h e", p=C_DH))
                load(wqT[:], w["c_wqT"].rearrange("(h p) d -> p h d", p=C_DH))
                for t, name in ((bo0, "a_bo"), (bo1, "c_bo"), (bv0, "a_bv"), (gb0, "a_gbias")):
                    load(t[:], w[name].partition_broadcast(P))
                load(gates[:, 0:2], gx.partition_broadcast(P))
                load(gates[:, 2:4], gf.partition_broadcast(P))
                load(ident[:], consts["ident"])
                load(headsel[:], consts["headsel"])
                load(rope[:], consts["rope"])
                load(causal[:], consts["causal"])
                sp.wait_ge(s_load, 16 * len(n_loads))

            all_loads = 16 * len(n_loads)

            @block.gpsimd
            def _(pool):
                pool.memset(d_up8[:], 0.0).then_inc(s_zrow, 1)
                pool.memset(ones[:], 1.0)
                pool.wait_ge(s_load, all_loads)
                pool.tensor_copy(ident16[:], ident[:])
                pool.tensor_copy(identh[:], ident[:])
                pool.tensor_copy(causal16[:], causal[:].unsqueeze(1).broadcast_to([P, HG, P]))

            @block.scalar
            def _(act):
                act.wait_ge(s_load, all_loads)
                act.activation(tg[:], gates[:], ACT.Tanh).then_inc(s_tg, 1)
                for g in range(NG):
                    act.wait_ge(s_mt, g + 1)
                    act.activation(mT[:, HG * g:HG * g + HG, :], bank[g][0:DC, :].rearrange("p (h d) -> p h d", h=HG),
                                   ACT.Copy, scale=C_DH ** -0.5)

            @block.tensor
            def _(pe):
                pe.wait_ge(s_load, all_loads)
                for g in range(NG):
                    for j in range(HG):
                        h = HG * g + j
                        last = pe.matmul(bank[g][0:DC, j * D:(j + 1) * D], wkT[:, h, :], wqT[:, h, :],
                                         start=True, stop=True)
                    last.then_inc(s_mt, 1)

            @block.vector
            def _(dve):
                dve.wait_ge(s_tg, 1)
                dve.tensor_scalar(small["a_wo"][:], small["a_wo"][:], tg[:, 0:1], None, ALU.mult)
                dve.tensor_scalar(a_wo8[:], a_wo8[:], tg[0:64, 0:1], None, ALU.mult)
                dve.tensor_scalar(c_wo[:], c_wo[:], tg[:, 1:2], None, ALU.mult)
                dve.tensor_scalar(bo0[:], bo0[:], tg[:, 0:1], None, ALU.mult)
                dve.tensor_scalar(bo1[:], bo1[:], tg[:, 1:2], None, ALU.mult)
                dve.tensor_scalar(small["a_bq"][:], small["a_bq"][:], A_SCALE, None, ALU.mult)
        prep.close()

        def stats(tag, bias=None, second=False, src=X):
            s_v = sem(tag + "_dve")
            s_sq = sem(tag + "_squared")
            s_rs = sem(tag + "_rstd")
            s_exp = sem(tag + "_exponent_set")
            own = ExitStack()
            sq = sb(tag + "_sq", [P, NB, D], ctx=own)
            expo = sb(tag + "_expo", [P, NB], ctx=own)
            rms_only = src is XC
            with nc.Block() as block:
                @block.vector
                def _(dve):
                    done = 0
                    if not rms_only:
                        dve.tensor_reduce(stat[:, 0, :], X[:], AX.X, ALU.add).then_inc(s_v, 1)
                        dve.wait_ge(s_v, 1)
                        dve.tensor_scalar(stat[:, 1, :], stat[:, 0, :], 1.0 / D, None, ALU.mult).then_inc(s_v, 1)
                        dve.wait_ge(s_v, 2)
                        dve.tensor_tensor(XC[:], X[:], stat[:, 1, :].unsqueeze(2).broadcast_to([P, NB, D]),
                                          ALU.subtract).then_inc(s_v, 1)
                        done = 3
                        if bias is not None:
                            dve.tensor_tensor(X[:], X[:], bias[:].unsqueeze(1).broadcast_to([P, NB, D]), ALU.add)
                    dve.wait_ge(s_sq, 1)
                    dve.tensor_reduce(stat[:, 2, :], sq[:], AX.X, ALU.add).then_inc(s_v, 1)
                    dve.wait_ge(s_v, done + 1)
                    dve.tensor_scalar(stat[:, 2, :], stat[:, 2, :], 1.0 / D, EPS, ALU.mult, ALU.add).then_inc(s_v, 1)
                    if second:
                        dve.wait_ge(s_rs, 1)
                        dve.tensor_tensor(XC[:], XC[:], stat[:, 3, :].unsqueeze(2).broadcast_to([P, NB, D]),
                                          ALU.mult).then_inc(s_v, 1)
                        dve.wait_ge(s_sq, 2)
                        dve.tensor_reduce(stat[:, 2, :], sq[:], AX.X, ALU.add).then_inc(s_v, 1)
                        dve.wait_ge(s_v, done + 4)
                        dve.tensor_scalar(stat[:, 2, :], stat[:, 2, :], 1.0 / D, EPS, ALU.mult,
                                          ALU.add).then_inc(s_v, 1)

                @block.scalar
                def _(act):
                    if not rms_only:
                        act.wait_ge(s_v, 3)
                    act.activation(sq[:], XC[:], ACT.Square).then_inc(s_sq, 1)
                    if second:
                        act.wait_ge(s_v, 6)
                        act.activation(sq[:], XC[:], ACT.Square).then_inc(s_sq, 1)

                @block.gpsimd
                def _(pool):
                    pool.memset(expo[:], -0.5).then_inc(s_exp, 1)
                    pool.wait_ge(s_exp, 1)
                    n = 2 if rms_only else 5
                    pool.wait_ge(s_v, n)
                    pool.tensor_tensor(stat[:, 3, :], stat[:, 2, :], expo[:], ALU.pow).then_inc(s_rs, 1)
                    if second:
                        pool.wait_ge(s_v, n + 3)
                        pool.tensor_tensor(stat[:, 3, :], stat[:, 2, :], expo[:], ALU.pow).then_inc(s_rs, 1)
            own.close()

        class Norm:

            def __init__(self, tag, ctx, banks, gain=None, lookahead=1):
                self.xn = [sb(f"{tag}_xn{i}", [P, 4, D], ctx=ctx) for i in range(2)]
                self.xs = [sb(f"{tag}_xs{i}", [P, 512], ctx=ctx) for i in range(2)]
                self.banks, self.gain = banks, gain
                self.s_scaled = sem(tag + "_scaled")
                self.s_turned = sem(tag + "_turned")
                self.s_xs = sem(tag + "_xs")
                self.s_used = sem(tag + "_xs_used")

            def scale(self, dve, q, u):
                wait(dve, self.s_turned, q - 1)
                dve.tensor_tensor(self.xn[u][:], XC[:, bass.ds(q * 4, 4), :],
                                  stat[:, 3, bass.ds(q * 4, 4)].unsqueeze(2).broadcast_to([P, 4, D]),
                                  ALU.mult).then_inc(self.s_scaled, 1)

            def turn(self, pe, q, u):
                pe.wait_ge(self.s_scaled, q + 1)
                wait(pe, self.s_xs, q - 1)
                for j in range(4):
                    t = pe.transpose(self.banks[u][:, j * P:(j + 1) * P], self.xn[u][:, j, :], ident[:])
                t.then_inc(self.s_turned, 1)

            def copy(self, act, q, u):
                act.wait_ge(self.s_turned, q + 1)
                wait(act, self.s_used, q - 1)
                if self.gain is None:
                    i = act.activation(self.xs[u][:], self.banks[u][:], ACT.Copy)
                else:
                    i = act.activation(self.xs[u][:], self.banks[u][:], ACT.Copy, scale=self.gain[:, 0:1])
                i.then_inc(self.s_xs, 1)

        def over_quads(eng, body):
            body(0, 0)
            body(1, 1)
            with stepped(eng, 2, NQ, 2) as q:
                body(q, 0)
                body(q + 1, 1)

        def attend(tag, ctx, QT, KT, V, nk, wo, raw, dst):
            clamp = raw is not None
            qs = [[sb(f"{tag}_qs_{part}{i}", [P, P], ctx=ctx) for part in ("high", "low")] for i in range(2)]
            ks = [[sb(f"{tag}_ks_{part}{i}", [P, nk], ctx=ctx) for part in ("high", "low")] for i in range(2)]
            kd = [[sb(f"{tag}_kd_{part}{i}", [P, HG, nk], ctx=ctx) for part in ("high", "low")] for i in range(2)]
            vh = [sb(f"{tag}_vh{i}", [nk, H, P], ctx=ctx) for i in range(2)]
            prob = [sb(f"{tag}_prob{i}", [P, HG, nk], ctx=ctx) for i in range(8)]
            probT = [sb(f"{tag}_probT{i}", [nk, HG * P], ctx=ctx) for i in range(2)]
            negmax = sb(tag + "_negmax", [P, 4, HG], ctx=ctx)
            shift = sb(tag + "_shift", [P, 4, HG], ctx=ctx)
            floor = sb(tag + "_floor", [P, 4, HG], ctx=ctx)
            low = sb(tag + "_low", [P, 1], ctx=ctx)
            recip = [sb(f"{tag}_recip{i}", [64, 2 * P], ctx=ctx) for i in range(2)]
            headT = [sb(f"{tag}_headT{i}", [64, 2 * P], ctx=ctx) for i in range(2)]
            score_b, turn_b, out_b = bank[0:4], bank[4:6], bank[6:8]
            s_high = sem(tag + "_qk_high")
            s_low_k = sem(tag + "_k_low")
            s_prep = sem(tag + "_keys_spread")
            s_vprep = sem(tag + "_values_spread")
            s_clear = sem(tag + "_values_cleared")
            s_score = sem(tag + "_scores")
            s_max = sem(tag + "_rowmax")
            s_shift = sem(tag + "_shift_ready")
            s_exp = sem(tag + "_exp")
            s_floor = sem(tag + "_floor_done")
            s_turn = sem(tag + "_probs_turned")
            s_copied = sem(tag + "_probs_copied")
            s_pv = sem(tag + "_pv")
            s_recip = sem(tag + "_recip_ready")
            s_head = sem(tag + "_heads_ready")
            s_y = sem(tag + "_projected")
            s_out = sem(tag + "_out_done")
            s_low = sem(tag + "_low_ready")
            s_probs = s_floor if clamp else s_exp

            def at(bb, k):
                return bb + k // NG, k % NG, (k // NG) % 2

            def own_columns(t, first):
                flat = t[:].rearrange("p h c -> p (h c)")
                head0 = flat[:, first:first + 8].unsqueeze(1).unsqueeze(1)
                return bass.AP(head0.tensor, head0.offset,
                               [list(flat.ap[0]), [8 * P, 2], [P + 8, 8], [1, 8]])

            with nc.Block() as block:
                @block.gpsimd
                def _(pool):
                    def spread(b, u):
                        pool.wait_ge(s_high, b + 1)
                        wait(pool, s_score, b * 4 - 4)
                        keep_low(pool, ks[u][1][:], KT[:, bass.ds(b * nk, nk)], ks[u][0][:]).then_inc(s_low_k, 1)
                        keep_low(pool, qs[u][1][:], QT[:, bass.ds(b * P, P)], qs[u][0][:])
                        pool.wait_ge(s_low_k, b + 1)
                        for part in range(2):
                            t = pool.tensor_tensor(kd[u][part][:].bitcast(F32R), ks[u][part][:].unsqueeze(1).broadcast_to([P, HG, nk]),
                                                   headsel[:].unsqueeze(2).broadcast_to([P, HG, nk]), ALU.mult)
                        t.then_inc(s_prep, 1)

                    def spread_values(b, u):
                        wait(pool, s_pv, b * 4 - 4)
                        pool.tensor_copy(own_columns(vh[u], 0),
                                         V[:, bass.ds(b * P, P)].rearrange("p (p2 i d) -> p p2 i d", p2=2, i=8))\
                            .then_inc(s_vprep, 1)

                    pool.memset(low[:], -CLAMP).then_inc(s_low, 1)
                    for u in range(2):
                        i = pool.memset(vh[u][:], 0.0)
                    i.then_inc(s_clear, 1)
                    pool.wait_ge(s_clear, 1)
                    for u in range(2):
                        i = pool.memset(own_columns(vh[u], 64), 1.0)
                    i.then_inc(s_clear, 1)
                    spread(0, 0)

                    def slot(bb, j):
                        b, g, u = at(bb, j)
                        if g == 1 and not absent(bb, j // 4 + 1, NB):
                            spread(b + 1, 1 - u)
                        if g == 2:
                            spread_values(b, u)

                    pipeline_b(pool, slot, 0)

                @block.tensor
                def _(pe):
                    pe.wait_ge(s_clear, 2)

                    def slot(bb, j):
                        if not absent(bb, j // 4, NB):
                            b, g, u = at(bb, j)
                            n = bb * 4 + j
                            if g == 0:
                                pe.wait_ge(s_prep, b + 1)
                            wait(pe, s_exp, n - 3)
                            if not clamp:
                                pe.matmul(score_b[g][:], ident16[:], causal16[:].rearrange("p h k -> p (h k)"),
                                          start=True, stop=False)
                            rows = slice(32 * g, 32 * g + 32)
                            split_product(pe, score_b[g][:, 0:HG * nk], [t[rows, :] for t in qs[u]],
                                          [t[rows].rearrange("p h k -> p (h k)") for t in kd[u]],
                                          start=clamp).then_inc(s_score, 1)
                        if not absent(bb, (j - 4) // 4, NB):
                            b, g, u = at(bb, j - 4)
                            n = bb * 4 + (j - 4)
                            pe.wait_ge(s_probs, n + 1)
                            wait(pe, s_copied, n - 1)
                            for h in range(HG):
                                t = pe.transpose(turn_b[g % 2][0:nk, h * P:(h + 1) * P], prob[(j - 4) % 8][:, h, :], ident[:])
                            t.then_inc(s_turn, 1)
                        if not absent(bb, (j - 6) // 4, NB):
                            b, g, u = at(bb, j - 6)
                            n = bb * 4 + (j - 6)
                            pe.wait_ge(s_copied, n + 1)
                            if g == 0:
                                pe.wait_ge(s_vprep, b + 1)
                                wait(pe, s_out, b - 1)
                            for h in range(HG):
                                k = (g % 2) * HG + h
                                t = pe.matmul(out_b[u][:, (g // 2) * P:(g // 2 + 1) * P], vh[u][:, g * HG + h, :],
                                              probT[g % 2][:, h * P:(h + 1) * P], start=(k == 0), stop=(k == 7))
                            t.then_inc(s_pv, 1)
                        if (j - 8) % 4 == 3 and not absent(bb, (j - 8) // 4, NB):
                            b, g, u = at(bb, j - 8)
                            pe.wait_ge(s_head, b + 1)
                            for half in range(2):
                                t = pe.matmul(out_b[u][:, 2 * P:2 * P + D], headT[u][:, half * P:(half + 1) * P],
                                              wo[:, half, :], start=(half == 0), stop=(half == 1))
                            t.then_inc(s_y, 1)

                    pipeline_b(pe, slot, 8)

                def copy_probs(eng, bb, k):
                    n = bb * 4 + k
                    g = k % NG
                    eng.wait_ge(s_turn, n + 1)
                    wait(eng, s_pv, n - 1)
                    if not clamp:
                        wait(eng, s_copied, n)
                    if clamp or g % 2:
                        i = nc.scalar.activation(probT[g % 2][:], turn_b[g % 2][0:nk, :], ACT.Copy)
                    else:
                        i = nc.vector.tensor_copy(probT[0][:], turn_b[0][0:nk, :])
                    i.then_inc(s_copied, 1)

                @block.scalar
                def _(act):
                    act.wait_ge(s_low, 1)

                    def slot(bb, j):
                        if not absent(bb, (j - 5) // 4, NB) and (clamp or (j - 5) % 2 == 1):
                            copy_probs(act, bb, j - 5)
                        if not absent(bb, j // 4, NB):
                            b, g, u = at(bb, j)
                            n = bb * 4 + j
                            act.wait_ge(s_shift, n + 1)
                            wait(act, s_turn, n - 7)
                            if clamp:
                                wait(act, s_floor, n - 3)
                                act.activation(floor[:, g, :], shift[:, g, :], ACT.Exp, bias=low[:, 0:1])
                            for h in range(HG):
                                acc = raw[:, bass.ds(n * 4 + h, 1)] if clamp else None
                                i = act.activation(prob[j % 8][:, h, :], score_b[g][:, h * nk:(h + 1) * nk], ACT.Exp,
                                                   bias=shift[:, g, h:h + 1], accum_out=acc)
                            i.then_inc(s_exp, 1)

                    pipeline_b(act, slot, 5)

                @block.vector
                def _(dve):
                    def high_parts(b, u):
                        wait(dve, s_score, b * 4 - 4)
                        keep_high(dve, ks[u][0][:], KT[:, bass.ds(b * nk, nk)])
                        keep_high(dve, qs[u][0][:], QT[:, bass.ds(b * P, P)]).then_inc(s_high, 1)
                    high_parts(0, 0)

                    def slot(bb, j):
                        if not clamp and not absent(bb, (j - 5) // 4, NB) and (j - 5) % 2 == 0:
                            copy_probs(dve, bb, j - 5)
                        if j % 4 == 0 and not absent(bb, j // 4 + 1, NB):
                            high_parts(bb + j // 4 + 1, 1 - (j // 4) % 2)
                        if not absent(bb, j // 4, NB):
                            b, g, u = at(bb, j)
                            n = bb * 4 + j
                            dve.wait_ge(s_score, n + 1)
                            wait(dve, s_exp, n - 3)
                            to = negmax if clamp else shift
                            i = dve.tensor_reduce(to[:, g, :], score_b[g][:, 0:HG * nk].rearrange("p (h k) -> p h k", h=HG),
                                                  AX.X, ALU.max, negate=True)
                            i.then_inc(s_max if clamp else s_shift, 1)
                            if clamp:
                                dve.wait_ge(s_max, n + 1)
                                dve.tensor_scalar(shift[:, g, :], negmax[:, g, :], CLAMP, -CLAMP, ALU.min,
                                                  ALU.max).then_inc(s_shift, 1)
                        if clamp and not absent(bb, (j - 2) // 4, NB):
                            g = (j - 2) % NG
                            dve.wait_ge(s_exp, bb * 4 + j - 1)
                            dve.scalar_tensor_tensor(prob[(j - 2) % 8][:], prob[(j - 2) % 8][:], 1.0,
                                                     floor[:, g, :].unsqueeze(2).broadcast_to([P, HG, nk]),
                                                     ALU.min, ALU.max).then_inc(s_floor, 1)
                        if (j - 7) % 4 == 3 and not absent(bb, (j - 7) // 4, NB):
                            b, g, u = at(bb, j - 7)
                            dve.wait_ge(s_pv, b * 4 + 4)
                            dve.reciprocal(recip[u][:], out_b[u][64:128, 0:2 * P]).then_inc(s_recip, 1)
                            dve.wait_ge(s_recip, b + 1)
                            wait(dve, s_y, b - 1)
                            dve.tensor_tensor(headT[u][:], out_b[u][0:64, 0:2 * P], recip[u][:], ALU.mult).then_inc(s_head, 1)
                        if (j - 9) % 4 == 3 and not absent(bb, (j - 9) // 4, NB):
                            b, g, u = at(bb, j - 9)
                            dve.wait_ge(s_y, b + 1)
                            d = dst[:, bass.ds(b, 1), :].rearrange("p b d -> p (b d)")
                            if clamp:
                                i = dve.tensor_copy(d, out_b[u][:, 2 * P:2 * P + D])
                            else:
                                i = dve.tensor_tensor(d, out_b[u][:, 2 * P:2 * P + D], d, ALU.add)
                            i.then_inc(s_out, 1)

                    pipeline_b(dve, slot, 9)

        def pipeline_b(eng, slot, tail):
            for bb in (0, 2):
                for j in range(8):
                    slot(bb, j)
            with stepped(eng, 4, NB - 2, 2) as bb:
                for j in range(8):
                    slot(bb, j)
            for j in range(8 + tail):
                slot(NB - 2, j)

        def dump():
            s_dump = sem("dumped")
            with nc.Block() as block:
                @block.sync
                def _(sp):
                    sp.dma_start(out.rearrange("b t d -> t b d"), X[:]).then_inc(s_dump, 16)
                    sp.wait_ge(s_dump, 16)

        stats("a_stat", bias=bo0)
        att = ExitStack()
        Y = sb("a_Y", [P, NB, D], ctx=att)
        cmean = sb("a_cmean", [DC, NB], ctx=att)
        raw = sb("a_raw", [P, NB * H], ctx=att)
        QT = sb("a_QT", [P, NB * P], ctx=att)
        KT = sb("a_KT", [P, NB * NKV], ctx=att)
        V = sb("a_V", [NKV, NB * D], ctx=att)
        own = ExitStack()
        norm = Norm("a", own, bank[0:2])
        cs = [sb(f"a_cs{i}", [DC, 4, NKV], ctx=own) for i in range(2)]
        s_cs = [sem(f"a_ctx_loaded{i}") for i in range(2)]
        s_kq = sem("a_qk_products")
        s_v = sem("a_v_product")
        s_qcopy = sem("a_q_copied")
        s_kcopy = sem("a_k_copied")
        s_vcopy = sem("a_v_copied")
        s_mean = sem("a_context_summed")
        with nc.Block() as block:
            @block.sync
            def _(sp):
                def body(q, u):
                    wait(sp, s_v, q - 1)
                    wait(sp, s_mean, q - 1)
                    sp.dma_start(cs[u][:], ctxT[bass.ds(q * 4, 4)].rearrange("b e t -> e b t")).then_inc(s_cs[u], 16)
                over_quads(sp, body)

            @block.tensor
            def _(pe):
                def body(q, u):
                    norm.turn(pe, q, u)
                    pe.wait_ge(s_cs[u], (q // 2) * 16 + 16 if isinstance(q, int) else (q - u) * 8 + 16)
                    wait(pe, s_kcopy, q)
                    pe.matmul(bank[3][:, 0:4 * NKV], small["a_wk"][:], cs[u][:].rearrange("p b t -> p (b t)"),
                              start=True, stop=True)
                    pe.wait_ge(norm.s_xs, q + 1)
                    wait(pe, s_qcopy, q)
                    pe.matmul(bank[2][:], small["a_wq"][:], norm.xs[u][:], start=True, stop=True).then_inc(norm.s_used, 1)
                    wait(pe, s_vcopy, q)
                    for j in range(4):
                        t = pe.matmul(bank[4][0:NKV, j * D:(j + 1) * D], cs[u][:, j, :], small["a_wv"][:],
                                      start=True, stop=True)
                    t.then_inc(s_v, 1)
                over_quads(pe, body)

            @block.scalar
            def _(act):
                def body(q, u):
                    norm.copy(act, q, u)
                    act.wait_ge(norm.s_used, q + 1)
                    act.activation(QT[:, bass.ds(q * 512, 512)], bank[2][:], ACT.Identity, scale=A_SCALE,
                                   bias=small["a_bq"][:, 0:1]).then_inc(s_qcopy, 1)
                over_quads(act, body)

            @block.vector
            def _(dve):
                def body(q, u):
                    norm.scale(dve, q, u)
                    dve.wait_ge(s_v, q + 1)
                    dve.tensor_scalar(KT[:, bass.ds(q * 4 * NKV, 4 * NKV)], bank[3][:, 0:4 * NKV],
                                      small["a_bk"][:, 0:1], None, ALU.add).then_inc(s_kcopy, 1)
                    dve.tensor_tensor(V[:, bass.ds(q * 512, 512)].rearrange("p (b c) -> p b c", b=4),
                                      bank[4][0:NKV, :].rearrange("p (b c) -> p b c", b=4),
                                      bv0[0:NKV, :].unsqueeze(1).broadcast_to([NKV, 4, D]), ALU.add)\
                        .then_inc(s_vcopy, 1)
                    dve.tensor_reduce(cmean[:, bass.ds(q * 4, 4)], cs[u][:], AX.X, ALU.add).then_inc(s_mean, 1)
                over_quads(dve, body)
        own.close()

        own = ExitStack()
        attend("a_att", own, QT, KT, V, NKV, a_wo8, raw, Y)
        own.close()

        own = ExitStack()
        odd = sb("odd", [P, NB * H], ctx=own)
        anyodd = sb("anyodd", [P, 1], ctx=own)
        oddmask = sb("oddmask", [P, 1], I32, ctx=own)
        vmeanT = sb("vmeanT", [D, NB], ctx=own)
        s_odd = sem("odd_found")
        s_oddsum = sem("odd_summed")
        s_vm = sem("mean_values")
        s_vmc = sem("mean_values_copied")
        s_flat = sem("uniform_projected")
        s_pick = sem("uniform_picked")
        with nc.Block() as block:
            @block.vector
            def _(dve):
                dve.tensor_tensor(odd[:], raw[:], raw[:], ALU.not_equal).then_inc(s_odd, 1)
                dve.wait_ge(s_odd, 1)
                dve.tensor_reduce(anyodd[:], odd[:], AX.X, ALU.max).then_inc(s_odd, 1)
                dve.wait_ge(s_oddsum, 1)
                dve.tensor_scalar(oddmask[:], bank[0][:, 0:1], 0.0, None, ALU.is_gt).then_inc(s_odd, 1)
                dve.wait_ge(s_odd, 3)
                for q in range(NQ):
                    dve.wait_ge(s_flat, q + 1)
                    dve.copy_predicated(Y[:, 4 * q:4 * q + 4, :].rearrange("p b d -> p (b d)"),
                                        oddmask[:].broadcast_to([P, 512]), bank[2 + q % 2][:]).then_inc(s_pick, 1)
                dve.wait_ge(s_pick, NQ)
                dve.tensor_tensor(X[:], X[:], Y[:], ALU.add)

            @block.scalar
            def _(act):
                act.wait_ge(s_vm, 1)
                act.activation(vmeanT[:], bank[1][:, 0:NB], ACT.Identity, scale=1.0 / NKV,
                               bias=small["a_bvc"][:, 0:1]).then_inc(s_vmc, 1)

            @block.tensor
            def _(pe):
                pe.matmul(bank[1][:, 0:NB], small["a_wv"][:], cmean[:], start=True, stop=True).then_inc(s_vm, 1)
                pe.wait_ge(s_odd, 2)
                pe.matmul(bank[0][:, 0:1], ones[:], anyodd[:], start=True, stop=True).then_inc(s_oddsum, 1)
                pe.wait_ge(s_vmc, 1)
                for q in range(NQ):
                    wait(pe, s_pick, q - 1)
                    for j in range(4):
                        t = pe.matmul(bank[2 + q % 2][:, j * D:(j + 1) * D],
                                      vmeanT[:, 4 * q + j:4 * q + j + 1].broadcast_to([D, P]), small["a_wo"][:],
                                      start=True, stop=True)
                    t.then_inc(s_flat, 1)
        own.close()
        att.close()
        if stop_after == 1:
            return dump()

        def experts(tag, XT, combT, nrows, wg, wu, wd, sel, units, start_from_zero, YT):
            own = ExitStack()
            groups = units // 4
            whole = [sb(f"{tag}_w_{k}", [P, 512], ctx=own) for k in ("gate", "up", "down")]
            wgs = [[sb(f"{tag}_wg_{part}{i}", [P, 512], ctx=own) for part in ("high", "low")] for i in range(2)]
            wus = [[sb(f"{tag}_wu_{part}{i}", [P, 512], ctx=own) for part in ("high", "low")] for i in range(2)]
            wds = [[sb(f"{tag}_wd_{part}{i}", [P, 512], ctx=own) for part in ("high", "low")] for i in range(2)]
            sels = [sb(f"{tag}_sel{i}", [nrows, 512], F16, ctx=own) for i in range(2)]
            act_s = [sb(f"{tag}_silu{i}", [P, 512], ctx=own) for i in range(2)]
            gu = [sb(f"{tag}_gu{i}", [P, 512], ctx=own) for i in range(2)]
            hid = [sb(f"{tag}_hid{i}", [P, 512], ctx=own) for i in range(2)]
            hid_high = [sb(f"{tag}_hid_high{i}", [P, 512], ctx=own) for i in range(4)]
            hid_low = [sb(f"{tag}_hid_low{i}", [P, 512], ctx=own) for i in range(4)]
            gate_b, up_b, comb_b, down_b = bank[0:2], bank[2:4], bank[4:6], bank[6:8]
            s_w = [sem(f"{tag}_weights{i}") for i in range(2)]
            s_zero = sem(tag + "_sum_cleared")
            s_g = sem(tag + "_gate")
            s_u = sem(tag + "_up")
            s_c = sem(tag + "_comb")
            s_silu = sem(tag + "_silu_done")
            s_gu = sem(tag + "_gated")
            s_wh = sem(tag + "_weights_high")
            s_wl = sem(tag + "_weights_split")
            s_p = sem(tag + "_hidden_product")
            s_hh = sem(tag + "_hidden_high")
            s_h = sem(tag + "_hidden_split")
            s_d = sem(tag + "_down")
            s_y = sem(tag + "_summed")

            def walk(eng, pair):
                def group(gr, wb, first=False, last=False):
                    pair(gr, 0, wb, None if first else 1 - wb)
                    pair(gr, 2, wb, wb, prepare=not last)
                    with stepped(eng, 4, NQ, 2) as c:
                        pair(gr, c, wb, wb)
                group(0, 0, first=True)
                group(1, 1)
                if groups > 4:
                    with stepped(eng, 2, groups - 2, 2) as gr:
                        group(gr, 0)
                        group(gr + 1, 1)
                group(groups - 2, 0)
                group(groups - 1, 1, last=True)

            def unit(gr, c, k):
                return gr * 32 + c * 4 + k

            with nc.Block() as block:
                @block.sync
                def _(sp):
                    def group(gr, wb):
                        wait(sp, s_d, gr * 32 - 32)
                        if isinstance(gr, int) and gr == 1:
                            sp.wait_ge(s_wl, 3)
                        for dst, src in ((whole[0], wg), (whole[1], wu)):
                            sp.dma_start(dst[:], src[:, bass.ds(gr * 512, 512)]).then_inc(s_w[wb], 16)
                        sp.dma_start(whole[2][:].rearrange("p (u d) -> p u d", u=4),
                                     wd[bass.ds(gr * 512, 512)].rearrange("(u p) d -> p u d", p=P))\
                            .then_inc(s_w[wb], 16)
                        sp.dma_start(sels[wb][:], sel[:, bass.ds(gr * 512, 512)]).then_inc(s_w[wb], 16)
                    group(0, 0)
                    group(1, 1)
                    with stepped(sp, 2, groups, 2) as gr:
                        group(gr, 0)
                        group(gr + 1, 1)

                def high_weights(dve, gr, wb, k):
                    if k == 0:
                        dve.wait_ge(s_w[wb], (gr - wb) * 32 + 64)
                        wait(dve, s_d, gr * 32 - 32)
                    keep_high(dve, (wgs, wus, wds)[k][wb][0][:], whole[k][:]).then_inc(s_wh, 1)

                def low_weights(pool, gr, wb, k):
                    t = (wgs, wus, wds)[k][wb]
                    pool.wait_ge(s_wh, gr * 3 + k + 1)
                    keep_low(pool, t[1][:], whole[k][:], t[0][:]).then_inc(s_wl, 1)

                @block.gpsimd
                def _(pool):
                    for k in range(3):
                        low_weights(pool, 0, 0, k)
                    if start_from_zero:
                        pool.memset(YT[:], 0.0).then_inc(s_zero, 1)

                    def pair(gr, c, wb, before, prepare=False):
                        for j in range(8):
                            n = unit(gr, c, j)
                            pool.wait_ge(s_hh, n + 1)
                            wait(pool, s_d, n - 3)
                            keep_low(pool, hid_low[j % 4][:], hid[j % 2][:], hid_high[j % 4][:]).then_inc(s_h, 1)
                            if prepare and j % 2 == 1 and j < 6:
                                low_weights(pool, gr + 1, 1 - wb, j // 2)
                    walk(pool, pair)

                @block.tensor
                def _(pe):
                    def down(gr, c, k, wb):
                        n = unit(gr, c, k)
                        u = k % 4
                        pe.wait_ge(s_h, n + 1)
                        if u == 0:
                            i = gr * 8 + c + k // 4
                            wait(pe, s_y, i - 1)
                        split_product(pe, down_b[(k // 4) % 2][:], [t[:, u * D:(u + 1) * D] for t in wds[wb]],
                                      (hid_high[k % 4][:], hid_low[k % 4][:]), start=(u == 0),
                                      stop=(u == 3)).then_inc(s_d, 1)

                    def pair(gr, c, wb, before, prepare=False):
                        for j in range(8):
                            n = unit(gr, c, j)
                            u = j % 4
                            x_parts = [t[:, bass.ds((c + j // 4) * 512, 512)] for t in XT]
                            if j == 0 and isinstance(c, int) and c == 0:
                                pe.wait_ge(s_w[wb], (gr - wb) * 32 + 64)
                                pe.wait_ge(s_wl, gr * 3 + 3)
                            wait(pe, s_silu, n - 1)
                            split_product(pe, gate_b[j % 2][:], [t[:, u * P:(u + 1) * P] for t in wgs[wb]],
                                          x_parts).then_inc(s_g, 1)
                            wait(pe, s_gu, n - 1)
                            split_product(pe, up_b[j % 2][:], [t[:, u * P:(u + 1) * P] for t in wus[wb]],
                                          x_parts).then_inc(s_u, 1)
                            wait(pe, s_p, n - 1)
                            pe.matmul(comb_b[j % 2][:], sels[wb][:, u * P:(u + 1) * P],
                                      combT[:, bass.ds((c + j // 4) * 512, 512)],
                                      start=True, stop=True).then_inc(s_c, 1)
                            if j >= 2:
                                down(gr, c, j - 2, wb)
                            elif before is not None:
                                down(gr, c, j - 2, before)
                    walk(pe, pair)
                    for k in (6, 7):
                        down(groups - 1, NQ - 2, k, 1)

                @block.scalar
                def _(act):
                    def pair(gr, c, wb, before, prepare=False):
                        for j in range(8):
                            n = unit(gr, c, j)
                            act.wait_ge(s_g, n + 1)
                            wait(act, s_gu, n - 1)
                            act.activation(act_s[j % 2][:], gate_b[j % 2][:], ACT.Silu).then_inc(s_silu, 1)
                    walk(act, pair)

                @block.vector
                def _(dve):
                    def add(gr, c, k):
                        n = unit(gr, c, k)
                        cc = c + k // 4
                        if isinstance(cc, int) and cc < 0:
                            cc += NQ
                        dve.wait_ge(s_d, n + 1)
                        y = YT[:, bass.ds(cc * 512, 512)]
                        dve.tensor_tensor(y, down_b[(k // 4) % 2][:], y, ALU.add).then_inc(s_y, 1)

                    def pair(gr, c, wb, before, prepare=False):
                        for j in range(8):
                            n = unit(gr, c, j)
                            dve.wait_ge(s_u, n + 1)
                            dve.wait_ge(s_silu, n + 1)
                            wait(dve, s_p, n - 1)
                            dve.tensor_tensor(gu[j % 2][:], up_b[j % 2][:], act_s[j % 2][:], ALU.mult).then_inc(s_gu, 1)
                            dve.wait_ge(s_gu, n + 1)
                            dve.wait_ge(s_c, n + 1)
                            wait(dve, s_h, n - 1)
                            dve.tensor_tensor(hid[j % 2][:], comb_b[j % 2][:], gu[j % 2][:], ALU.mult).then_inc(s_p, 1)
                            dve.wait_ge(s_p, n + 1)
                            wait(dve, s_d, n - 3)
                            keep_high(dve, hid_high[j % 4][:], hid[j % 2][:]).then_inc(s_hh, 1)
                            if prepare and j % 2 == 1 and j < 6:
                                high_weights(dve, gr + 1, 1 - wb, j // 2)
                            if (j - 3) % 4 == 3 and (j >= 3 or before is not None):
                                add(gr, c, j - 3)
                    for k in range(3):
                        high_weights(dve, 0, 0, k)
                    if start_from_zero:
                        dve.wait_ge(s_zero, 1)
                    walk(dve, pair)
                    add(groups - 1, NQ - 2, 7)
            own.close()

        def add_experts(tag, YT, gate, store):
            own = ExitStack()
            ys = [sb(f"{tag}_ys{i}", [P, 512], ctx=own) for i in range(2)]
            s_ys = sem(tag + "_placed")
            s_t = sem(tag + "_turned")
            s_x = sem(tag + "_added")
            s_st = sem(tag + "_stored")
            with nc.Block() as block:
                @block.scalar
                def _(act):
                    def body(q, u):
                        wait(act, s_t, q - 1)
                        act.activation(ys[u][:], YT[:, bass.ds(q * 512, 512)], ACT.Copy,
                                       scale=gate).then_inc(s_ys, 1)
                    over_quads(act, body)

                @block.tensor
                def _(pe):
                    def body(q, u):
                        pe.wait_ge(s_ys, q + 1)
                        wait(pe, s_x, q - 1)
                        for j in range(4):
                            t = pe.transpose(bank[u][:, j * P:(j + 1) * P], ys[u][:, j * P:(j + 1) * P], ident[:])
                        t.then_inc(s_t, 1)
                    over_quads(pe, body)

                @block.vector
                def _(dve):
                    def body(q, u):
                        dve.wait_ge(s_t, q + 1)
                        d = X[:, bass.ds(q * 4, 4), :].rearrange("p b d -> p (b d)")
                        dve.tensor_tensor(d, bank[u][:], d, ALU.add).then_inc(s_x, 1)
                    over_quads(dve, body)

                if store:
                    @block.sync
                    def _(sp):
                        def body(q, u):
                            sp.wait_ge(s_x, q + 1)
                            sp.dma_start(out[bass.ds(q * 4, 4)].rearrange("b t d -> t b d"),
                                         X[:, bass.ds(q * 4, 4), :]).then_inc(s_st, 16)
                        over_quads(sp, body)
                        sp.wait_ge(s_st, 16 * NQ)
            own.close()

        BIG = 1e30

        def pad_top(pool, t, first, total, last_sem):
            for k in range(first, total):
                i = pool.memset(t[:, :, k:k + 1], BIG * (k - first + 1))
            i.then_inc(last_sem, 1)

        def route(tag, ctx, XT, combT, norm, gateT, ne, logits_to_scores, keep_store):
            s_logit = sem(tag + "_logits")
            s_xhigh = sem(tag + "_xt_high")
            s_xt = sem(tag + "_xt_stored")
            s_cb = sem(tag + "_comb_halves")
            s_ct = sem(tag + "_comb_turned")
            s_cc = sem(tag + "_comb_copied")
            cb = [sb(f"{tag}_cb{i}", [P, 4, P], F16, ctx=ctx) for i in range(2)]
            cbank = [bank[4 + i][:].bitcast(F16)[:, 0:512] for i in range(2)]
            s_cb0 = sem(tag + "_comb_padded")
            router_b = bank[2:4]

            def finish_comb(dve, chain, comb, q, u):
                wait(dve, s_ct, q - 1)
                chain(dve.tensor_copy(cb[u][:, :, 0:ne], comb))
                dve.tensor_tensor(cb[u][:, :, ne:2 * ne], comb, cb[u][:, :, 0:ne], ALU.subtract).then_inc(s_cb, 1)

            with nc.Block() as block:
                dve_scores, act_scores, pool_setup = logits_to_scores(router_b, s_logit, finish_comb)

                @block.gpsimd
                def _(pool):
                    pool_setup(pool)
                    for u in range(2):
                        i = pool.memset(cb[u][:], 0.0)
                    i.then_inc(s_cb0, 1)

                    def body(q, u):
                        pool.wait_ge(s_xhigh, q + 1)
                        chunk = bass.ds(q * 512, 512)
                        keep_low(pool, XT[1][:, chunk], norm.xs[u][:], XT[0][:, chunk]).then_inc(s_xt, 1)
                    over_quads(pool, body)

                @block.tensor
                def _(pe):
                    def router(q, u):
                        norm.turn(pe, q, u)
                        pe.wait_ge(norm.s_xs, q + 1)
                        wait(pe, s_cb, q - 1)
                        for j in range(4):
                            t = pe.matmul(router_b[u][:, j * ne:(j + 1) * ne], norm.xs[u][:, j * P:(j + 1) * P], gateT[:],
                                          start=True, stop=True)
                        t.then_inc(s_logit, 1)

                    def turn_comb(q, u):
                        pe.wait_ge(s_cb, q + 1)
                        wait(pe, s_cc, q - 1)
                        for j in range(4):
                            t = pe.transpose(cbank[u][:, j * P:(j + 1) * P], cb[u][:, j, :], identh[:])
                        t.then_inc(s_ct, 1)

                    router(0, 0)
                    router(1, 1)
                    turn_comb(0, 0)
                    turn_comb(1, 1)
                    with stepped(pe, 2, NQ, 2) as q:
                        router(q, 0)
                        router(q + 1, 1)
                        turn_comb(q, 0)
                        turn_comb(q + 1, 1)

                @block.scalar
                def _(act):
                    def body(q, u):
                        act.wait_ge(norm.s_turned, q + 1)
                        wait(act, s_xt, q - 1)
                        wait(act, s_logit, q - 1)
                        kw = {} if norm.gain is None else {"scale": norm.gain[:, 0:1]}
                        act.activation(norm.xs[u][:], norm.banks[u][:], ACT.Copy, **kw).then_inc(norm.s_xs, 1)
                        act_scores(act, q, u)
                    over_quads(act, body)

                @block.vector
                def _(dve):
                    def early(q, u):
                        norm.scale(dve, q, u)
                        dve.wait_ge(norm.s_xs, q + 1)
                        keep_high(dve, XT[0][:, bass.ds(q * 512, 512)], norm.xs[u][:]).then_inc(s_xhigh, 1)
                        dve_scores(dve, q, u)
                    def late(q, u):
                        dve.wait_ge(s_ct, q + 1)
                        dve.tensor_copy(combT[:, bass.ds(q * 512, 512)], cbank[u]).then_inc(s_cc, 1)
                    dve.wait_ge(s_cb0, 1)
                    early(0, 0)
                    early(1, 1)
                    late(0, 0)
                    late(1, 1)
                    with stepped(dve, 2, NQ, 2) as q:
                        early(q, 0)
                        early(q + 1, 1)
                        late(q, 0)
                        late(q + 1, 1)

        token = sb("token", [P, 1])

        class Chain:

            def __init__(self, eng, s, start):
                self.eng, self.s, self.n = eng, s, start

            def carried(self, i):
                self(i)
                self.eng.memset(token[:], 0.0)

            def __call__(self, i):
                i.then_inc(self.s, 1)
                self.n = self.n + 1
                self.eng.wait_ge(self.s, self.n)

        stats("b_stat")
        moe = ExitStack()
        XT = [sb(f"b_XT_{part}", [P, NB * P], ctx=moe) for part in ("high", "low")]
        YT = sb("b_YT", [P, NB * P], ctx=moe)
        combT = sb("b_combT", [P, NB * P], F16, ctx=moe)
        own = ExitStack()
        norm = Norm("b", own, bank[0:2])
        G0 = 8
        sig = [sb(f"b_sig{i}", [P, 4, E0], ctx=own) for i in range(2)]
        sc = sb("b_sc", [P, 4, E0], ctx=own)
        gs = sb("b_gs", [P, 4, G0 + 4], ctx=own)
        gr_ = sb("b_gr", [P, 4, G0 + 4], ctx=own)
        g8 = sb("b_g8", [P, 4, 8], ctx=own)
        ms = sb("b_ms", [P, 4, E0 + 2], ctx=own)
        mr = sb("b_mr", [P, 4, E0 + 2], ctx=own)
        m8 = sb("b_m8", [P, 4, 8], ctx=own)
        cw = sb("b_cw", [P, 4, E0], ctx=own)
        ssum = sb("b_ssum", [P, 4], ctx=own)
        s_sig = sem("b_sigmoid")
        s_bv = sem("b_route_steps")
        s_pad = sem("b_padded")
        B_STEPS = 13

        def b_scores(router_b, s_logit, finish_comb):
            def dve_scores(dve, q, u):
                chain = Chain(dve, s_bv, q * B_STEPS)
                if isinstance(q, int) and q == 0:
                    dve.wait_ge(s_pad, 2)
                dve.wait_ge(s_sig, q + 1)
                chain(dve.tensor_tensor(sc[:], sig[u][:], gb0[:].unsqueeze(1).broadcast_to([P, 4, E0]), ALU.add))
                chain.carried(dve.tensor_reduce(gs[:, :, 0:G0], sc[:].rearrange("p j (g e) -> p j g e", g=G0), AX.X, ALU.max))
                for j in range(4):
                    i = dve.max(g8[:, j, :], gs[:, j, :])
                chain.carried(i)
                for j in range(4):
                    i = dve.match_replace(gr_[:, j, :], g8[:, j, :], gs[:, j, :], -BIG)
                chain(i)
                chain(dve.tensor_tensor(gr_[:, :, 0:G0], gr_[:, :, 0:G0], gs[:, :, 0:G0], ALU.not_equal))
                chain.carried(dve.tensor_tensor(ms[:, :, 0:E0].rearrange("p j (g e) -> p j g e", g=G0),
                                        sc[:].rearrange("p j (g e) -> p j g e", g=G0),
                                        gr_[:, :, 0:G0].unsqueeze(3).broadcast_to([P, 4, G0, E0 // G0]), ALU.mult))
                for j in range(4):
                    i = dve.max(m8[:, j, :], ms[:, j, :])
                chain.carried(i)
                for j in range(4):
                    i = dve.match_replace(mr[:, j, :], m8[:, j, :], ms[:, j, :], -BIG)
                chain(i)
                chain(dve.tensor_tensor(cw[:], mr[:, :, 0:E0], ms[:, :, 0:E0], ALU.not_equal))
                chain(dve.tensor_tensor(cw[:], cw[:], ms[:, :, 0:E0], ALU.mult))
                chain(dve.tensor_reduce(ssum[:], cw[:], AX.X, ALU.add))
                chain(dve.tensor_scalar(ssum[:], ssum[:], 1e-8, 1.0 / COMB_UP, ALU.add, ALU.mult))
                dve.reciprocal(ssum[:], ssum[:]).then_inc(s_rc, 1)
                dve.wait_ge(s_rc, q + 1)
                dve.tensor_tensor(cw[:], cw[:], ssum[:].unsqueeze(2).broadcast_to([P, 4, E0]), ALU.mult).then_inc(s_cwd, 1)
                dve.wait_ge(s_cwd, q + 1)
                finish_comb(dve, chain, cw[:], q, u)

            def act_scores(act, q, u):
                act.wait_ge(s_logit, q + 1)
                wait(act, s_bv, (q - 2) * B_STEPS + 1)
                act.activation(sig[u][:].rearrange("p j e -> p (j e)"), router_b[u][:, 0:4 * E0],
                               ACT.Sigmoid).then_inc(s_sig, 1)

            def pool_setup(pool):
                pad_top(pool, gs, G0, G0 + 4, s_pad)
                pad_top(pool, ms, E0, E0 + 2, s_pad)
            return dve_scores, act_scores, pool_setup

        s_rc = sem("b_recip")
        s_cwd = sem("b_weights_ready")
        route("b_route", own, XT, combT, norm, small["a_gate"], E0, b_scores, None)
        own.close()

        own = ExitStack()
        s_silu_t = [sb(f"sh_silu{i}", [P, 512], ctx=own) for i in range(2)]
        s_hid = [sb(f"sh_hid{i}", [P, 512], ctx=own) for i in range(2)]
        s_hid_high = [sb(f"sh_hid_high{i}", [P, 512], ctx=own) for i in range(2)]
        s_hid_low = [sb(f"sh_hid_low{i}", [P, 512], ctx=own) for i in range(2)]
        sh_w = [[sb(f"sh_w{i}_{part}", [P, P], ctx=own) for part in ("high", "low")] for i in range(3)]
        s_swh = sem("sh_weights_high")
        s_swl = sem("sh_weights_split")
        s_shp = sem("sh_product")
        s_shhh = sem("sh_hidden_high")
        s_sg = sem("sh_gate_up")
        s_ss = sem("sh_silu_done")
        s_shh = sem("sh_hidden")
        s_sd = sem("sh_down")
        s_sy = sem("sh_copied")
        with nc.Block() as block:
            @block.gpsimd
            def _(pool):
                for k, name in enumerate(("sgT", "suT", "sdT")):
                    pool.wait_ge(s_swh, k + 1)
                    keep_low(pool, sh_w[k][1][:], small[name][:], sh_w[k][0][:]).then_inc(s_swl, 1)

                def body(q, u):
                    pool.wait_ge(s_shhh, q + 1)
                    wait(pool, s_sd, q - 1)
                    keep_low(pool, s_hid_low[u][:], s_hid[u][:], s_hid_high[u][:]).then_inc(s_shh, 1)
                over_quads(pool, body)

            @block.tensor
            def _(pe):
                def first(q, u):
                    wait(pe, s_shp, q - 1)
                    x_parts = [t[:, bass.ds(q * 512, 512)] for t in XT]
                    split_product(pe, bank[u][:], [t[:] for t in sh_w[0]], x_parts)
                    split_product(pe, bank[2 + u][:], [t[:] for t in sh_w[1]], x_parts).then_inc(s_sg, 1)

                def second(q, u):
                    pe.wait_ge(s_shh, q + 1)
                    wait(pe, s_sy, q - 1)
                    split_product(pe, bank[4 + u][:], [t[:] for t in sh_w[2]],
                                  (s_hid_high[u][:], s_hid_low[u][:])).then_inc(s_sd, 1)

                pe.wait_ge(s_swl, 3)
                first(0, 0)
                first(1, 1)
                second(0, 0)
                with stepped(pe, 2, NQ, 2) as q:
                    first(q, 0)
                    second(q - 1, 1)
                    first(q + 1, 1)
                    second(q, 0)
                second(NQ - 1, 1)

            @block.scalar
            def _(act):
                def body(q, u):
                    act.wait_ge(s_sg, q + 1)
                    wait(act, s_shp, q - 1)
                    act.activation(s_silu_t[u][:], bank[u][:], ACT.Silu).then_inc(s_ss, 1)
                over_quads(act, body)

            @block.vector
            def _(dve):
                for k, name in enumerate(("sgT", "suT", "sdT")):
                    keep_high(dve, sh_w[k][0][:], small[name][:]).then_inc(s_swh, 1)

                def body(q, u):
                    dve.wait_ge(s_ss, q + 1)
                    wait(dve, s_shh, q - 1)
                    dve.tensor_tensor(s_hid[u][:], bank[2 + u][:], s_silu_t[u][:], ALU.mult).then_inc(s_shp, 1)
                    dve.wait_ge(s_shp, q + 1)
                    wait(dve, s_sd, q - 1)
                    keep_high(dve, s_hid_high[u][:], s_hid[u][:]).then_inc(s_shhh, 1)
                    dve.wait_ge(s_sd, q + 1)
                    dve.tensor_copy(YT[:, bass.ds(q * 512, 512)], bank[4 + u][:]).then_inc(s_sy, 1)
                over_quads(dve, body)
        own.close()
        experts("b_moe", XT, combT, P, w["b_wgT"], w["b_wuT"], w["b_wdT"], consts["sel0"], E0 * I0 // P, False, YT)
        add_experts("b_add", YT, tg[:, 2:3], False)
        moe.close()
        renew_semaphores()
        if stop_after == 2:
            return dump()

        stats("c_stat", bias=bo1)
        att = ExitStack()
        XT = [sb(f"c_XT_{part}", [P, NB * P], ctx=att) for part in ("high", "low")]
        own = ExitStack()
        norm = Norm("cn", own, bank[0:2])
        s_xhigh = sem("cn_high")
        with nc.Block() as block:
            @block.tensor
            def _(pe):
                over_quads(pe, lambda q, u: norm.turn(pe, q, u))

            @block.scalar
            def _(act):
                def body(q, u):
                    act.wait_ge(norm.s_turned, q + 1)
                    act.activation(XT[0][:, bass.ds(q * 512, 512)].bitcast(F32R), bank[u][:], ACT.Copy).then_inc(s_xhigh, 1)
                over_quads(act, body)

            @block.vector
            def _(dve):
                def low(q, u):
                    dve.wait_ge(s_xhigh, q + 1)
                    chunk = bass.ds(q * 512, 512)
                    keep_low(dve, XT[1][:, chunk], bank[u][:], XT[0][:, chunk]).then_inc(norm.s_xs, 1)
                norm.scale(dve, 0, 0)
                norm.scale(dve, 1, 1)
                low(0, 0)
                with stepped(dve, 2, NQ, 2) as q:
                    norm.scale(dve, q, 0)
                    low(q - 1, 1)
                    norm.scale(dve, q + 1, 1)
                    low(q, 0)
                low(NQ - 1, 1)
        own.close()

        own = ExitStack()

        def parts(name, shape, count=None):
            if count is None:
                return [sb(f"{name}_{part}", shape, ctx=own) for part in ("high", "low")]
            return [parts(f"{name}{i}", shape) for i in range(count)]

        wvp = parts("c_wvp", [DC, H * C_DH])
        cs = [sb(f"c_cs{i}", [DC, NKV], ctx=own) for i in range(2)]
        csp = parts("c_csp", [DC, NKV], 2)
        xs = parts("c_xs", [P, P], 2)
        ts = parts("c_ts", [P, HG * NKV], 2)
        vs = [sb(f"c_vs{i}", [NKV, H, P], ctx=own) for i in range(2)]
        prob = [sb(f"c_prob{i}", [P, HG, NKV], ctx=own) for i in range(8)]
        probT = [sb(f"c_probT{i}", [NKV, HG * P], ctx=own) for i in range(2)]
        shift = sb("c_shift", [P, 8, HG], ctx=own)
        sums = sb("c_sums", [P, 8, HG], ctx=own)
        recip = sb("c_recip", [P, 8, HG], ctx=own)
        oT = [sb(f"c_oT{i}", [P, 8, P], ctx=own) for i in range(2)]
        key_b, side_b, score_b, turn_b, out_b = bank[0], bank[1], bank[2:4], bank[4:6], bank[6:8]
        s_cs = [sem(f"c_ctx_loaded{i}") for i in range(2)]
        s_wh = sem("c_weights_high")
        s_wl = sem("c_weights_split")
        s_ch = sem("c_ctx_high")
        s_cl = sem("c_ctx_split")
        s_xs = sem("c_xs_placed")
        s_key = sem("c_keys")
        s_kh = sem("c_keys_high")
        s_kcopy = sem("c_keys_split")
        s_score = sem("c_scores")
        s_shift = sem("c_shift_ready")
        s_exp = sem("c_exp")
        s_recip = sem("c_recip_ready")
        s_norm = sem("c_probs_normed")
        s_turn = sem("c_probs_turned")
        s_copied = sem("c_probs_copied")
        s_v = sem("c_values")
        s_vcopy = sem("c_values_copied")
        s_vzero = sem("c_values_cleared")
        s_pv = sem("c_pv")
        s_ocopy = sem("c_heads_copied")
        s_y = sem("c_projected")
        s_add = sem("c_added")

        def at(bb, k):
            return bb + k // NG, k % NG, (k // NG) % 2

        def here(bb, k):
            return not absent(bb, k // 4, NB)

        def value_columns(t, half):
            first = t[:].rearrange("p h c -> p (h c)")[:, half * 8 * P:half * 8 * P + C_DH]
            first = first.unsqueeze(1).unsqueeze(1)
            return bass.AP(first.tensor, first.offset, [list(first.ap[0]), [2 * P, 4], [P + C_DH, 2], [1, C_DH]])

        with nc.Block() as block:
            @block.sync
            def _(sp):
                def body(b, u):
                    wait(sp, s_cl, b - 1)
                    wait(sp, s_key, b * 4 - 4)
                    sp.dma_start(cs[u][:], ctxT[b] if isinstance(b, int) else
                                 ctxT[bass.ds(b, 1)].rearrange("b e t -> e (b t)")).then_inc(s_cs[u], 16)
                body(0, 0)
                body(1, 1)
                with stepped(sp, 2, NB, 2) as b:
                    body(b, 0)
                    body(b + 1, 1)

            @block.gpsimd
            def _(pool):
                pool.wait_ge(s_wh, 1)
                keep_low(pool, wvp[1][:], small["c_wv"][:], wvp[0][:]).then_inc(s_wl, 1)
                for u in range(2):
                    i = pool.memset(vs[u][:], 0.0)
                i.then_inc(s_vzero, 1)

                def place_tokens(b, u):
                    wait(pool, s_score, b * 4 - 4)
                    for part in range(2):
                        i = pool.tensor_copy(xs[u][part][:].bitcast(F32R), XT[part][:, bass.ds(b * P, P)])
                    i.then_inc(s_xs, 1)

                def low_context(b, u):
                    pool.wait_ge(s_ch, b + 1)
                    keep_low(pool, csp[u][1][:], cs[u][:], csp[u][0][:]).then_inc(s_cl, 1)

                low_context(0, 0)
                place_tokens(0, 0)

                def slot(bb, j):
                    if here(bb, j - 3):
                        n = bb * 4 + (j - 3)
                        k = (j - 3) % 8
                        pool.wait_ge(s_recip, n + 1)
                        pool.tensor_tensor(prob[k][:], prob[k][:],
                                           recip[:, k, :].unsqueeze(2).broadcast_to([P, HG, NKV]),
                                           ALU.mult).then_inc(s_norm, 1)
                    if j % 4 == 2 and here(bb, j + 4):
                        b, g, u = at(bb, j + 4)
                        low_context(b, u)
                        place_tokens(b, u)
                pipeline_b(pool, slot, 3)

            @block.tensor
            def _(pe):
                pe.wait_ge(s_wl, 1)

                def values(b, u, half):
                    wait(pe, s_vcopy, b * 2 + half)
                    if half == 0:
                        pe.wait_ge(s_cl, b + 1)
                    else:
                        wait(pe, s_add, b - 2)
                    split_product(pe, side_b[0:NKV, :], [t[:] for t in csp[u]],
                                  [t[:, half * 512:(half + 1) * 512] for t in wvp]).then_inc(s_v, 1)

                def slot(bb, j):
                    if here(bb, j):
                        b, g, u = at(bb, j)
                        n = bb * 4 + j
                        if g == 0:
                            pe.wait_ge(s_cs[u], (b - u) * 8 + 16)
                        wait(pe, s_kcopy, n)
                        for h in range(HG):
                            t = pe.matmul(key_b[:, h * NKV:(h + 1) * NKV], mT[:, g * HG + h, :], cs[u][:],
                                          start=True, stop=True)
                        t.then_inc(s_key, 1)
                    if here(bb, j - 1):
                        b, g, u = at(bb, j - 1)
                        n = bb * 4 + (j - 1)
                        if g == 0:
                            pe.wait_ge(s_xs, b + 1)
                        pe.wait_ge(s_kcopy, n + 1)
                        wait(pe, s_exp, n - 1)
                        split_product(pe, score_b[g % 2][:, 0:HG * NKV], [t[:] for t in xs[u]],
                                      [t[:] for t in ts[g % 2]]).then_inc(s_score, 1)
                    if here(bb, j - 5):
                        b, g, u = at(bb, j - 5)
                        n = bb * 4 + (j - 5)
                        pe.wait_ge(s_norm, n + 1)
                        wait(pe, s_copied, n - 1)
                        for h in range(HG):
                            t = pe.transpose(turn_b[g % 2][0:NKV, h * P:(h + 1) * P], prob[(j - 5) % 8][:, h, :],
                                             ident[:])
                        t.then_inc(s_turn, 1)
                    if here(bb, j - 7):
                        b, g, u = at(bb, j - 7)
                        n = bb * 4 + (j - 7)
                        half = g // 2
                        pe.wait_ge(s_copied, n + 1)
                        if g % 2 == 0:
                            pe.wait_ge(s_vcopy, b * 2 + 1 + half)
                            wait(pe, s_ocopy, b * 2 - 1 + half)
                        for h in range(HG):
                            pair = (g % 2) * 2 + h // 2
                            t = pe.matmul(out_b[half][:, pair * P:(pair + 1) * P], vs[u][:, g * HG + h, :],
                                          probT[g % 2][:, h * P:(h + 1) * P], start=(h % 2 == 0), stop=(h % 2 == 1))
                        t.then_inc(s_pv, 1)
                    if j % 4 in (0, 3) and here(bb, j):
                        b, g, u = at(bb, j)
                        values(b, u, g // 2)
                    if (j - 10) % 4 == 3 and here(bb, j - 10):
                        b, g, u = at(bb, j - 10)
                        pe.wait_ge(s_ocopy, b * 2 + 2)
                        if isinstance(b, int) and b >= NB - 3:
                            pe.wait_ge(s_vcopy, NB * 2)
                            if b > NB - 3:
                                pe.wait_ge(s_add, b)
                        else:
                            pe.wait_ge(s_vcopy, b * 2 + 7)
                        for k in range(8):
                            t = pe.matmul(side_b[:, 0:D], oT[u][:, k, :], c_wo[:, k, :], start=(k == 0), stop=(k == 7))
                        t.then_inc(s_y, 1)
                pipeline_b(pe, slot, 10)

            @block.scalar
            def _(act):
                act.wait_ge(s_vzero, 1)

                def slot(bb, j):
                    if j % 4 in (0, 1) and here(bb, j - 1):
                        b, g, u = at(bb, j - 1)
                        half = g // 2
                        act.wait_ge(s_v, b * 2 + 1 + half)
                        wait(act, s_pv, b * 4 - 6 + 2 * half)
                        act.activation(value_columns(vs[u], half),
                                       side_b[0:NKV, :].rearrange("p (r s v) -> p r s v", r=4, s=2),
                                       ACT.Copy).then_inc(s_vcopy, 1)
                    if here(bb, j - 6):
                        b, g, u = at(bb, j - 6)
                        n = bb * 4 + (j - 6)
                        act.wait_ge(s_turn, n + 1)
                        wait(act, s_pv, n - 1)
                        act.activation(probT[g % 2][:], turn_b[g % 2][0:NKV, :], ACT.Copy).then_inc(s_copied, 1)
                    if here(bb, j - 1):
                        b, g, u = at(bb, j - 1)
                        n = bb * 4 + (j - 1)
                        k = (j - 1) % 8
                        act.wait_ge(s_shift, n + 1)
                        wait(act, s_turn, n - 7)
                        for h in range(HG):
                            i = act.activation(prob[k][:, h, :], score_b[g % 2][:, h * NKV:(h + 1) * NKV], ACT.Exp,
                                               bias=shift[:, k, h:h + 1], accum_out=sums[:, k, h:h + 1])
                        i.then_inc(s_exp, 1)
                pipeline_b(act, slot, 6)

            @block.vector
            def _(dve):
                keep_high(dve, wvp[0][:], small["c_wv"][:]).then_inc(s_wh, 1)

                def high_context(b, u):
                    dve.wait_ge(s_cs[u], (b - u) * 8 + 16)
                    wait(dve, s_v, b * 2 - 2)
                    keep_high(dve, csp[u][0][:], cs[u][:]).then_inc(s_ch, 1)
                high_context(0, 0)

                def slot(bb, j):
                    if here(bb, j):
                        b, g, u = at(bb, j)
                        n = bb * 4 + j
                        dve.wait_ge(s_key, n + 1)
                        wait(dve, s_score, n - 1)
                        keep_high(dve, ts[g % 2][0][:], key_b[:, 0:HG * NKV]).then_inc(s_kh, 1)
                        dve.wait_ge(s_kh, n + 1)
                        keep_low(dve, ts[g % 2][1][:], key_b[:, 0:HG * NKV], ts[g % 2][0][:]).then_inc(s_kcopy, 1)
                    if (j - 11) % 4 == 3 and here(bb, j - 11):
                        b, g, u = at(bb, j - 11)
                        dve.wait_ge(s_y, b + 1)
                        d = X[:, bass.ds(b, 1), :].rearrange("p b d -> p (b d)")
                        dve.tensor_tensor(d, side_b[:, 0:D], d, ALU.add).then_inc(s_add, 1)
                    if here(bb, j - 1):
                        b, g, u = at(bb, j - 1)
                        n = bb * 4 + (j - 1)
                        dve.wait_ge(s_score, n + 1)
                        wait(dve, s_exp, n - 7)
                        dve.tensor_reduce(shift[:, (j - 1) % 8, :],
                                          score_b[g % 2][:, 0:HG * NKV].rearrange("p (h k) -> p h k", h=HG),
                                          AX.X, ALU.max, negate=True).then_inc(s_shift, 1)
                    if here(bb, j - 3):
                        n = bb * 4 + (j - 3)
                        k = (j - 3) % 8
                        dve.wait_ge(s_exp, n + 1)
                        wait(dve, s_norm, n - 7)
                        dve.reciprocal(recip[:, k, :], sums[:, k, :]).then_inc(s_recip, 1)
                    if (j - 8) % 2 == 1 and here(bb, j - 8):
                        b, g, u = at(bb, j - 8)
                        half = g // 2
                        dve.wait_ge(s_pv, b * 4 + 2 + 2 * half)
                        wait(dve, s_y, b - 1)
                        dve.tensor_copy(oT[u][:, half * 4:half * 4 + 4, :].rearrange("p k t -> p (k t)"),
                                        out_b[half][:]).then_inc(s_ocopy, 1)
                    if j % 4 == 2 and here(bb, j + 4):
                        b, g, u = at(bb, j + 4)
                        high_context(b, u)
                pipeline_b(dve, slot, 11)
        own.close()
        att.close()
        if stop_after == 3:
            return dump()

        stats("d_stat", second=True)
        Z = XC
        att = ExitStack()
        QT = sb("d_QT", [P, NB * P], ctx=att)
        KT = sb("d_KT", [P, NB * P], ctx=att)
        V = sb("d_V", [P, NB * P], ctx=att)
        own = ExitStack()
        norm = Norm("d", own, bank[0:2], gain=small["g1"])
        wrot = sb("d_wrot", [LAT, 4, P], ctx=own)
        lat = [sb(f"d_lat{i}", [LAT, 512], ctx=own) for i in range(2)]
        part = [sb(f"d_part{i}", [P, 4, 512], ctx=own) for i in range(2)]
        s_wrot = sem("d_wrot_ready")
        s_v0 = sem("d_values_cleared")
        s_latp = sem("d_latent")
        s_lat = sem("d_latent_copied")
        s_rot = sem("d_rope_products")
        s_part = sem("d_rope_parts")
        s_sum = sem("d_rope_summed")
        s_v = sem("d_values")
        s_vcopy = sem("d_values_copied")
        with nc.Block() as block:
            @block.gpsimd
            def _(pool):
                pool.memset(V[:], 0.0).then_inc(s_v0, 1)
                pool.memset(wrot[:], 0.0).then_inc(s_wrot, 1)
                pool.wait_ge(s_wrot, 1)
                for k, name in enumerate(("d_q", "d_k")):
                    src = small[name][:].rearrange("p (h i two) -> p h i two", h=H, two=2)
                    dst = wrot[:, 2 * k, :].rearrange("p (h i two) -> p h i two", h=H, two=2)
                    turned = wrot[:, 2 * k + 1, :].rearrange("p (h i two) -> p h i two", h=H, two=2)
                    pool.tensor_copy(dst[:, :, 0:2, :], src)
                    pool.tensor_copy(turned[:, :, 0:2, 0], src[:, :, :, 1])
                    i = pool.tensor_copy(turned[:, :, 0:2, 1], src[:, :, :, 0])
                i.then_inc(s_wrot, 1)

                def body(q, u):
                    pool.wait_ge(s_part, q + 1)
                    pool.tensor_tensor(QT[:, bass.ds(q * 512, 512)], part[u][:, 0, :], part[u][:, 1, :], ALU.add)
                    pool.tensor_tensor(KT[:, bass.ds(q * 512, 512)], part[u][:, 2, :], part[u][:, 3, :],
                                       ALU.add).then_inc(s_sum, 1)
                over_quads(pool, body)

            @block.tensor
            def _(pe):
                pe.wait_ge(s_wrot, 2)

                def body(q, u):
                    norm.turn(pe, q, u)
                    pe.wait_ge(norm.s_xs, q + 1)
                    wait(pe, s_lat, q)
                    pe.matmul(bank[2][0:LAT, :], small["d_down"][:], norm.xs[u][:], start=True,
                              stop=True).then_inc(norm.s_used, 1)
                    pe.wait_ge(s_lat, q + 1)
                    wait(pe, s_vcopy, q)
                    for j in range(4):
                        t = pe.matmul(bank[3][:, j * LAT:(j + 1) * LAT], lat[u][:, j * P:(j + 1) * P],
                                      small["d_v"][:], start=True, stop=True)
                    t.then_inc(s_v, 1)
                    wait(pe, s_part, q)
                    for k in range(4):
                        t = pe.matmul(bank[4 + k][:], wrot[:, k, :], lat[u][:], start=True, stop=True)
                    t.then_inc(s_rot, 1)
                over_quads(pe, body)

            @block.scalar
            def _(act):
                act.wait_ge(s_v0, 1)

                def body(q, u):
                    norm.copy(act, q, u)
                    act.wait_ge(norm.s_used, q + 1)
                    wait(act, s_rot, q - 1)
                    act.activation(lat[u][:], bank[2][0:LAT, :], ACT.Copy).then_inc(s_lat, 1)
                    act.wait_ge(s_v, q + 1)
                    act.activation(V[:, bass.ds(q * 512, 512)].rearrange("p (b h v) -> p b h v", b=4, h=H)[:, :, :, 0:4],
                                   bank[3][:, 0:4 * LAT].rearrange("p (b h v) -> p b h v", b=4, h=H),
                                   ACT.Copy).then_inc(s_vcopy, 1)
                over_quads(act, body)

            @block.vector
            def _(dve):
                def body(q, u):
                    norm.scale(dve, q, u)
                    dve.wait_ge(s_rot, q + 1)
                    wait(dve, s_sum, q - 1)
                    for k in range(4):
                        t = dve.tensor_tensor(part[u][:, k, :].rearrange("p (b t) -> p b t", b=4),
                                              bank[4 + k][:].rearrange("p (b t) -> p b t", b=4),
                                              rope[:, k, :].unsqueeze(1).broadcast_to([P, 4, P]), ALU.mult)
                    t.then_inc(s_part, 1)
                over_quads(dve, body)
        own.close()
        own = ExitStack()
        attend("dt", own, QT, KT, V, P, d_up8, None, Z)
        own.close()
        att.close()

        stats("e_stat", src=XC)
        moe = ExitStack()
        XT = [sb(f"e_XT_{part}", [P, NB * P], ctx=moe) for part in ("high", "low")]
        YT = sb("e_YT", [P, NB * P], ctx=moe)
        combT = sb("e_combT", [P, NB * P], F16, ctx=moe)
        own = ExitStack()
        norm = Norm("e", own, bank[0:2], gain=small["g2"])
        ex = [sb(f"e_exp{i}", [P, 4, E1], ctx=own) for i in range(2)]
        lg = [sb(f"e_logit{i}", [P, 4, E1], ctx=own) for i in range(2)]
        mx = sb("e_max", [P, 4], ctx=own)
        pr = sb("e_probs", [P, 4, E1 + 6], ctx=own)
        pm = sb("e_matched", [P, 4, E1 + 6], ctx=own)
        p8 = sb("e_p8", [P, 4, 8], ctx=own)
        ew = sb("e_w", [P, 4, E1], ctx=own)
        es = sb("e_sum", [P, 4], ctx=own)
        s_lg = sem("e_shifted")
        s_ex = sem("e_exp_done")
        s_mx = sem("e_max_ready")
        s_ev = sem("e_route_steps")
        s_epad = sem("e_padded")
        E_STEPS = 11

        def e_scores(router_b, s_logit, finish_comb):
            def dve_scores(dve, q, u):
                if isinstance(q, int) and q == 0:
                    dve.wait_ge(s_epad, 1)
                dve.wait_ge(s_logit, q + 1)
                logits = router_b[u][:, 0:4 * E1].rearrange("p (j e) -> p j e", j=4)
                dve.tensor_reduce(mx[:], logits, AX.X, ALU.max).then_inc(s_mx, 1)
                dve.wait_ge(s_mx, q + 1)
                dve.tensor_tensor(lg[u][:], logits, mx[:].unsqueeze(2).broadcast_to([P, 4, E1]),
                                  ALU.subtract).then_inc(s_lg, 1)
                chain = Chain(dve, s_ev, q * E_STEPS)
                dve.wait_ge(s_ex, q + 1)
                chain(dve.tensor_reduce(es[:], ex[u][:], AX.X, ALU.add))
                chain(dve.reciprocal(es[:], es[:]))
                chain.carried(dve.tensor_tensor(pr[:, :, 0:E1], ex[u][:], es[:].unsqueeze(2).broadcast_to([P, 4, E1]), ALU.mult))
                for j in range(4):
                    i = dve.max(p8[:, j, :], pr[:, j, :])
                chain.carried(i)
                for j in range(4):
                    i = dve.match_replace(pm[:, j, :], p8[:, j, :], pr[:, j, :], -BIG)
                chain(i)
                chain(dve.tensor_tensor(ew[:], pm[:, :, 0:E1], pr[:, :, 0:E1], ALU.not_equal))
                chain(dve.tensor_tensor(ew[:], ew[:], pr[:, :, 0:E1], ALU.mult))
                chain(dve.tensor_reduce(es[:], ew[:], AX.X, ALU.add))
                chain(dve.tensor_scalar(es[:], es[:], 1.0 / COMB_UP, None, ALU.mult))
                chain(dve.reciprocal(es[:], es[:]))
                dve.tensor_tensor(ew[:], ew[:], es[:].unsqueeze(2).broadcast_to([P, 4, E1]), ALU.mult).then_inc(s_ewd, 1)
                dve.wait_ge(s_ewd, q + 1)
                finish_comb(dve, chain, ew[:], q, u)

            def act_scores(act, q, u):
                act.wait_ge(s_lg, q + 1)
                wait(act, s_ev, (q - 2) * E_STEPS + 3)
                act.activation(ex[u][:], lg[u][:], ACT.Exp).then_inc(s_ex, 1)

            def pool_setup(pool):
                pad_top(pool, pr, E1, E1 + 6, s_epad)
            return dve_scores, act_scores, pool_setup

        s_ewd = sem("e_weights_ready")
        route("e_route", own, XT, combT, norm, small["d_router"], E1, e_scores, None)
        own.close()
        s_res = sem("e_residual")
        with nc.Block() as block:
            @block.vector
            def _(dve):
                dve.scalar_tensor_tensor(X[:].rearrange("p b d -> p (b d)"), Z[:].rearrange("p b d -> p (b d)"),
                                         tg[:, 3:4], X[:].rearrange("p b d -> p (b d)"), ALU.mult,
                                         ALU.add).then_inc(s_res, 1)
        experts("e_moe", XT, combT, P, w["e_wg"], w["e_wu"], w["e_wd"], consts["sel1"], E1 * I1 // P, True, YT)
        add_experts("e_add", YT, tg[:, 3:4], True)
        moe.close()


def constants():
    head = (np.arange(P) % 32) // 8
    headsel = (head[:, None] == np.arange(HG)[None, :]).astype(np.float32)
    d = np.arange(P) % 8
    inv = (np.float32(1.0) / np.float32(10000.0) ** (np.arange(0, 4, 2, dtype=np.float32) / np.float32(4))).astype(np.float32)
    ang = (np.arange(P, dtype=np.float32)[None, :] * inv[np.minimum(d // 2, 1)][:, None]).astype(np.float32)
    used = (d < 4).astype(np.float32)[:, None]
    cos = (np.cos(ang) * used).astype(np.float32)
    sin = (np.sin(ang) * used * np.where(d % 2 == 0, -1.0, 1.0)[:, None]).astype(np.float32)
    rope = np.stack([cos * 0.5, sin * 0.5, cos, sin], axis=1).astype(np.float32)
    causal = np.where(np.arange(P)[None, :] > np.arange(P)[:, None], -1e30, 0.0).astype(np.float32)

    def sel(ne, width):
        e = np.arange(ne * width) // width
        one = (np.arange(ne)[:, None] == e[None, :]).astype(np.float32) / COMB_UP
        both = np.zeros((P, ne * width), np.float16)
        both[0:ne] = one
        both[ne:2 * ne] = one
        return both
    return {"ident": np.eye(P, dtype=np.float32), "headsel": headsel, "rope": rope, "causal": causal,
            "sel0": sel(E0, I0), "sel1": sel(E1, I1)}


def layout(i):
    t = np.ascontiguousarray
    n = {k: np.asarray(v) for k, v in i.items()}
    w = {
        "a_wq": n["L0_xattn_Wq"], "a_wk": n["L0_xattn_Wk"], "a_wv": n["L0_xattn_Wv"], "a_wo": n["L0_xattn_Wo"],
        "a_bq": n["L0_xattn_bq"].reshape(D, 1), "a_bk": n["L0_xattn_bk"].reshape(D, 1),
        "a_bv": n["L0_xattn_bv"], "a_bvc": n["L0_xattn_bv"].reshape(D, 1), "a_bo": n["L0_xattn_bo"],
        "a_gate": t(n["L0_ffn_gate_w"].T), "a_gbias": n["L0_ffn_gate_bias"],
        "b_wgT": t(n["L0_ffn_eg_w"].reshape(E0 * I0, D).T), "b_wuT": t(n["L0_ffn_eu_w"].reshape(E0 * I0, D).T),
        "b_wdT": t(n["L0_ffn_ed_w"].transpose(0, 2, 1)).reshape(E0 * I0, D),
        "sgT": t(n["L0_ffn_sg_w"].T), "suT": t(n["L0_ffn_su_w"].T), "sdT": t(n["L0_ffn_sd_w"].T),
        "c_wv": n["L1_xattn_Wv"], "c_wo": n["L1_xattn_Wo"], "c_bo": n["L1_xattn_bo"],
        "c_wkT": t(n["L1_xattn_Wk"].T), "c_wqT": t(n["L1_xattn_Wq"].T),
        "g1": n["L1_ffn_g1"].reshape(D, 1), "g2": n["L1_ffn_g2"].reshape(D, 1),
        "d_down": n["L1_ffn_w_down"], "d_q": n["L1_ffn_wq"], "d_k": n["L1_ffn_wk"], "d_v": n["L1_ffn_wv"],
        "d_up": n["L1_ffn_w_up"], "d_router": n["L1_ffn_router_w"],
        "e_wg": t(n["L1_ffn_w1"].transpose(1, 0, 2)).reshape(D, E1 * I1),
        "e_wu": t(n["L1_ffn_w3"].transpose(1, 0, 2)).reshape(D, E1 * I1),
        "e_wd": n["L1_ffn_w2"].reshape(E1 * I1, D),
    }
    main = {"x": n["x"], "ctxT": t(n["ctx_768"].transpose(0, 2, 1)), "gx": n["g_xattn"], "gf": n["g_ffn"]}
    return main, w


def kernel(stop_after=99, **inputs):
    import concourse.bacc as bacc
    from concourse.bass_utils import run_bass_kernel_spmd

    nc = bacc.Bacc("TRN2", target_bir_lowering=False, num_devices=1)
    main, w = layout(inputs)
    arrays = {}

    def declare(group):
        aps = {}
        for name, a in group.items():
            arrays["in_" + name] = a
            aps[name] = nc.dram_tensor("in_" + name, a.shape, mybir.dt.from_np(a.dtype), kind="ExternalInput").ap()
        return aps

    m, weights, consts = declare(main), declare(w), declare(constants())
    out = nc.dram_tensor("out_0", (NB, P, D), F32, kind="ExternalOutput").ap()
    build(nc, m["x"], m["ctxT"], m["gx"], m["gf"], weights, consts, out, stop_after)
    r = run_bass_kernel_spmd(nc, [arrays], core_ids=[0])
    return r.results[0]["out_0"]
```

```python
from contextlib import ExitStack, contextmanager

import numpy as np
import concourse.bass as bass
from concourse import mybir

F32 = mybir.dt.float32
F32R = mybir.dt.float32r
F16 = mybir.dt.float16
BF16 = mybir.dt.bfloat16
I32 = mybir.dt.int32
ALU = mybir.AluOpType
ACT = mybir.ActivationFunctionType
AX = mybir.AxisListType

P = 128
NB = 32
NQ = NB // 4
D = 128
DC = 96
NKV = 120
H = 16
HG = 4
NG = H // HG
EPS = 1e-5
CLAMP = 1e4
A_SCALE = 8 ** -0.5
C_DH = 64
E0, I0, TG0, K0 = 64, 64, 4, 6
E1, I1, K1 = 8, 256, 2
HIGH_BITS = -4096
COMB_UP = 4096.0
LAT = 64


def wait(eng, sem, count):
    if isinstance(count, int) and count <= 0:
        return
    eng.wait_ge(sem, count)


@contextmanager
def stepped(eng, start, end, step):
    with eng.Fori(start // step, end // step) as k:
        yield k * step


def absent(base, k, items):
    return isinstance(base, int) and not 0 <= base + k < items


def keep_high(eng, high, x):
    return eng.tensor_copy(high.bitcast(F32R), x)


def keep_low(eng, low, x, high):
    return eng.tensor_tensor(low.bitcast(F32R), x, high, ALU.subtract)


def split_product(pe, out, w, x, start=True, stop=True):
    pe.matmul(out, w[0].bitcast(F32R), x[0].bitcast(F32R), start=start, stop=False)
    pe.matmul(out, w[1].bitcast(F32R), x[0].bitcast(F32R), start=False, stop=False)
    return pe.matmul(out, w[0].bitcast(F32R), x[1].bitcast(F32R), start=False, stop=stop)


def build(nc, x, ctxT, gx, gf, w, consts, out, stop_after=99):
    top = ExitStack()
    with top:
        def sb(name, shape, dt=F32, ctx=top):
            return ctx.enter_context(nc.sbuf_tensor(name, shape, dt))

        in_use = []

        def sem(name):
            in_use.append(nc.alloc_semaphore(name))
            return in_use[-1]

        def renew_semaphores():
            nc.clear_and_free_semaphores(list(in_use))
            in_use.clear()
            nc.all_engine_barrier()

        bank = [top.enter_context(nc.psum_tensor(f"bank{i}", [P, 512], F32)) for i in range(8)]

        X = sb("X", [P, NB, D])
        XC = sb("XC", [P, NB, D])
        stat = sb("stat", [P, 4, NB])
        ident = sb("ident", [P, P])
        ones = sb("ones", [P, P])
        gates = sb("gates", [P, 4])
        tg = sb("tg", [P, 4])
        headsel = sb("headsel", [P, HG])

        s_load = sem("loaded")
        s_tg = sem("gates_tanh")
        s_zrow = sem("zero_rows_set")
        small = {}

        def load_small(name, shape):
            small[name] = sb("w_" + name, shape)
            return small[name]

        for name, shape in (("a_wq", [D, D]), ("a_wk", [DC, D]), ("a_wv", [DC, D]),
                            ("a_bq", [D, 1]), ("a_bk", [D, 1]), ("a_bvc", [D, 1]), ("a_wo", [D, D]), ("a_gate", [D, E0]),
                            ("sgT", [D, D]), ("suT", [D, D]), ("sdT", [D, D]),
                            ("c_wv", [DC, H * C_DH]), ("g1", [D, 1]), ("g2", [D, 1]),
                            ("d_down", [D, LAT]), ("d_q", [LAT, LAT]), ("d_k", [LAT, LAT]),
                            ("d_v", [LAT, LAT]), ("d_router", [D, E1])):
            load_small(name, shape)
        c_wo = sb("c_wo", [P, 8, D])
        a_wo8 = sb("a_wo8", [64, 2, D])
        d_up8 = sb("d_up8", [64, 2, D])
        mT = sb("mT", [DC, H, D])
        bo0 = sb("bo0", [P, D])
        bo1 = sb("bo1", [P, D])
        bv0 = sb("bv0", [P, D])
        gb0 = sb("gb0", [P, E0])
        rope = sb("rope", [P, 4, P])
        causal = sb("causal", [P, P])
        causal16 = sb("causal16", [P, HG, P], BF16)
        ident16 = sb("ident16", [P, P], BF16)
        identh = sb("identh", [P, P], F16)

        prep = ExitStack()
        wkT = sb("wkT", [C_DH, H, DC], ctx=prep)
        wqT = sb("wqT", [C_DH, H, D], ctx=prep)
        s_mt = sem("m_ready")
        s_mtfree = sem("m_copied")
        s_const = sem("constants_ready")
        loads = []

        def load(eng, dst, src, s):
            eng.dma_start(dst, src).then_inc(s, 16)
            if s is s_load:
                loads.append(1)

        small_names = list(small)
        many_loads = len(small_names) + 1 + 8 + 3 + 4 + 2 + 4

        class Setup:

            @staticmethod
            def sync(sp):
                for q in range(4):
                    load(sp, X[:, 8 * q:8 * q + 8, :], x[8 * q:8 * q + 8].rearrange("b t d -> t b d"), s_xload)
                load(sp, ident[:], consts["ident"], s_load)
                load(sp, headsel[:], consts["headsel"], s_load)
                load(sp, rope[:], consts["rope"], s_load)
                load(sp, causal[:], consts["causal"], s_load)
                load(sp, wkT[:], w["c_wkT"].rearrange("(h p) e -> p h e", p=C_DH), s_load)
                load(sp, wqT[:], w["c_wqT"].rearrange("(h p) d -> p h d", p=C_DH), s_load)
                load(sp, c_wo[:], w["c_wo"].rearrange("(j p) d -> p j d", p=P), s_load)
                for t, name in ((bo1, "c_bo"), (bv0, "a_bv"), (gb0, "a_gbias")):
                    load(sp, t[:], w[name].partition_broadcast(P), s_load)
                sp.wait_ge(s_zrow, 1)
                for i in range(8):
                    load(sp, d_up8[8 * i:8 * i + 4], w["d_up"].rearrange("(p i d) n -> i d p n", p=2, i=8)[i], s_load)

            @staticmethod
            def scalar(act):
                load(act, gates[:, 0:2], gx.partition_broadcast(P), s_load)
                load(act, gates[:, 2:4], gf.partition_broadcast(P), s_load)
                load(act, bo0[:], w["a_bo"].partition_broadcast(P), s_load)
                load(act, a_wo8[:], w["a_wo"].rearrange("(p r) n -> r p n", p=2), s_load)
                for name in small_names:
                    load(act, small[name][:], w[name], s_load)
                act.wait_ge(s_load, all_loads)
                act.activation(tg[:], gates[:], ACT.Tanh).then_inc(s_tg, 1)
                for g in range(NG):
                    act.wait_ge(s_mt, g + 1)
                    act.activation(mT[:, HG * g:HG * g + HG, :], bank[g][0:DC, :].rearrange("p (h d) -> p h d", h=HG),
                                   ACT.Copy, scale=C_DH ** -0.5)

            @staticmethod
            def tensor(pe):
                pe.wait_ge(s_load, all_loads)
                for g in range(NG):
                    for j in range(HG):
                        h = HG * g + j
                        last = pe.matmul(bank[g][0:DC, j * D:(j + 1) * D], wkT[:, h, :], wqT[:, h, :],
                                         start=True, stop=True)
                    last.then_inc(s_mt, 1)

            @staticmethod
            def gpsimd_first(pool):
                pool.memset(d_up8[:], 0.0).then_inc(s_zrow, 1)
                pool.memset(ones[:], 1.0)

            @staticmethod
            def gpsimd_last(pool):
                pool.wait_ge(s_load, all_loads)
                pool.tensor_copy(ident16[:], ident[:])
                pool.tensor_copy(identh[:], ident[:])
                pool.tensor_copy(causal16[:], causal[:].unsqueeze(1).broadcast_to([P, HG, P]))

            @staticmethod
            def vector(dve):
                dve.wait_ge(s_tg, 1)
                dve.tensor_scalar(bo0[:], bo0[:], tg[:, 0:1], None, ALU.mult).then_inc(s_bo, 1)
                dve.tensor_scalar(small["a_wo"][:], small["a_wo"][:], tg[:, 0:1], None, ALU.mult)
                dve.tensor_scalar(a_wo8[:], a_wo8[:], tg[0:64, 0:1], None, ALU.mult)
                dve.tensor_scalar(c_wo[:], c_wo[:], tg[:, 1:2], None, ALU.mult)
                dve.tensor_scalar(bo1[:], bo1[:], tg[:, 1:2], None, ALU.mult)
                dve.tensor_scalar(small["a_bq"][:], small["a_bq"][:], A_SCALE, None, ALU.mult)
                dve.wait_ge(s_bo, 1)

        s_xload = sem("tokens_loaded")
        s_bo = sem("bias_gated")
        all_loads = 16 * many_loads

        def stats(tag, bias=None, second=False, src=X, setup=None):
            s_bn = sem(tag + "_tile_stats")
            s_mv = sem(tag + "_mean_and_variance")
            s_msq = sem(tag + "_mean_squares")
            s_cen = sem(tag + "_centred")
            s_rs = sem(tag + "_rstd")
            s_exp = sem(tag + "_exponent_set")
            own = ExitStack()
            bn = sb(tag + "_bn", [P, NB, 6], ctx=own)
            mv = sb(tag + "_mv", [P, NB, 2], ctx=own)
            expo = sb(tag + "_expo", [P, NB], ctx=own)
            rms_only = src is XC
            with nc.Block() as block:
                if setup is not None:
                    block.sync(setup.sync)
                    block.scalar(setup.scalar)
                    block.tensor(setup.tensor)

                @block.vector
                def _(dve):
                    for b in range(NB):
                        if setup is not None and b == 0:
                            dve.wait_ge(s_xload, 64)
                        i = dve.bn_stats(bn[:, b, :], src[:, b, :])
                    i.then_inc(s_bn, 1)
                    dve.wait_ge(s_bn, 1)
                    for b in range(NB):
                        i = dve.bn_aggr(mv[:, b, :], bn[:, b, :])
                    i.then_inc(s_mv, 1)
                    dve.wait_ge(s_mv, 1)
                    if rms_only:
                        dve.tensor_tensor(stat[:, 0, :], mv[:, :, 0], mv[:, :, 0], ALU.mult).then_inc(s_mv, 1)
                        dve.wait_ge(s_mv, 2)
                        dve.scalar_tensor_tensor(stat[:, 2, :], stat[:, 0, :], EPS, mv[:, :, 1], ALU.add,
                                                 ALU.add).then_inc(s_msq, 1)
                    else:
                        dve.tensor_scalar(stat[:, 2, :], mv[:, :, 1], EPS, None, ALU.add).then_inc(s_msq, 1)
                        dve.tensor_tensor(XC[:], X[:], mv[:, :, 0:1].broadcast_to([P, NB, D]),
                                          ALU.subtract).then_inc(s_cen, 1)
                    if setup is not None:
                        setup.vector(dve)
                    if bias is not None:
                        dve.tensor_tensor(X[:], X[:], bias[:].unsqueeze(1).broadcast_to([P, NB, D]), ALU.add)
                    if second:
                        dve.wait_ge(s_rs, 1)
                        dve.tensor_tensor(stat[:, 0, :], stat[:, 3, :], stat[:, 3, :], ALU.mult).then_inc(s_mv, 1)
                        dve.wait_ge(s_mv, 2)
                        dve.tensor_tensor(stat[:, 1, :], stat[:, 0, :], mv[:, :, 1], ALU.mult).then_inc(s_mv, 1)
                        dve.wait_ge(s_mv, 3)
                        dve.tensor_scalar(stat[:, 2, :], stat[:, 1, :], EPS, None, ALU.add).then_inc(s_msq, 1)
                        dve.wait_ge(s_cen, 1)
                        dve.tensor_tensor(XC[:], XC[:], stat[:, 3, :].unsqueeze(2).broadcast_to([P, NB, D]),
                                          ALU.mult).then_inc(s_cen, 1)

                @block.gpsimd
                def _(pool):
                    if setup is not None:
                        setup.gpsimd_first(pool)
                    pool.memset(expo[:], -0.5).then_inc(s_exp, 1)
                    pool.wait_ge(s_exp, 1)
                    pool.wait_ge(s_msq, 1)
                    pool.tensor_tensor(stat[:, 3, :], stat[:, 2, :], expo[:], ALU.pow).then_inc(s_rs, 1)
                    if second:
                        pool.wait_ge(s_msq, 2)
                        pool.wait_ge(s_cen, 2)
                        pool.tensor_tensor(stat[:, 3, :], stat[:, 2, :], expo[:], ALU.pow).then_inc(s_rs, 1)
                    if setup is not None:
                        setup.gpsimd_last(pool)
            own.close()

        class Norm:

            def __init__(self, tag, ctx, banks, gain=None, lookahead=1):
                self.xn = [sb(f"{tag}_xn{i}", [P, 4, D], ctx=ctx) for i in range(2)]
                self.xs = [sb(f"{tag}_xs{i}", [P, 512], ctx=ctx) for i in range(2)]
                self.banks, self.gain = banks, gain
                self.s_scaled = sem(tag + "_scaled")
                self.s_turned = sem(tag + "_turned")
                self.s_xs = sem(tag + "_xs")
                self.s_used = sem(tag + "_xs_used")

            def scale(self, dve, q, u):
                wait(dve, self.s_turned, q - 1)
                dve.tensor_tensor(self.xn[u][:], XC[:, bass.ds(q * 4, 4), :],
                                  stat[:, 3, bass.ds(q * 4, 4)].unsqueeze(2).broadcast_to([P, 4, D]),
                                  ALU.mult).then_inc(self.s_scaled, 1)

            def turn(self, pe, q, u):
                pe.wait_ge(self.s_scaled, q + 1)
                wait(pe, self.s_xs, q - 1)
                for j in range(4):
                    t = pe.transpose(self.banks[u][:, j * P:(j + 1) * P], self.xn[u][:, j, :], ident[:])
                t.then_inc(self.s_turned, 1)

            def copy(self, act, q, u):
                act.wait_ge(self.s_turned, q + 1)
                wait(act, self.s_used, q - 1)
                if self.gain is None:
                    i = act.activation(self.xs[u][:], self.banks[u][:], ACT.Copy)
                else:
                    i = act.activation(self.xs[u][:], self.banks[u][:], ACT.Copy, scale=self.gain[:, 0:1])
                i.then_inc(self.s_xs, 1)

        def quads_ahead(eng, before, body, most=2):
            before()
            body(0, 0, most)
            body(1, 1, most)
            with stepped(eng, 2, NQ - 2, 2) as q:
                body(q, 0, most)
                body(q + 1, 1, most)
            body(NQ - 2, 0, 1)
            body(NQ - 1, 1, 0)

        def over_quads(eng, body):
            body(0, 0)
            body(1, 1)
            with stepped(eng, 2, NQ, 2) as q:
                body(q, 0)
                body(q + 1, 1)

        def attend(tag, ctx, QT, KT, V, nk, wo, raw, dst):
            clamp = raw is not None
            qs = [[sb(f"{tag}_qs_{part}{i}", [P, P], ctx=ctx) for part in ("high", "low")] for i in range(2)]
            ks = [[sb(f"{tag}_ks_{part}{i}", [P, nk], ctx=ctx) for part in ("high", "low")] for i in range(2)]
            kd = [[sb(f"{tag}_kd_{part}{i}", [P, HG, nk], ctx=ctx) for part in ("high", "low")] for i in range(2)]
            vh = [sb(f"{tag}_vh{i}", [nk, H, P], ctx=ctx) for i in range(2)]
            prob = [sb(f"{tag}_prob{i}", [P, HG, nk], ctx=ctx) for i in range(8)]
            probT = [sb(f"{tag}_probT{i}", [nk, HG * P], ctx=ctx) for i in range(2)]
            negmax = sb(tag + "_negmax", [P, 4, HG], ctx=ctx)
            shift = sb(tag + "_shift", [P, 4, HG], ctx=ctx)
            floor = sb(tag + "_floor", [P, 4, HG], ctx=ctx)
            low = sb(tag + "_low", [P, 1], ctx=ctx)
            recip = [sb(f"{tag}_recip{i}", [64, 2 * P], ctx=ctx) for i in range(2)]
            headT = [sb(f"{tag}_headT{i}", [64, 2 * P], ctx=ctx) for i in range(2)]
            score_b, turn_b, out_b = bank[0:4], bank[4:6], bank[6:8]
            s_high = sem(tag + "_qk_high")
            s_low_k = sem(tag + "_k_low")
            s_prep = sem(tag + "_keys_spread")
            s_vprep = sem(tag + "_values_spread")
            s_clear = sem(tag + "_values_cleared")
            s_score = sem(tag + "_scores")
            s_max = sem(tag + "_rowmax")
            s_shift = sem(tag + "_shift_ready")
            s_exp = sem(tag + "_exp")
            s_floor = sem(tag + "_floor_done")
            s_turn = sem(tag + "_probs_turned")
            s_copied = sem(tag + "_probs_copied")
            s_pv = sem(tag + "_pv")
            s_recip = sem(tag + "_recip_ready")
            s_head = sem(tag + "_heads_ready")
            s_y = sem(tag + "_projected")
            s_out = sem(tag + "_out_done")
            s_low = sem(tag + "_low_ready")
            s_probs = s_floor if clamp else s_exp

            def at(bb, k):
                return bb + k // NG, k % NG, (k // NG) % 2

            def own_columns(t, first):
                flat = t[:].rearrange("p h c -> p (h c)")
                head0 = flat[:, first:first + 8].unsqueeze(1).unsqueeze(1)
                return bass.AP(head0.tensor, head0.offset,
                               [list(flat.ap[0]), [8 * P, 2], [P + 8, 8], [1, 8]])

            with nc.Block() as block:
                @block.gpsimd
                def _(pool):
                    def spread(b, u):
                        pool.wait_ge(s_high, b + 1)
                        wait(pool, s_score, b * 4 - 4)
                        keep_low(pool, ks[u][1][:], KT[:, bass.ds(b * nk, nk)], ks[u][0][:]).then_inc(s_low_k, 1)
                        keep_low(pool, qs[u][1][:], QT[:, bass.ds(b * P, P)], qs[u][0][:])
                        pool.wait_ge(s_low_k, b + 1)
                        for part in range(2):
                            t = pool.tensor_tensor(kd[u][part][:].bitcast(F32R), ks[u][part][:].unsqueeze(1).broadcast_to([P, HG, nk]),
                                                   headsel[:].unsqueeze(2).broadcast_to([P, HG, nk]), ALU.mult)
                        t.then_inc(s_prep, 1)

                    def spread_values(b, u):
                        wait(pool, s_pv, b * 4 - 4)
                        pool.tensor_copy(own_columns(vh[u], 0),
                                         V[:, bass.ds(b * P, P)].rearrange("p (p2 i d) -> p p2 i d", p2=2, i=8))\
                            .then_inc(s_vprep, 1)

                    pool.memset(low[:], -CLAMP).then_inc(s_low, 1)
                    for u in range(2):
                        i = pool.memset(vh[u][:], 0.0)
                    i.then_inc(s_clear, 1)
                    pool.wait_ge(s_clear, 1)
                    for u in range(2):
                        i = pool.memset(own_columns(vh[u], 64), 1.0)
                    i.then_inc(s_clear, 1)
                    spread(0, 0)

                    def slot(bb, j):
                        b, g, u = at(bb, j)
                        if g == 1 and not absent(bb, j // 4 + 1, NB):
                            spread(b + 1, 1 - u)
                        if g == 2:
                            spread_values(b, u)

                    pipeline_b(pool, slot, 0)

                @block.tensor
                def _(pe):
                    pe.wait_ge(s_clear, 2)

                    def slot(bb, j):
                        if not absent(bb, j // 4, NB):
                            b, g, u = at(bb, j)
                            n = bb * 4 + j
                            if g == 0:
                                pe.wait_ge(s_prep, b + 1)
                            wait(pe, s_exp, n - 3)
                            if not clamp:
                                pe.matmul(score_b[g][:], ident16[:], causal16[:].rearrange("p h k -> p (h k)"),
                                          start=True, stop=False)
                            rows = slice(32 * g, 32 * g + 32)
                            split_product(pe, score_b[g][:, 0:HG * nk], [t[rows, :] for t in qs[u]],
                                          [t[rows].rearrange("p h k -> p (h k)") for t in kd[u]],
                                          start=clamp).then_inc(s_score, 1)
                        if not absent(bb, (j - 4) // 4, NB):
                            b, g, u = at(bb, j - 4)
                            n = bb * 4 + (j - 4)
                            pe.wait_ge(s_probs, n + 1)
                            wait(pe, s_copied, n - 1)
                            for h in range(HG):
                                t = pe.transpose(turn_b[g % 2][0:nk, h * P:(h + 1) * P], prob[(j - 4) % 8][:, h, :], ident[:])
                            t.then_inc(s_turn, 1)
                        if not absent(bb, (j - 6) // 4, NB):
                            b, g, u = at(bb, j - 6)
                            n = bb * 4 + (j - 6)
                            pe.wait_ge(s_copied, n + 1)
                            if g == 0:
                                pe.wait_ge(s_vprep, b + 1)
                                wait(pe, s_out, b - 1)
                            for h in range(HG):
                                k = (g % 2) * HG + h
                                t = pe.matmul(out_b[u][:, (g // 2) * P:(g // 2 + 1) * P], vh[u][:, g * HG + h, :],
                                              probT[g % 2][:, h * P:(h + 1) * P], start=(k == 0), stop=(k == 7))
                            t.then_inc(s_pv, 1)
                        if (j - 8) % 4 == 3 and not absent(bb, (j - 8) // 4, NB):
                            b, g, u = at(bb, j - 8)
                            pe.wait_ge(s_head, b + 1)
                            for half in range(2):
                                t = pe.matmul(out_b[u][:, 2 * P:2 * P + D], headT[u][:, half * P:(half + 1) * P],
                                              wo[:, half, :], start=(half == 0), stop=(half == 1))
                            t.then_inc(s_y, 1)

                    pipeline_b(pe, slot, 8)

                def copy_probs(eng, bb, k):
                    n = bb * 4 + k
                    g = k % NG
                    eng.wait_ge(s_turn, n + 1)
                    wait(eng, s_pv, n - 1)
                    if not clamp:
                        wait(eng, s_copied, n)
                    if clamp or g % 2:
                        i = nc.scalar.activation(probT[g % 2][:], turn_b[g % 2][0:nk, :], ACT.Copy)
                    else:
                        i = nc.vector.tensor_copy(probT[0][:], turn_b[0][0:nk, :])
                    i.then_inc(s_copied, 1)

                @block.scalar
                def _(act):
                    act.wait_ge(s_low, 1)

                    def slot(bb, j):
                        if not absent(bb, (j - 5) // 4, NB) and (clamp or (j - 5) % 2 == 1):
                            copy_probs(act, bb, j - 5)
                        if not absent(bb, j // 4, NB):
                            b, g, u = at(bb, j)
                            n = bb * 4 + j
                            act.wait_ge(s_shift, n + 1)
                            wait(act, s_turn, n - 7)
                            if clamp:
                                wait(act, s_floor, n - 3)
                                act.activation(floor[:, g, :], shift[:, g, :], ACT.Exp, bias=low[:, 0:1])
                            for h in range(HG):
                                acc = raw[:, bass.ds(n * 4 + h, 1)] if clamp else None
                                i = act.activation(prob[j % 8][:, h, :], score_b[g][:, h * nk:(h + 1) * nk], ACT.Exp,
                                                   bias=shift[:, g, h:h + 1], accum_out=acc)
                            i.then_inc(s_exp, 1)

                    pipeline_b(act, slot, 5)

                @block.vector
                def _(dve):
                    def high_parts(b, u):
                        wait(dve, s_score, b * 4 - 4)
                        keep_high(dve, ks[u][0][:], KT[:, bass.ds(b * nk, nk)])
                        keep_high(dve, qs[u][0][:], QT[:, bass.ds(b * P, P)]).then_inc(s_high, 1)
                    high_parts(0, 0)

                    def slot(bb, j):
                        if not clamp and not absent(bb, (j - 5) // 4, NB) and (j - 5) % 2 == 0:
                            copy_probs(dve, bb, j - 5)
                        if j % 4 == 0 and not absent(bb, j // 4 + 1, NB):
                            high_parts(bb + j // 4 + 1, 1 - (j // 4) % 2)
                        if not absent(bb, j // 4, NB):
                            b, g, u = at(bb, j)
                            n = bb * 4 + j
                            dve.wait_ge(s_score, n + 1)
                            wait(dve, s_exp, n - 3)
                            to = negmax if clamp else shift
                            i = dve.tensor_reduce(to[:, g, :], score_b[g][:, 0:HG * nk].rearrange("p (h k) -> p h k", h=HG),
                                                  AX.X, ALU.max, negate=True)
                            i.then_inc(s_max if clamp else s_shift, 1)
                            if clamp:
                                dve.wait_ge(s_max, n + 1)
                                dve.tensor_scalar(shift[:, g, :], negmax[:, g, :], CLAMP, -CLAMP, ALU.min,
                                                  ALU.max).then_inc(s_shift, 1)
                        if clamp and not absent(bb, (j - 2) // 4, NB):
                            g = (j - 2) % NG
                            dve.wait_ge(s_exp, bb * 4 + j - 1)
                            dve.scalar_tensor_tensor(prob[(j - 2) % 8][:], prob[(j - 2) % 8][:], 1.0,
                                                     floor[:, g, :].unsqueeze(2).broadcast_to([P, HG, nk]),
                                                     ALU.min, ALU.max).then_inc(s_floor, 1)
                        if (j - 7) % 4 == 3 and not absent(bb, (j - 7) // 4, NB):
                            b, g, u = at(bb, j - 7)
                            dve.wait_ge(s_pv, b * 4 + 4)
                            dve.reciprocal(recip[u][:], out_b[u][64:128, 0:2 * P]).then_inc(s_recip, 1)
                            dve.wait_ge(s_recip, b + 1)
                            wait(dve, s_y, b - 1)
                            dve.tensor_tensor(headT[u][:], out_b[u][0:64, 0:2 * P], recip[u][:], ALU.mult).then_inc(s_head, 1)
                        if (j - 9) % 4 == 3 and not absent(bb, (j - 9) // 4, NB):
                            b, g, u = at(bb, j - 9)
                            dve.wait_ge(s_y, b + 1)
                            d = dst[:, bass.ds(b, 1), :].rearrange("p b d -> p (b d)")
                            if clamp:
                                i = dve.tensor_copy(d, out_b[u][:, 2 * P:2 * P + D])
                            else:
                                i = dve.tensor_tensor(d, out_b[u][:, 2 * P:2 * P + D], d, ALU.add)
                            i.then_inc(s_out, 1)

                    pipeline_b(dve, slot, 9)

        def pipeline_b(eng, slot, tail):
            for bb in (0, 2):
                for j in range(8):
                    slot(bb, j)
            with stepped(eng, 4, NB - 2, 2) as bb:
                for j in range(8):
                    slot(bb, j)
            for j in range(8 + tail):
                slot(NB - 2, j)

        def dump():
            s_dump = sem("dumped")
            with nc.Block() as block:
                @block.sync
                def _(sp):
                    sp.dma_start(out.rearrange("b t d -> t b d"), X[:]).then_inc(s_dump, 16)
                    sp.wait_ge(s_dump, 16)

        stats("a_stat", bias=bo0, setup=Setup)
        prep.close()
        assert len(loads) == many_loads
        att = ExitStack()
        Y = sb("a_Y", [P, NB, D], ctx=att)
        cmean = sb("a_cmean", [DC, NB], ctx=att)
        raw = sb("a_raw", [P, NB * H], ctx=att)
        QT = sb("a_QT", [P, NB * P], ctx=att)
        KT = sb("a_KT", [P, NB * NKV], ctx=att)
        V = sb("a_V", [NKV, NB * D], ctx=att)
        own = ExitStack()
        norm = Norm("a", own, bank[0:2])
        cs = [sb(f"a_cs{i}", [DC, 4, NKV], ctx=own) for i in range(2)]
        s_cs = [sem(f"a_ctx_loaded{i}") for i in range(2)]
        q_b, k_b, v_b = bank[2:4], bank[4:6], bank[6:8]
        s_k = sem("a_k_product")
        s_v = sem("a_v_product")
        s_qcopy = sem("a_q_copied")
        s_kcopy = sem("a_k_copied")
        s_vcopy = sem("a_v_copied")
        s_mean = sem("a_context_summed")
        with nc.Block() as block:
            @block.sync
            def _(sp):
                def body(q, u):
                    wait(sp, s_v, q - 1)
                    wait(sp, s_mean, q - 1)
                    sp.dma_start(cs[u][:], ctxT[bass.ds(q * 4, 4)].rearrange("b e t -> e b t")).then_inc(s_cs[u], 16)
                over_quads(sp, body)

            @block.tensor
            def _(pe):
                def body(q, u, ahead):
                    if ahead:
                        norm.turn(pe, q + 1, 1 - u)
                    pe.wait_ge(s_cs[u], (q // 2) * 16 + 16 if isinstance(q, int) else (q - u) * 8 + 16)
                    wait(pe, s_kcopy, q - 1)
                    pe.matmul(k_b[u][:, 0:4 * NKV], small["a_wk"][:], cs[u][:].rearrange("p b t -> p (b t)"),
                              start=True, stop=True).then_inc(s_k, 1)
                    wait(pe, s_vcopy, q - 1)
                    for j in range(4):
                        t = pe.matmul(v_b[u][0:NKV, j * D:(j + 1) * D], cs[u][:, j, :], small["a_wv"][:],
                                      start=True, stop=True)
                    t.then_inc(s_v, 1)
                    pe.wait_ge(norm.s_xs, q + 1)
                    wait(pe, s_qcopy, q - 1)
                    pe.matmul(q_b[u][:], small["a_wq"][:], norm.xs[u][:], start=True, stop=True).then_inc(norm.s_used, 1)
                quads_ahead(pe, lambda: norm.turn(pe, 0, 0), body, 1)

            @block.scalar
            def _(act):
                def body(q, u, ahead):
                    if ahead:
                        norm.copy(act, q + 1, 1 - u)
                    act.wait_ge(norm.s_used, q + 1)
                    act.activation(QT[:, bass.ds(q * 512, 512)], q_b[u][:], ACT.Identity, scale=A_SCALE,
                                   bias=small["a_bq"][:, 0:1]).then_inc(s_qcopy, 1)
                quads_ahead(act, lambda: norm.copy(act, 0, 0), body, 1)

            @block.vector
            def _(dve):
                def before():
                    norm.scale(dve, 0, 0)
                    norm.scale(dve, 1, 1)

                def body(q, u, ahead):
                    dve.wait_ge(s_k, q + 1)
                    dve.tensor_scalar(KT[:, bass.ds(q * 4 * NKV, 4 * NKV)], k_b[u][:, 0:4 * NKV],
                                      small["a_bk"][:, 0:1], None, ALU.add).then_inc(s_kcopy, 1)
                    if ahead == 2:
                        norm.scale(dve, q + 2, u)
                    dve.wait_ge(s_v, q + 1)
                    dve.tensor_tensor(V[:, bass.ds(q * 512, 512)].rearrange("p (b c) -> p b c", b=4),
                                      v_b[u][0:NKV, :].rearrange("p (b c) -> p b c", b=4),
                                      bv0[0:NKV, :].unsqueeze(1).broadcast_to([NKV, 4, D]), ALU.add)\
                        .then_inc(s_vcopy, 1)
                    dve.tensor_reduce(cmean[:, bass.ds(q * 4, 4)], cs[u][:], AX.X, ALU.add).then_inc(s_mean, 1)
                quads_ahead(dve, before, body)
        own.close()

        own = ExitStack()
        attend("a_att", own, QT, KT, V, NKV, a_wo8, raw, Y)
        own.close()

        own = ExitStack()
        odd = sb("odd", [P, NB * H], ctx=own)
        anyodd = sb("anyodd", [P, 1], ctx=own)
        oddmask = sb("oddmask", [P, 1], I32, ctx=own)
        vmeanT = sb("vmeanT", [D, NB], ctx=own)
        s_odd = sem("odd_found")
        s_oddsum = sem("odd_summed")
        s_vm = sem("mean_values")
        s_vmc = sem("mean_values_copied")
        s_flat = sem("uniform_projected")
        s_pick = sem("uniform_picked")
        with nc.Block() as block:
            @block.vector
            def _(dve):
                dve.tensor_tensor(odd[:], raw[:], raw[:], ALU.not_equal).then_inc(s_odd, 1)
                dve.wait_ge(s_odd, 1)
                dve.tensor_reduce(anyodd[:], odd[:], AX.X, ALU.max).then_inc(s_odd, 1)
                dve.wait_ge(s_oddsum, 1)
                dve.tensor_scalar(oddmask[:], bank[0][:, 0:1], 0.0, None, ALU.is_gt).then_inc(s_odd, 1)
                dve.wait_ge(s_odd, 3)
                for q in range(NQ):
                    dve.wait_ge(s_flat, q + 1)
                    dve.copy_predicated(Y[:, 4 * q:4 * q + 4, :].rearrange("p b d -> p (b d)"),
                                        oddmask[:].broadcast_to([P, 512]), bank[2 + q % 2][:]).then_inc(s_pick, 1)
                dve.wait_ge(s_pick, NQ)
                dve.tensor_tensor(X[:], X[:], Y[:], ALU.add)

            @block.scalar
            def _(act):
                act.wait_ge(s_vm, 1)
                act.activation(vmeanT[:], bank[1][:, 0:NB], ACT.Identity, scale=1.0 / NKV,
                               bias=small["a_bvc"][:, 0:1]).then_inc(s_vmc, 1)

            @block.tensor
            def _(pe):
                pe.matmul(bank[1][:, 0:NB], small["a_wv"][:], cmean[:], start=True, stop=True).then_inc(s_vm, 1)
                pe.wait_ge(s_odd, 2)
                pe.matmul(bank[0][:, 0:1], ones[:], anyodd[:], start=True, stop=True).then_inc(s_oddsum, 1)
                pe.wait_ge(s_vmc, 1)
                for q in range(NQ):
                    wait(pe, s_pick, q - 1)
                    for j in range(4):
                        t = pe.matmul(bank[2 + q % 2][:, j * D:(j + 1) * D],
                                      vmeanT[:, 4 * q + j:4 * q + j + 1].broadcast_to([D, P]), small["a_wo"][:],
                                      start=True, stop=True)
                    t.then_inc(s_flat, 1)
        own.close()
        att.close()
        if stop_after == 1:
            return dump()

        def experts(tag, XT, combT, nrows, wg, wu, wd, sel, units, share, start_from_zero, YT):
            own = ExitStack()
            groups = units // 4
            whole = [sb(f"{tag}_w_{k}", [P, 512], ctx=own) for k in ("gate", "up", "down")]
            wgs = [[sb(f"{tag}_wg_{part}{i}", [P, 512], ctx=own) for part in ("high", "low")] for i in range(2)]
            wus = [[sb(f"{tag}_wu_{part}{i}", [P, 512], ctx=own) for part in ("high", "low")] for i in range(2)]
            wds = [[sb(f"{tag}_wd_{part}{i}", [P, 512], ctx=own) for part in ("high", "low")] for i in range(2)]
            sels = [sb(f"{tag}_sel{i}", [nrows, 512], F16, ctx=own) for i in range(2)]
            act_s = [sb(f"{tag}_silu{i}", [P, 512], ctx=own) for i in range(2)]
            gu = [sb(f"{tag}_gu{i}", [P, 512], ctx=own) for i in range(2)]
            hid = [sb(f"{tag}_hid{i}", [P, 512], ctx=own) for i in range(2)]
            hid_high = [sb(f"{tag}_hid_high{i}", [P, 512], ctx=own) for i in range(4)]
            hid_low = [sb(f"{tag}_hid_low{i}", [P, 512], ctx=own) for i in range(4)]
            gate_b, up_b, comb_b, down_b = bank[0:2], bank[2:4], bank[4:6], bank[6:8]
            s_w = [sem(f"{tag}_weights{i}") for i in range(2)]
            s_zero = sem(tag + "_sum_cleared")
            s_g = sem(tag + "_gate")
            s_u = sem(tag + "_up")
            s_c = sem(tag + "_comb")
            s_silu = sem(tag + "_silu_done")
            s_gu = sem(tag + "_gated")
            s_wh = sem(tag + "_weights_high")
            s_wl = sem(tag + "_weights_split")
            s_p = sem(tag + "_hidden_product")
            s_hh = sem(tag + "_hidden_high")
            s_h = sem(tag + "_hidden_split")
            s_d = sem(tag + "_down")
            s_y = sem(tag + "_summed")

            def walk(eng, pair):
                def group(gr, wb, first=False, last=False):
                    pair(gr, 0, wb, None if first else 1 - wb)
                    pair(gr, 2, wb, wb, prepare=not last)
                    with stepped(eng, 4, NQ, 2) as c:
                        pair(gr, c, wb, wb)
                group(0, 0, first=True)
                group(1, 1)
                if groups > 4:
                    with stepped(eng, 2, groups - 2, 2) as gr:
                        group(gr, 0)
                        group(gr + 1, 1)
                group(groups - 2, 0)
                group(groups - 1, 1, last=True)

            def unit(gr, c, k, per=1):
                return gr * (32 // per) + c * (4 // per) + k // per

            with nc.Block() as block:
                @block.sync
                def _(sp):
                    def group(gr, wb):
                        wait(sp, s_d, gr * 32 - 32)
                        if isinstance(gr, int) and gr == 1:
                            sp.wait_ge(s_wl, 3)
                        for dst, src in ((whole[0], wg), (whole[1], wu)):
                            sp.dma_start(dst[:], src[:, bass.ds(gr * 512, 512)]).then_inc(s_w[wb], 16)
                        sp.dma_start(whole[2][:].rearrange("p (u d) -> p u d", u=4),
                                     wd[bass.ds(gr * 512, 512)].rearrange("(u p) d -> p u d", p=P))\
                            .then_inc(s_w[wb], 16)
                        sp.dma_start(sels[wb][:], sel[:, bass.ds(gr * 512, 512)]).then_inc(s_w[wb], 16)
                    group(0, 0)
                    group(1, 1)
                    with stepped(sp, 2, groups, 2) as gr:
                        group(gr, 0)
                        group(gr + 1, 1)

                def high_weights(dve, gr, wb, k):
                    if k == 0:
                        dve.wait_ge(s_w[wb], (gr - wb) * 32 + 64)
                        wait(dve, s_d, gr * 32 - 32)
                    keep_high(dve, (wgs, wus, wds)[k][wb][0][:], whole[k][:]).then_inc(s_wh, 1)

                def low_weights(pool, gr, wb, k):
                    t = (wgs, wus, wds)[k][wb]
                    pool.wait_ge(s_wh, gr * 3 + k + 1)
                    keep_low(pool, t[1][:], whole[k][:], t[0][:]).then_inc(s_wl, 1)

                @block.gpsimd
                def _(pool):
                    for k in range(3):
                        low_weights(pool, 0, 0, k)
                    if start_from_zero:
                        pool.memset(YT[:], 0.0).then_inc(s_zero, 1)

                    def pair(gr, c, wb, before, prepare=False):
                        for j in range(8):
                            n = unit(gr, c, j)
                            pool.wait_ge(s_hh, n + 1)
                            wait(pool, s_d, n - 3)
                            keep_low(pool, hid_low[j % 4][:], hid[j % 2][:], hid_high[j % 4][:]).then_inc(s_h, 1)
                            if prepare and j % 2 == 1 and j < 6:
                                low_weights(pool, gr + 1, 1 - wb, j // 2)
                    walk(pool, pair)

                @block.tensor
                def _(pe):
                    def down(gr, c, k, wb):
                        n = unit(gr, c, k)
                        u = k % 4
                        pe.wait_ge(s_h, n + 1)
                        if u == 0:
                            i = gr * 8 + c + k // 4
                            wait(pe, s_y, i - 1)
                        split_product(pe, down_b[(k // 4) % 2][:], [t[:, u * D:(u + 1) * D] for t in wds[wb]],
                                      (hid_high[k % 4][:], hid_low[k % 4][:]), start=(u == 0),
                                      stop=(u == 3)).then_inc(s_d, 1)

                    def pair(gr, c, wb, before, prepare=False):
                        for j in range(8):
                            n = unit(gr, c, j)
                            u = j % 4
                            x_parts = [t[:, bass.ds((c + j // 4) * 512, 512)] for t in XT]
                            if j == 0 and isinstance(c, int) and c == 0:
                                pe.wait_ge(s_w[wb], (gr - wb) * 32 + 64)
                                pe.wait_ge(s_wl, gr * 3 + 3)
                            wait(pe, s_silu, n - 1)
                            split_product(pe, gate_b[j % 2][:], [t[:, u * P:(u + 1) * P] for t in wgs[wb]],
                                          x_parts).then_inc(s_g, 1)
                            wait(pe, s_gu, n - 1)
                            split_product(pe, up_b[j % 2][:], [t[:, u * P:(u + 1) * P] for t in wus[wb]],
                                          x_parts).then_inc(s_u, 1)
                            if j % share == 0:
                                wait(pe, s_p, n - share)
                                pe.matmul(comb_b[(j // share) % 2][:], sels[wb][:, u * P:(u + 1) * P],
                                          combT[:, bass.ds((c + j // 4) * 512, 512)],
                                          start=True, stop=True).then_inc(s_c, 1)
                            if j >= 2:
                                down(gr, c, j - 2, wb)
                            elif before is not None:
                                down(gr, c, j - 2, before)
                    walk(pe, pair)
                    for k in (6, 7):
                        down(groups - 1, NQ - 2, k, 1)

                @block.scalar
                def _(act):
                    def pair(gr, c, wb, before, prepare=False):
                        for j in range(8):
                            n = unit(gr, c, j)
                            act.wait_ge(s_g, n + 1)
                            wait(act, s_gu, n - 1)
                            act.activation(act_s[j % 2][:], gate_b[j % 2][:], ACT.Silu).then_inc(s_silu, 1)
                    walk(act, pair)

                @block.vector
                def _(dve):
                    def add(gr, c, k):
                        n = unit(gr, c, k)
                        cc = c + k // 4
                        if isinstance(cc, int) and cc < 0:
                            cc += NQ
                        dve.wait_ge(s_d, n + 1)
                        y = YT[:, bass.ds(cc * 512, 512)]
                        dve.tensor_tensor(y, down_b[(k // 4) % 2][:], y, ALU.add).then_inc(s_y, 1)

                    def pair(gr, c, wb, before, prepare=False):
                        for j in range(8):
                            n = unit(gr, c, j)
                            dve.wait_ge(s_u, n + 1)
                            dve.wait_ge(s_silu, n + 1)
                            wait(dve, s_p, n - 1)
                            dve.tensor_tensor(gu[j % 2][:], up_b[j % 2][:], act_s[j % 2][:], ALU.mult).then_inc(s_gu, 1)
                            dve.wait_ge(s_gu, n + 1)
                            dve.wait_ge(s_c, unit(gr, c, j, share) + 1)
                            wait(dve, s_h, n - 1)
                            dve.tensor_tensor(hid[j % 2][:], comb_b[(j // share) % 2][:], gu[j % 2][:], ALU.mult).then_inc(s_p, 1)
                            dve.wait_ge(s_p, n + 1)
                            wait(dve, s_d, n - 3)
                            keep_high(dve, hid_high[j % 4][:], hid[j % 2][:]).then_inc(s_hh, 1)
                            if prepare and j % 2 == 1 and j < 6:
                                high_weights(dve, gr + 1, 1 - wb, j // 2)
                            if (j - 3) % 4 == 3 and (j >= 3 or before is not None):
                                add(gr, c, j - 3)
                    for k in range(3):
                        high_weights(dve, 0, 0, k)
                    if start_from_zero:
                        dve.wait_ge(s_zero, 1)
                    walk(dve, pair)
                    add(groups - 1, NQ - 2, 7)
            own.close()

        def add_experts(tag, YT, gate, store):
            own = ExitStack()
            ys = [sb(f"{tag}_ys{i}", [P, 512], ctx=own) for i in range(2)]
            s_ys = sem(tag + "_placed")
            s_t = sem(tag + "_turned")
            s_x = sem(tag + "_added")
            s_st = sem(tag + "_stored")
            with nc.Block() as block:
                @block.scalar
                def _(act):
                    def body(q, u):
                        wait(act, s_t, q - 1)
                        act.activation(ys[u][:], YT[:, bass.ds(q * 512, 512)], ACT.Copy,
                                       scale=gate).then_inc(s_ys, 1)
                    over_quads(act, body)

                @block.tensor
                def _(pe):
                    def body(q, u):
                        pe.wait_ge(s_ys, q + 1)
                        wait(pe, s_x, q - 1)
                        for j in range(4):
                            t = pe.transpose(bank[u][:, j * P:(j + 1) * P], ys[u][:, j * P:(j + 1) * P], ident[:])
                        t.then_inc(s_t, 1)
                    over_quads(pe, body)

                @block.vector
                def _(dve):
                    def body(q, u):
                        dve.wait_ge(s_t, q + 1)
                        d = X[:, bass.ds(q * 4, 4), :].rearrange("p b d -> p (b d)")
                        dve.tensor_tensor(d, bank[u][:], d, ALU.add).then_inc(s_x, 1)
                    over_quads(dve, body)

                if store:
                    @block.sync
                    def _(sp):
                        def body(q, u):
                            sp.wait_ge(s_x, q + 1)
                            sp.dma_start(out[bass.ds(q * 4, 4)].rearrange("b t d -> t b d"),
                                         X[:, bass.ds(q * 4, 4), :]).then_inc(s_st, 16)
                        over_quads(sp, body)
                        sp.wait_ge(s_st, 16 * NQ)
            own.close()

        BIG = 1e30

        def pad_top(pool, t, first, total, last_sem):
            for k in range(first, total):
                i = pool.memset(t[:, :, k:k + 1], BIG * (k - first + 1))
            i.then_inc(last_sem, 1)

        def route(tag, ctx, XT, combT, norm, gateT, ne, logits_to_scores, keep_store):
            s_logit = sem(tag + "_logits")
            s_xhigh = sem(tag + "_xt_high")
            s_xt = sem(tag + "_xt_stored")
            s_cb = sem(tag + "_comb_halves")
            s_ct = sem(tag + "_comb_turned")
            s_cc = sem(tag + "_comb_copied")
            cb = [sb(f"{tag}_cb{i}", [P, 4, P], F16, ctx=ctx) for i in range(2)]
            cbank = [bank[4 + i][:].bitcast(F16)[:, 0:512] for i in range(2)]
            s_cb0 = sem(tag + "_comb_padded")
            router_b = bank[2:4]

            def finish_comb(dve, chain, comb, q, u):
                wait(dve, s_ct, q - 1)
                chain(dve.tensor_copy(cb[u][:, :, 0:ne], comb))
                dve.tensor_tensor(cb[u][:, :, ne:2 * ne], comb, cb[u][:, :, 0:ne], ALU.subtract).then_inc(s_cb, 1)

            with nc.Block() as block:
                dve_scores, act_scores, pool_setup = logits_to_scores(router_b, s_logit, finish_comb)

                @block.gpsimd
                def _(pool):
                    pool_setup(pool)
                    for u in range(2):
                        i = pool.memset(cb[u][:], 0.0)
                    i.then_inc(s_cb0, 1)

                    def body(q, u):
                        pool.wait_ge(s_xhigh, q + 1)
                        chunk = bass.ds(q * 512, 512)
                        keep_low(pool, XT[1][:, chunk], norm.xs[u][:], XT[0][:, chunk]).then_inc(s_xt, 1)
                    over_quads(pool, body)

                @block.tensor
                def _(pe):
                    def router(q, u):
                        norm.turn(pe, q, u)
                        pe.wait_ge(norm.s_xs, q + 1)
                        wait(pe, s_cb, q - 1)
                        for j in range(4):
                            t = pe.matmul(router_b[u][:, j * ne:(j + 1) * ne], norm.xs[u][:, j * P:(j + 1) * P], gateT[:],
                                          start=True, stop=True)
                        t.then_inc(s_logit, 1)

                    def turn_comb(q, u):
                        pe.wait_ge(s_cb, q + 1)
                        wait(pe, s_cc, q - 1)
                        for j in range(4):
                            t = pe.transpose(cbank[u][:, j * P:(j + 1) * P], cb[u][:, j, :], identh[:])
                        t.then_inc(s_ct, 1)

                    def body(q, u, ahead):
                        if ahead:
                            router(q + 1, 1 - u)
                        turn_comb(q, u)
                    quads_ahead(pe, lambda: router(0, 0), body, 1)

                @block.scalar
                def _(act):
                    def body(q, u):
                        act.wait_ge(norm.s_turned, q + 1)
                        wait(act, s_xt, q - 1)
                        wait(act, s_logit, q - 1)
                        kw = {} if norm.gain is None else {"scale": norm.gain[:, 0:1]}
                        act.activation(norm.xs[u][:], norm.banks[u][:], ACT.Copy, **kw).then_inc(norm.s_xs, 1)
                        act_scores(act, q, u)
                    over_quads(act, body)

                @block.vector
                def _(dve):
                    def high(q, u):
                        dve.wait_ge(norm.s_xs, q + 1)
                        keep_high(dve, XT[0][:, bass.ds(q * 512, 512)], norm.xs[u][:]).then_inc(s_xhigh, 1)

                    def store_comb(q, u):
                        dve.wait_ge(s_ct, q + 1)
                        dve.tensor_copy(combT[:, bass.ds(q * 512, 512)], cbank[u]).then_inc(s_cc, 1)

                    def before():
                        dve.wait_ge(s_cb0, 1)
                        norm.scale(dve, 0, 0)
                        norm.scale(dve, 1, 1)
                        high(0, 0)

                    def body(q, u, ahead):
                        if ahead == 2:
                            norm.scale(dve, q + 2, u)
                        dve_scores(dve, q, u)
                        if not (isinstance(q, int) and q == 0):
                            store_comb(q - 1, 1 - u)
                        if ahead:
                            high(q + 1, 1 - u)
                    quads_ahead(dve, before, body)
                    store_comb(NQ - 1, 1)

        token = sb("token", [P, 1])

        class Chain:

            def __init__(self, eng, s, start):
                self.eng, self.s, self.n = eng, s, start

            def carried(self, i):
                self(i)
                self.eng.memset(token[:], 0.0)

            def __call__(self, i):
                i.then_inc(self.s, 1)
                self.n = self.n + 1
                self.eng.wait_ge(self.s, self.n)

        stats("b_stat")
        moe = ExitStack()
        XT = [sb(f"b_XT_{part}", [P, NB * P], ctx=moe) for part in ("high", "low")]
        YT = sb("b_YT", [P, NB * P], ctx=moe)
        combT = sb("b_combT", [P, NB * P], F16, ctx=moe)
        own = ExitStack()
        norm = Norm("b", own, bank[0:2])
        G0 = 8
        sig = [sb(f"b_sig{i}", [P, 4, E0], ctx=own) for i in range(2)]
        sc = sb("b_sc", [P, 4, E0], ctx=own)
        gs = sb("b_gs", [P, 4, G0 + 4], ctx=own)
        gr_ = sb("b_gr", [P, 4, G0 + 4], ctx=own)
        g8 = sb("b_g8", [P, 4, 8], ctx=own)
        ms = sb("b_ms", [P, 4, E0 + 2], ctx=own)
        mr = sb("b_mr", [P, 4, E0 + 2], ctx=own)
        m8 = sb("b_m8", [P, 4, 8], ctx=own)
        cw = sb("b_cw", [P, 4, E0], ctx=own)
        ssum = sb("b_ssum", [P, 4], ctx=own)
        s_sig = sem("b_sigmoid")
        s_bv = sem("b_route_steps")
        s_pad = sem("b_padded")
        B_STEPS = 13

        def b_scores(router_b, s_logit, finish_comb):
            def dve_scores(dve, q, u):
                chain = Chain(dve, s_bv, q * B_STEPS)
                if isinstance(q, int) and q == 0:
                    dve.wait_ge(s_pad, 2)
                dve.wait_ge(s_sig, q + 1)
                chain(dve.tensor_tensor(sc[:], sig[u][:], gb0[:].unsqueeze(1).broadcast_to([P, 4, E0]), ALU.add))
                chain.carried(dve.tensor_reduce(gs[:, :, 0:G0], sc[:].rearrange("p j (g e) -> p j g e", g=G0), AX.X, ALU.max))
                for j in range(4):
                    i = dve.max(g8[:, j, :], gs[:, j, :])
                chain.carried(i)
                for j in range(4):
                    i = dve.match_replace(gr_[:, j, :], g8[:, j, :], gs[:, j, :], -BIG)
                chain(i)
                chain(dve.tensor_tensor(gr_[:, :, 0:G0], gr_[:, :, 0:G0], gs[:, :, 0:G0], ALU.not_equal))
                chain.carried(dve.tensor_tensor(ms[:, :, 0:E0].rearrange("p j (g e) -> p j g e", g=G0),
                                        sc[:].rearrange("p j (g e) -> p j g e", g=G0),
                                        gr_[:, :, 0:G0].unsqueeze(3).broadcast_to([P, 4, G0, E0 // G0]), ALU.mult))
                for j in range(4):
                    i = dve.max(m8[:, j, :], ms[:, j, :])
                chain.carried(i)
                for j in range(4):
                    i = dve.match_replace(mr[:, j, :], m8[:, j, :], ms[:, j, :], -BIG)
                chain(i)
                chain(dve.tensor_tensor(cw[:], mr[:, :, 0:E0], ms[:, :, 0:E0], ALU.not_equal))
                chain(dve.tensor_tensor(cw[:], cw[:], ms[:, :, 0:E0], ALU.mult))
                chain(dve.tensor_reduce(ssum[:], cw[:], AX.X, ALU.add))
                chain(dve.tensor_scalar(ssum[:], ssum[:], 1e-8, 1.0 / COMB_UP, ALU.add, ALU.mult))
                dve.reciprocal(ssum[:], ssum[:]).then_inc(s_rc, 1)
                dve.wait_ge(s_rc, q + 1)
                dve.tensor_tensor(cw[:], cw[:], ssum[:].unsqueeze(2).broadcast_to([P, 4, E0]), ALU.mult).then_inc(s_cwd, 1)
                dve.wait_ge(s_cwd, q + 1)
                finish_comb(dve, chain, cw[:], q, u)

            def act_scores(act, q, u):
                act.wait_ge(s_logit, q + 1)
                wait(act, s_bv, (q - 2) * B_STEPS + 1)
                act.activation(sig[u][:].rearrange("p j e -> p (j e)"), router_b[u][:, 0:4 * E0],
                               ACT.Sigmoid).then_inc(s_sig, 1)

            def pool_setup(pool):
                pad_top(pool, gs, G0, G0 + 4, s_pad)
                pad_top(pool, ms, E0, E0 + 2, s_pad)
            return dve_scores, act_scores, pool_setup

        s_rc = sem("b_recip")
        s_cwd = sem("b_weights_ready")
        route("b_route", own, XT, combT, norm, small["a_gate"], E0, b_scores, None)
        own.close()

        own = ExitStack()
        s_silu_t = [sb(f"sh_silu{i}", [P, 512], ctx=own) for i in range(2)]
        s_hid = [sb(f"sh_hid{i}", [P, 512], ctx=own) for i in range(2)]
        s_hid_high = [sb(f"sh_hid_high{i}", [P, 512], ctx=own) for i in range(2)]
        s_hid_low = [sb(f"sh_hid_low{i}", [P, 512], ctx=own) for i in range(2)]
        sh_w = [[sb(f"sh_w{i}_{part}", [P, P], ctx=own) for part in ("high", "low")] for i in range(3)]
        s_swh = sem("sh_weights_high")
        s_swl = sem("sh_weights_split")
        s_shp = sem("sh_product")
        s_shhh = sem("sh_hidden_high")
        s_sg = sem("sh_gate_up")
        s_ss = sem("sh_silu_done")
        s_shh = sem("sh_hidden")
        s_sd = sem("sh_down")
        s_sy = sem("sh_copied")
        with nc.Block() as block:
            @block.gpsimd
            def _(pool):
                for k, name in enumerate(("sgT", "suT", "sdT")):
                    pool.wait_ge(s_swh, k + 1)
                    keep_low(pool, sh_w[k][1][:], small[name][:], sh_w[k][0][:]).then_inc(s_swl, 1)

                def body(q, u):
                    pool.wait_ge(s_shhh, q + 1)
                    wait(pool, s_sd, q - 1)
                    keep_low(pool, s_hid_low[u][:], s_hid[u][:], s_hid_high[u][:]).then_inc(s_shh, 1)
                over_quads(pool, body)

            @block.tensor
            def _(pe):
                def first(q, u):
                    wait(pe, s_shp, q - 1)
                    x_parts = [t[:, bass.ds(q * 512, 512)] for t in XT]
                    split_product(pe, bank[u][:], [t[:] for t in sh_w[0]], x_parts)
                    split_product(pe, bank[2 + u][:], [t[:] for t in sh_w[1]], x_parts).then_inc(s_sg, 1)

                def second(q, u):
                    pe.wait_ge(s_shh, q + 1)
                    wait(pe, s_sy, q - 1)
                    split_product(pe, bank[4 + u][:], [t[:] for t in sh_w[2]],
                                  (s_hid_high[u][:], s_hid_low[u][:])).then_inc(s_sd, 1)

                pe.wait_ge(s_swl, 3)
                first(0, 0)
                first(1, 1)
                first(2, 0)
                second(0, 0)
                first(3, 1)
                second(1, 1)
                with stepped(pe, 4, NQ, 2) as q:
                    first(q, 0)
                    second(q - 2, 0)
                    first(q + 1, 1)
                    second(q - 1, 1)
                second(NQ - 2, 0)
                second(NQ - 1, 1)

            @block.scalar
            def _(act):
                def body(q, u):
                    act.wait_ge(s_sg, q + 1)
                    wait(act, s_shp, q - 1)
                    act.activation(s_silu_t[u][:], bank[u][:], ACT.Silu).then_inc(s_ss, 1)
                over_quads(act, body)

            @block.vector
            def _(dve):
                for k, name in enumerate(("sgT", "suT", "sdT")):
                    keep_high(dve, sh_w[k][0][:], small[name][:]).then_inc(s_swh, 1)

                def body(q, u):
                    dve.wait_ge(s_ss, q + 1)
                    wait(dve, s_shh, q - 1)
                    dve.tensor_tensor(s_hid[u][:], bank[2 + u][:], s_silu_t[u][:], ALU.mult).then_inc(s_shp, 1)
                    dve.wait_ge(s_shp, q + 1)
                    wait(dve, s_sd, q - 1)
                    keep_high(dve, s_hid_high[u][:], s_hid[u][:]).then_inc(s_shhh, 1)

                def store(q, u):
                    dve.wait_ge(s_sd, q + 1)
                    dve.tensor_copy(YT[:, bass.ds(q * 512, 512)], bank[4 + u][:]).then_inc(s_sy, 1)

                body(0, 0)
                body(1, 1)
                with stepped(dve, 2, NQ, 2) as q:
                    body(q, 0)
                    store(q - 2, 0)
                    body(q + 1, 1)
                    store(q - 1, 1)
                store(NQ - 2, 0)
                store(NQ - 1, 1)
        own.close()
        experts("b_moe", XT, combT, P, w["b_wgT"], w["b_wuT"], w["b_wdT"], consts["sel0"], E0 * I0 // P, 1, False, YT)
        add_experts("b_add", YT, tg[:, 2:3], False)
        moe.close()
        renew_semaphores()
        if stop_after == 2:
            return dump()

        stats("c_stat", bias=bo1)
        att = ExitStack()
        XT = [sb(f"c_XT_{part}", [P, NB * P], ctx=att) for part in ("high", "low")]
        own = ExitStack()
        norm = Norm("cn", own, bank[0:2])
        s_xhigh = sem("cn_high")
        with nc.Block() as block:
            @block.tensor
            def _(pe):
                over_quads(pe, lambda q, u: norm.turn(pe, q, u))

            @block.scalar
            def _(act):
                def body(q, u):
                    act.wait_ge(norm.s_turned, q + 1)
                    act.activation(XT[0][:, bass.ds(q * 512, 512)].bitcast(F32R), bank[u][:], ACT.Copy).then_inc(s_xhigh, 1)
                over_quads(act, body)

            @block.vector
            def _(dve):
                def low(q, u):
                    dve.wait_ge(s_xhigh, q + 1)
                    chunk = bass.ds(q * 512, 512)
                    keep_low(dve, XT[1][:, chunk], bank[u][:], XT[0][:, chunk]).then_inc(norm.s_xs, 1)
                norm.scale(dve, 0, 0)
                norm.scale(dve, 1, 1)
                low(0, 0)
                with stepped(dve, 2, NQ, 2) as q:
                    norm.scale(dve, q, 0)
                    low(q - 1, 1)
                    norm.scale(dve, q + 1, 1)
                    low(q, 0)
                low(NQ - 1, 1)
        own.close()

        own = ExitStack()

        def parts(name, shape, count=None):
            if count is None:
                return [sb(f"{name}_{part}", shape, ctx=own) for part in ("high", "low")]
            return [parts(f"{name}{i}", shape) for i in range(count)]

        wvp = parts("c_wvp", [DC, H * C_DH])
        cs = [sb(f"c_cs{i}", [DC, NKV], ctx=own) for i in range(2)]
        csp = parts("c_csp", [DC, NKV], 2)
        xs = parts("c_xs", [P, P], 2)
        ts = parts("c_ts", [P, HG * NKV], 2)
        vs = [sb(f"c_vs{i}", [NKV, H, P], ctx=own) for i in range(2)]
        prob = [sb(f"c_prob{i}", [P, HG, NKV], ctx=own) for i in range(8)]
        probT = [sb(f"c_probT{i}", [NKV, HG * P], ctx=own) for i in range(2)]
        shift = sb("c_shift", [P, 8, HG], ctx=own)
        sums = sb("c_sums", [P, 8, HG], ctx=own)
        recip = sb("c_recip", [P, 8, HG], ctx=own)
        oT = [sb(f"c_oT{i}", [P, 8, P], ctx=own) for i in range(2)]
        key_b, side_b, score_b, turn_b, out_b = bank[0], bank[1], bank[2:4], bank[4:6], bank[6:8]
        s_cs = [sem(f"c_ctx_loaded{i}") for i in range(2)]
        s_wh = sem("c_weights_high")
        s_wl = sem("c_weights_split")
        s_ch = sem("c_ctx_high")
        s_cl = sem("c_ctx_split")
        s_xs = sem("c_xs_placed")
        s_key = sem("c_keys")
        s_kh = sem("c_keys_high")
        s_kcopy = sem("c_keys_split")
        s_score = sem("c_scores")
        s_shift = sem("c_shift_ready")
        s_exp = sem("c_exp")
        s_recip = sem("c_recip_ready")
        s_norm = sem("c_probs_normed")
        s_turn = sem("c_probs_turned")
        s_copied = sem("c_probs_copied")
        s_v = sem("c_values")
        s_vcopy = sem("c_values_copied")
        s_vzero = sem("c_values_cleared")
        s_pv = sem("c_pv")
        s_ocopy = sem("c_heads_copied")
        s_y = sem("c_projected")
        s_add = sem("c_added")

        def at(bb, k):
            return bb + k // NG, k % NG, (k // NG) % 2

        def here(bb, k):
            return not absent(bb, k // 4, NB)

        def value_columns(t, half):
            first = t[:].rearrange("p h c -> p (h c)")[:, half * 8 * P:half * 8 * P + C_DH]
            first = first.unsqueeze(1).unsqueeze(1)
            return bass.AP(first.tensor, first.offset, [list(first.ap[0]), [2 * P, 4], [P + C_DH, 2], [1, C_DH]])

        with nc.Block() as block:
            @block.sync
            def _(sp):
                def body(b, u):
                    wait(sp, s_cl, b - 1)
                    wait(sp, s_key, b * 4 - 4)
                    sp.dma_start(cs[u][:], ctxT[b] if isinstance(b, int) else
                                 ctxT[bass.ds(b, 1)].rearrange("b e t -> e (b t)")).then_inc(s_cs[u], 16)
                body(0, 0)
                body(1, 1)
                with stepped(sp, 2, NB, 2) as b:
                    body(b, 0)
                    body(b + 1, 1)

            @block.gpsimd
            def _(pool):
                pool.wait_ge(s_wh, 1)
                keep_low(pool, wvp[1][:], small["c_wv"][:], wvp[0][:]).then_inc(s_wl, 1)
                for u in range(2):
                    i = pool.memset(vs[u][:], 0.0)
                i.then_inc(s_vzero, 1)

                def place_tokens(b, u):
                    wait(pool, s_score, b * 4 - 4)
                    for part in range(2):
                        i = pool.tensor_copy(xs[u][part][:].bitcast(F32R), XT[part][:, bass.ds(b * P, P)])
                    i.then_inc(s_xs, 1)

                def low_context(b, u):
                    pool.wait_ge(s_ch, b + 1)
                    keep_low(pool, csp[u][1][:], cs[u][:], csp[u][0][:]).then_inc(s_cl, 1)

                low_context(0, 0)
                place_tokens(0, 0)

                def slot(bb, j):
                    if here(bb, j - 3):
                        n = bb * 4 + (j - 3)
                        k = (j - 3) % 8
                        pool.wait_ge(s_recip, n + 1)
                        pool.tensor_tensor(prob[k][:], prob[k][:],
                                           recip[:, k, :].unsqueeze(2).broadcast_to([P, HG, NKV]),
                                           ALU.mult).then_inc(s_norm, 1)
                    if j % 4 == 2 and here(bb, j + 4):
                        b, g, u = at(bb, j + 4)
                        low_context(b, u)
                        place_tokens(b, u)
                pipeline_b(pool, slot, 3)

            @block.tensor
            def _(pe):
                pe.wait_ge(s_wl, 1)

                def values(b, u, half):
                    wait(pe, s_vcopy, b * 2 + half)
                    if half == 0:
                        pe.wait_ge(s_cl, b + 1)
                    else:
                        wait(pe, s_add, b - 2)
                    split_product(pe, side_b[0:NKV, :], [t[:] for t in csp[u]],
                                  [t[:, half * 512:(half + 1) * 512] for t in wvp]).then_inc(s_v, 1)

                def slot(bb, j):
                    if here(bb, j):
                        b, g, u = at(bb, j)
                        n = bb * 4 + j
                        if g == 0:
                            pe.wait_ge(s_cs[u], (b - u) * 8 + 16)
                        wait(pe, s_kcopy, n)
                        for h in range(HG):
                            t = pe.matmul(key_b[:, h * NKV:(h + 1) * NKV], mT[:, g * HG + h, :], cs[u][:],
                                          start=True, stop=True)
                        t.then_inc(s_key, 1)
                    if here(bb, j - 1):
                        b, g, u = at(bb, j - 1)
                        n = bb * 4 + (j - 1)
                        if g == 0:
                            pe.wait_ge(s_xs, b + 1)
                        pe.wait_ge(s_kcopy, n + 1)
                        wait(pe, s_exp, n - 1)
                        split_product(pe, score_b[g % 2][:, 0:HG * NKV], [t[:] for t in xs[u]],
                                      [t[:] for t in ts[g % 2]]).then_inc(s_score, 1)
                    if here(bb, j - 5):
                        b, g, u = at(bb, j - 5)
                        n = bb * 4 + (j - 5)
                        pe.wait_ge(s_norm, n + 1)
                        wait(pe, s_copied, n - 1)
                        for h in range(HG):
                            t = pe.transpose(turn_b[g % 2][0:NKV, h * P:(h + 1) * P], prob[(j - 5) % 8][:, h, :],
                                             ident[:])
                        t.then_inc(s_turn, 1)
                    if here(bb, j - 7):
                        b, g, u = at(bb, j - 7)
                        n = bb * 4 + (j - 7)
                        half = g // 2
                        pe.wait_ge(s_copied, n + 1)
                        if g % 2 == 0:
                            pe.wait_ge(s_vcopy, b * 2 + 1 + half)
                            wait(pe, s_ocopy, b * 2 - 1 + half)
                        for h in range(HG):
                            pair = (g % 2) * 2 + h // 2
                            t = pe.matmul(out_b[half][:, pair * P:(pair + 1) * P], vs[u][:, g * HG + h, :],
                                          probT[g % 2][:, h * P:(h + 1) * P], start=(h % 2 == 0), stop=(h % 2 == 1))
                        t.then_inc(s_pv, 1)
                    if j % 4 in (0, 3) and here(bb, j):
                        b, g, u = at(bb, j)
                        values(b, u, g // 2)
                    if (j - 10) % 4 == 3 and here(bb, j - 10):
                        b, g, u = at(bb, j - 10)
                        pe.wait_ge(s_ocopy, b * 2 + 2)
                        if isinstance(b, int) and b >= NB - 3:
                            pe.wait_ge(s_vcopy, NB * 2)
                            if b > NB - 3:
                                pe.wait_ge(s_add, b)
                        else:
                            pe.wait_ge(s_vcopy, b * 2 + 7)
                        for k in range(8):
                            t = pe.matmul(side_b[:, 0:D], oT[u][:, k, :], c_wo[:, k, :], start=(k == 0), stop=(k == 7))
                        t.then_inc(s_y, 1)
                pipeline_b(pe, slot, 10)

            @block.scalar
            def _(act):
                act.wait_ge(s_vzero, 1)

                def slot(bb, j):
                    if j % 4 in (0, 1) and here(bb, j - 1):
                        b, g, u = at(bb, j - 1)
                        half = g // 2
                        act.wait_ge(s_v, b * 2 + 1 + half)
                        wait(act, s_pv, b * 4 - 6 + 2 * half)
                        act.activation(value_columns(vs[u], half),
                                       side_b[0:NKV, :].rearrange("p (r s v) -> p r s v", r=4, s=2),
                                       ACT.Copy).then_inc(s_vcopy, 1)
                    if here(bb, j - 6):
                        b, g, u = at(bb, j - 6)
                        n = bb * 4 + (j - 6)
                        act.wait_ge(s_turn, n + 1)
                        wait(act, s_pv, n - 1)
                        act.activation(probT[g % 2][:], turn_b[g % 2][0:NKV, :], ACT.Copy).then_inc(s_copied, 1)
                    if here(bb, j - 1):
                        b, g, u = at(bb, j - 1)
                        n = bb * 4 + (j - 1)
                        k = (j - 1) % 8
                        act.wait_ge(s_shift, n + 1)
                        wait(act, s_turn, n - 7)
                        for h in range(HG):
                            i = act.activation(prob[k][:, h, :], score_b[g % 2][:, h * NKV:(h + 1) * NKV], ACT.Exp,
                                               bias=shift[:, k, h:h + 1], accum_out=sums[:, k, h:h + 1])
                        i.then_inc(s_exp, 1)
                pipeline_b(act, slot, 6)

            @block.vector
            def _(dve):
                keep_high(dve, wvp[0][:], small["c_wv"][:]).then_inc(s_wh, 1)

                def high_context(b, u):
                    dve.wait_ge(s_cs[u], (b - u) * 8 + 16)
                    wait(dve, s_v, b * 2 - 2)
                    keep_high(dve, csp[u][0][:], cs[u][:]).then_inc(s_ch, 1)
                high_context(0, 0)

                def slot(bb, j):
                    if here(bb, j):
                        b, g, u = at(bb, j)
                        n = bb * 4 + j
                        dve.wait_ge(s_key, n + 1)
                        wait(dve, s_score, n - 1)
                        keep_high(dve, ts[g % 2][0][:], key_b[:, 0:HG * NKV]).then_inc(s_kh, 1)
                        dve.wait_ge(s_kh, n + 1)
                        keep_low(dve, ts[g % 2][1][:], key_b[:, 0:HG * NKV], ts[g % 2][0][:]).then_inc(s_kcopy, 1)
                    if (j - 11) % 4 == 3 and here(bb, j - 11):
                        b, g, u = at(bb, j - 11)
                        dve.wait_ge(s_y, b + 1)
                        d = X[:, bass.ds(b, 1), :].rearrange("p b d -> p (b d)")
                        dve.tensor_tensor(d, side_b[:, 0:D], d, ALU.add).then_inc(s_add, 1)
                    if here(bb, j - 1):
                        b, g, u = at(bb, j - 1)
                        n = bb * 4 + (j - 1)
                        dve.wait_ge(s_score, n + 1)
                        wait(dve, s_exp, n - 7)
                        dve.tensor_reduce(shift[:, (j - 1) % 8, :],
                                          score_b[g % 2][:, 0:HG * NKV].rearrange("p (h k) -> p h k", h=HG),
                                          AX.X, ALU.max, negate=True).then_inc(s_shift, 1)
                    if here(bb, j - 3):
                        n = bb * 4 + (j - 3)
                        k = (j - 3) % 8
                        dve.wait_ge(s_exp, n + 1)
                        wait(dve, s_norm, n - 7)
                        dve.reciprocal(recip[:, k, :], sums[:, k, :]).then_inc(s_recip, 1)
                    if (j - 8) % 2 == 1 and here(bb, j - 8):
                        b, g, u = at(bb, j - 8)
                        half = g // 2
                        dve.wait_ge(s_pv, b * 4 + 2 + 2 * half)
                        wait(dve, s_y, b - 1)
                        dve.tensor_copy(oT[u][:, half * 4:half * 4 + 4, :].rearrange("p k t -> p (k t)"),
                                        out_b[half][:]).then_inc(s_ocopy, 1)
                    if j % 4 == 2 and here(bb, j + 4):
                        b, g, u = at(bb, j + 4)
                        high_context(b, u)
                pipeline_b(dve, slot, 11)
        own.close()
        att.close()
        if stop_after == 3:
            return dump()

        stats("d_stat", second=True)
        Z = XC
        att = ExitStack()
        QT = sb("d_QT", [P, NB * P], ctx=att)
        KT = sb("d_KT", [P, NB * P], ctx=att)
        V = sb("d_V", [P, NB * P], ctx=att)
        own = ExitStack()
        norm = Norm("d", own, bank[0:2], gain=small["g1"])
        wrot = sb("d_wrot", [LAT, 4, P], ctx=own)
        lat = [sb(f"d_lat{i}", [LAT, 512], ctx=own) for i in range(2)]
        part = [sb(f"d_part{i}", [P, 4, 512], ctx=own) for i in range(2)]
        s_wrot = sem("d_wrot_ready")
        s_v0 = sem("d_values_cleared")
        s_latp = sem("d_latent")
        s_lat = sem("d_latent_copied")
        s_rot = sem("d_rope_products")
        s_part = sem("d_rope_parts")
        s_sum = sem("d_rope_summed")
        s_v = sem("d_values")
        s_vcopy = sem("d_values_copied")
        with nc.Block() as block:
            @block.gpsimd
            def _(pool):
                pool.memset(wrot[:], 0.0).then_inc(s_wrot, 1)
                pool.wait_ge(s_wrot, 1)
                for k, name in enumerate(("d_q", "d_k")):
                    src = small[name][:].rearrange("p (h i two) -> p h i two", h=H, two=2)
                    dst = wrot[:, 2 * k, :].rearrange("p (h i two) -> p h i two", h=H, two=2)
                    turned = wrot[:, 2 * k + 1, :].rearrange("p (h i two) -> p h i two", h=H, two=2)
                    pool.tensor_copy(dst[:, :, 0:2, :], src)
                    pool.tensor_copy(turned[:, :, 0:2, 0], src[:, :, :, 1])
                    i = pool.tensor_copy(turned[:, :, 0:2, 1], src[:, :, :, 0])
                i.then_inc(s_wrot, 1)
                pool.memset(V[:], 0.0).then_inc(s_v0, 1)

                def body(q, u):
                    pool.wait_ge(s_part, 4 * q + 2)
                    pool.tensor_tensor(QT[:, bass.ds(q * 512, 512)], part[u][:, 0, :], part[u][:, 1, :],
                                       ALU.add).then_inc(s_sum, 1)
                    pool.wait_ge(s_part, 4 * q + 4)
                    pool.tensor_tensor(KT[:, bass.ds(q * 512, 512)], part[u][:, 2, :], part[u][:, 3, :],
                                       ALU.add).then_inc(s_sum, 1)
                over_quads(pool, body)

            @block.tensor
            def _(pe):
                pe.wait_ge(s_wrot, 2)

                def down(q, u):
                    pe.wait_ge(norm.s_xs, q + 1)
                    wait(pe, s_lat, q)
                    pe.matmul(bank[2][0:LAT, :], small["d_down"][:], norm.xs[u][:], start=True,
                              stop=True).then_inc(norm.s_used, 1)

                def rope_product(q, u, k):
                    wait(pe, s_part, 4 * q - 3 + k)
                    pe.matmul(bank[4 + k][:], wrot[:, k, :], lat[u][:], start=True, stop=True).then_inc(s_rot, 1)

                def before():
                    norm.turn(pe, 0, 0)
                    down(0, 0)

                def body(q, u, ahead):
                    if ahead:
                        norm.turn(pe, q + 1, 1 - u)
                    pe.wait_ge(s_lat, q + 1)
                    rope_product(q, u, 0)
                    rope_product(q, u, 1)
                    if ahead:
                        down(q + 1, 1 - u)
                    rope_product(q, u, 2)
                    rope_product(q, u, 3)
                    wait(pe, s_vcopy, q)
                    for j in range(4):
                        t = pe.matmul(bank[3][:, j * LAT:(j + 1) * LAT], lat[u][:, j * P:(j + 1) * P],
                                      small["d_v"][:], start=True, stop=True)
                    t.then_inc(s_v, 1)
                quads_ahead(pe, before, body, 1)

            @block.scalar
            def _(act):
                def latents(q, u):
                    act.wait_ge(norm.s_used, q + 1)
                    wait(act, s_v, q - 1)
                    act.activation(lat[u][:], bank[2][0:LAT, :], ACT.Copy).then_inc(s_lat, 1)

                def before():
                    norm.copy(act, 0, 0)
                    latents(0, 0)
                    act.wait_ge(s_v0, 1)

                def body(q, u, ahead):
                    if ahead:
                        norm.copy(act, q + 1, 1 - u)
                        latents(q + 1, 1 - u)
                    act.wait_ge(s_v, q + 1)
                    act.activation(V[:, bass.ds(q * 512, 512)].rearrange("p (b h v) -> p b h v", b=4, h=H)[:, :, :, 0:4],
                                   bank[3][:, 0:4 * LAT].rearrange("p (b h v) -> p b h v", b=4, h=H),
                                   ACT.Copy).then_inc(s_vcopy, 1)
                quads_ahead(act, before, body, 1)

            @block.vector
            def _(dve):
                def before():
                    norm.scale(dve, 0, 0)
                    norm.scale(dve, 1, 1)

                def body(q, u, ahead):
                    wait(dve, s_sum, 2 * q - 2)
                    for k in range(4):
                        dve.wait_ge(s_rot, 4 * q + k + 1)
                        dve.tensor_tensor(part[u][:, k, :].rearrange("p (b t) -> p b t", b=4),
                                          bank[4 + k][:].rearrange("p (b t) -> p b t", b=4),
                                          rope[:, k, :].unsqueeze(1).broadcast_to([P, 4, P]), ALU.mult).then_inc(s_part, 1)
                    if ahead == 2:
                        norm.scale(dve, q + 2, u)
                quads_ahead(dve, before, body)
        own.close()
        own = ExitStack()
        attend("dt", own, QT, KT, V, P, d_up8, None, Z)
        own.close()
        att.close()

        stats("e_stat", src=XC)
        moe = ExitStack()
        XT = [sb(f"e_XT_{part}", [P, NB * P], ctx=moe) for part in ("high", "low")]
        YT = sb("e_YT", [P, NB * P], ctx=moe)
        combT = sb("e_combT", [P, NB * P], F16, ctx=moe)
        own = ExitStack()
        norm = Norm("e", own, bank[0:2], gain=small["g2"])
        ex = [sb(f"e_exp{i}", [P, 4, E1], ctx=own) for i in range(2)]
        lg = [sb(f"e_logit{i}", [P, 4, E1], ctx=own) for i in range(2)]
        mx = sb("e_max", [P, 4], ctx=own)
        pr = sb("e_probs", [P, 4, E1 + 6], ctx=own)
        pm = sb("e_matched", [P, 4, E1 + 6], ctx=own)
        p8 = sb("e_p8", [P, 4, 8], ctx=own)
        ew = sb("e_w", [P, 4, E1], ctx=own)
        es = sb("e_sum", [P, 4], ctx=own)
        s_lg = sem("e_shifted")
        s_ex = sem("e_exp_done")
        s_mx = sem("e_max_ready")
        s_ev = sem("e_route_steps")
        s_epad = sem("e_padded")
        E_STEPS = 11

        def e_scores(router_b, s_logit, finish_comb):
            def dve_scores(dve, q, u):
                if isinstance(q, int) and q == 0:
                    dve.wait_ge(s_epad, 1)
                dve.wait_ge(s_logit, q + 1)
                logits = router_b[u][:, 0:4 * E1].rearrange("p (j e) -> p j e", j=4)
                dve.tensor_reduce(mx[:], logits, AX.X, ALU.max).then_inc(s_mx, 1)
                dve.wait_ge(s_mx, q + 1)
                dve.tensor_tensor(lg[u][:], logits, mx[:].unsqueeze(2).broadcast_to([P, 4, E1]),
                                  ALU.subtract).then_inc(s_lg, 1)
                chain = Chain(dve, s_ev, q * E_STEPS)
                dve.wait_ge(s_ex, q + 1)
                chain(dve.tensor_reduce(es[:], ex[u][:], AX.X, ALU.add))
                chain(dve.reciprocal(es[:], es[:]))
                chain.carried(dve.tensor_tensor(pr[:, :, 0:E1], ex[u][:], es[:].unsqueeze(2).broadcast_to([P, 4, E1]), ALU.mult))
                for j in range(4):
                    i = dve.max(p8[:, j, :], pr[:, j, :])
                chain.carried(i)
                for j in range(4):
                    i = dve.match_replace(pm[:, j, :], p8[:, j, :], pr[:, j, :], -BIG)
                chain(i)
                chain(dve.tensor_tensor(ew[:], pm[:, :, 0:E1], pr[:, :, 0:E1], ALU.not_equal))
                chain(dve.tensor_tensor(ew[:], ew[:], pr[:, :, 0:E1], ALU.mult))
                chain(dve.tensor_reduce(es[:], ew[:], AX.X, ALU.add))
                chain(dve.tensor_scalar(es[:], es[:], 1.0 / COMB_UP, None, ALU.mult))
                chain(dve.reciprocal(es[:], es[:]))
                dve.tensor_tensor(ew[:], ew[:], es[:].unsqueeze(2).broadcast_to([P, 4, E1]), ALU.mult).then_inc(s_ewd, 1)
                dve.wait_ge(s_ewd, q + 1)
                finish_comb(dve, chain, ew[:], q, u)

            def act_scores(act, q, u):
                act.wait_ge(s_lg, q + 1)
                wait(act, s_ev, (q - 2) * E_STEPS + 3)
                act.activation(ex[u][:], lg[u][:], ACT.Exp).then_inc(s_ex, 1)

            def pool_setup(pool):
                pad_top(pool, pr, E1, E1 + 6, s_epad)
            return dve_scores, act_scores, pool_setup

        s_ewd = sem("e_weights_ready")
        route("e_route", own, XT, combT, norm, small["d_router"], E1, e_scores, None)
        own.close()
        s_res = sem("e_residual")
        with nc.Block() as block:
            @block.vector
            def _(dve):
                dve.scalar_tensor_tensor(X[:].rearrange("p b d -> p (b d)"), Z[:].rearrange("p b d -> p (b d)"),
                                         tg[:, 3:4], X[:].rearrange("p b d -> p (b d)"), ALU.mult,
                                         ALU.add).then_inc(s_res, 1)
        experts("e_moe", XT, combT, P, w["e_wg"], w["e_wu"], w["e_wd"], consts["sel1"], E1 * I1 // P, I1 // P, True, YT)
        add_experts("e_add", YT, tg[:, 3:4], True)
        moe.close()


def constants():
    head = (np.arange(P) % 32) // 8
    headsel = (head[:, None] == np.arange(HG)[None, :]).astype(np.float32)
    d = np.arange(P) % 8
    inv = (np.float32(1.0) / np.float32(10000.0) ** (np.arange(0, 4, 2, dtype=np.float32) / np.float32(4))).astype(np.float32)
    ang = (np.arange(P, dtype=np.float32)[None, :] * inv[np.minimum(d // 2, 1)][:, None]).astype(np.float32)
    used = (d < 4).astype(np.float32)[:, None]
    cos = (np.cos(ang) * used).astype(np.float32)
    sin = (np.sin(ang) * used * np.where(d % 2 == 0, -1.0, 1.0)[:, None]).astype(np.float32)
    rope = np.stack([cos * 0.5, sin * 0.5, cos, sin], axis=1).astype(np.float32)
    causal = np.where(np.arange(P)[None, :] > np.arange(P)[:, None], -1e30, 0.0).astype(np.float32)

    def sel(ne, width):
        e = np.arange(ne * width) // width
        one = (np.arange(ne)[:, None] == e[None, :]).astype(np.float32) / COMB_UP
        both = np.zeros((P, ne * width), np.float16)
        both[0:ne] = one
        both[ne:2 * ne] = one
        return both
    return {"ident": np.eye(P, dtype=np.float32), "headsel": headsel, "rope": rope, "causal": causal,
            "sel0": sel(E0, I0), "sel1": sel(E1, I1)}


def layout(i):
    t = np.ascontiguousarray
    n = {k: np.asarray(v) for k, v in i.items()}
    w = {
        "a_wq": n["L0_xattn_Wq"], "a_wk": n["L0_xattn_Wk"], "a_wv": n["L0_xattn_Wv"], "a_wo": n["L0_xattn_Wo"],
        "a_bq": n["L0_xattn_bq"].reshape(D, 1), "a_bk": n["L0_xattn_bk"].reshape(D, 1),
        "a_bv": n["L0_xattn_bv"], "a_bvc": n["L0_xattn_bv"].reshape(D, 1), "a_bo": n["L0_xattn_bo"],
        "a_gate": t(n["L0_ffn_gate_w"].T), "a_gbias": n["L0_ffn_gate_bias"],
        "b_wgT": t(n["L0_ffn_eg_w"].reshape(E0 * I0, D).T), "b_wuT": t(n["L0_ffn_eu_w"].reshape(E0 * I0, D).T),
        "b_wdT": t(n["L0_ffn_ed_w"].transpose(0, 2, 1)).reshape(E0 * I0, D),
        "sgT": t(n["L0_ffn_sg_w"].T), "suT": t(n["L0_ffn_su_w"].T), "sdT": t(n["L0_ffn_sd_w"].T),
        "c_wv": n["L1_xattn_Wv"], "c_wo": n["L1_xattn_Wo"], "c_bo": n["L1_xattn_bo"],
        "c_wkT": t(n["L1_xattn_Wk"].T), "c_wqT": t(n["L1_xattn_Wq"].T),
        "g1": n["L1_ffn_g1"].reshape(D, 1), "g2": n["L1_ffn_g2"].reshape(D, 1),
        "d_down": n["L1_ffn_w_down"], "d_q": n["L1_ffn_wq"], "d_k": n["L1_ffn_wk"], "d_v": n["L1_ffn_wv"],
        "d_up": n["L1_ffn_w_up"], "d_router": n["L1_ffn_router_w"],
        "e_wg": t(n["L1_ffn_w1"].transpose(1, 0, 2)).reshape(D, E1 * I1),
        "e_wu": t(n["L1_ffn_w3"].transpose(1, 0, 2)).reshape(D, E1 * I1),
        "e_wd": n["L1_ffn_w2"].reshape(E1 * I1, D),
    }
    main = {"x": n["x"], "ctxT": t(n["ctx_768"].transpose(0, 2, 1)), "gx": n["g_xattn"], "gf": n["g_ffn"]}
    return main, w


def kernel(stop_after=99, **inputs):
    import concourse.bacc as bacc
    from concourse.bass_utils import run_bass_kernel_spmd

    nc = bacc.Bacc("TRN2", target_bir_lowering=False, num_devices=1)
    main, w = layout(inputs)
    arrays = {}

    def declare(group):
        aps = {}
        for name, a in group.items():
            arrays["in_" + name] = a
            aps[name] = nc.dram_tensor("in_" + name, a.shape, mybir.dt.from_np(a.dtype), kind="ExternalInput").ap()
        return aps

    m, weights, consts = declare(main), declare(w), declare(constants())
    out = nc.dram_tensor("out_0", (NB, P, D), F32, kind="ExternalOutput").ap()
    build(nc, m["x"], m["ctxT"], m["gx"], m["gf"], weights, consts, out, stop_after)
    r = run_bass_kernel_spmd(nc, [arrays], core_ids=[0])
    return r.results[0]["out_0"]
```
